# Optimizing a Trainium2 kernel written in Bass

```python
import numpy as np
import jax
import jax.numpy as jnp

def _softmax(x, axis=-1):
    return jax.nn.softmax(x, axis=axis)

def _gelu(x):
    return jax.nn.gelu(x, approximate=True)

def _silu(x):
    return jax.nn.silu(x)

def _sigmoid(x):
    return jax.nn.sigmoid(x)

def _layernorm(x, axis=-1, eps=1e-05):
    m = jnp.mean(x, axis=axis, keepdims=True)
    v = jnp.var(x, axis=axis, keepdims=True)
    return (x - m) / jnp.sqrt(v + eps)

def _scatter_add(tgt, idx, src, axis=0):
    return tgt.at[idx].add(src)

def _segment_sum(src, seg, n):
    return jax.ops.segment_sum(src, seg, n)
kernel_name = 'mk_cond_seq_d4_seqx_r8_7a886b'

def setup_inputs(seed: int=0):
    np.random.seed(seed)
    _w = jnp.asarray

    def _rec_inputs():
        import jax
        import jax.numpy as jnp
        _rk = jax.random.key(seed)
        x = -0.000125 + 0.9999 * jax.random.normal(jax.random.fold_in(_rk, 1), (16, 128, 128), jnp.float32)
        _lenS = 128 - jax.random.randint(jax.random.fold_in(_rk, 7), (16,), 0, max(1, 128 // 4) + 1, jnp.int32)
        _lenS2 = 128 - jax.random.randint(jax.random.fold_in(_rk, 8), (16,), 0, max(1, 128 // 4) + 1, jnp.int32)
        itok_B_0_15 = jax.random.randint(jax.random.fold_in(_rk, 11), (16,), 0, 16, jnp.int32)
        itok_B_34_63 = jax.random.randint(jax.random.fold_in(_rk, 13), (16,), 34, 64, jnp.int32)
        fside_Bx16xSxS_0 = -1.47943e-05 + 1.00017 * jax.random.normal(jax.random.fold_in(_rk, 14), (16, 16, 128, 128), jnp.float32)
        itok_B_0_7 = jax.random.randint(jax.random.fold_in(_rk, 15), (16,), 0, 8, jnp.int32)
        itok_B_6_14 = jax.random.randint(jax.random.fold_in(_rk, 16), (16,), 6, 15, jnp.int32)
        _validS = jnp.arange(128)[None, :] < _lenS[:, None]
        _validS2 = jnp.arange(128)[None, :] < _lenS2[:, None]
        _causal = jnp.tril(jnp.ones((128, 128), dtype=bool))
        mask_Bx1xSxS_bk0 = jnp.logical_not(jnp.broadcast_to(_validS[:, None, None, :], (16, 1, 128, 128)))
        return (x, itok_B_0_15, itok_B_34_63, fside_Bx16xSxS_0, itok_B_0_7, itok_B_6_14, mask_Bx1xSxS_bk0)
    x, itok_B_0_15, itok_B_34_63, fside_Bx16xSxS_0, itok_B_0_7, itok_B_6_14, mask_Bx1xSxS_bk0 = _rec_inputs()

    def _L0_cond_setup():
        import jax, jax.numpy as jnp
        import numpy as np
        B, S, D = (32, 128, 128)
        A = 32
        E = 16
        LN_EPS = 1e-05
        key = jax.random.key(seed)
        ks = jax.random.split(key, 10)
        s = lambda fan_in: 1.0 / np.sqrt(fan_in)
        return {'hidden_states': jax.random.normal(ks[0], (B, S, D), dtype=jnp.float32), 'domain_id': jax.random.randint(ks[1], (B,), 0, E, dtype=jnp.int64), 'down_W': jax.random.uniform(ks[2], (A, D), jnp.float32, -s(D), s(D)), 'down_b': jax.random.uniform(ks[3], (A,), jnp.float32, -s(D), s(D)), 'up_W': jax.random.uniform(ks[4], (D, A), jnp.float32, -s(A), s(A)), 'up_b': jax.random.uniform(ks[5], (D,), jnp.float32, -s(A), s(A)), 'expert_W': jax.random.uniform(ks[6], (E, A, A), jnp.float32, -s(A), s(A)), 'expert_b': jax.random.uniform(ks[7], (E, A), jnp.float32, -s(A), s(A)), 'domain_emb': jax.random.normal(ks[8], (E, A), dtype=jnp.float32), 'ln_gamma': jnp.ones((D,), jnp.float32), 'ln_beta': jnp.zeros((D,), jnp.float32)}
    _L0_cond_all = _L0_cond_setup()
    _L0_cond_in = {k: v for k, v in _L0_cond_all.items() if k in ('down_W', 'down_b', 'up_W', 'up_b', 'expert_W', 'expert_b', 'domain_emb', 'ln_gamma', 'ln_beta')}
    del _L0_cond_all

    def _L1_cond_setup():
        import jax, jax.numpy as jnp
        import numpy as np
        import math
        D_MODEL = 128
        N_HEAD = 16
        HEAD_DIM = D_MODEL // N_HEAD
        D_FF = 512
        NUM_STEPS = 100.0
        RESCALE = 4000.0
        EPS = 1e-05

        def _sin_emb(t):
            half = D_MODEL // 2
            x = t.astype(jnp.float32) / NUM_STEPS * RESCALE
            freqs = jnp.exp(jnp.arange(half, dtype=jnp.float32) * (-math.log(10000.0) / (half - 1)))
            e = x[:, None] * freqs[None, :]
            return jnp.concatenate([jnp.sin(e), jnp.cos(e)], axis=-1)

        def _ln(x):
            m = jnp.mean(x, axis=-1, keepdims=True)
            v = jnp.var(x, axis=-1, keepdims=True)
            return (x - m) / jnp.sqrt(v + EPS)

        def _gelu2(x):
            return x * jax.nn.sigmoid(1.702 * x)
        key = jax.random.key(seed)
        ks = jax.random.split(key, 24)
        B, S, D, F = (4, 64, D_MODEL, D_FF)
        std = 0.02
        inp = {'src': jax.random.normal(ks[0], (B, S, D), dtype=jnp.float32), 'src_mask': jax.random.randint(ks[1], (B, 1, S, S), 0, 2).astype(bool), 'timestep': jax.random.randint(ks[2], (B,), 0, 100, dtype=jnp.int32), 'attention_bias': jax.random.normal(ks[3], (B, N_HEAD, S, S), dtype=jnp.float32), 'W_ada': jax.random.normal(ks[4], (D, 2 * D), dtype=jnp.float32) * std, 'b_ada': jnp.zeros((2 * D,), dtype=jnp.float32), 'Wq': jax.random.normal(ks[5], (D, D), dtype=jnp.float32) * std, 'bq': jnp.zeros((D,), dtype=jnp.float32), 'Wk': jax.random.normal(ks[6], (D, D), dtype=jnp.float32) * std, 'bk': jnp.zeros((D,), dtype=jnp.float32), 'Wv': jax.random.normal(ks[7], (D, D), dtype=jnp.float32) * std, 'bv': jnp.zeros((D,), dtype=jnp.float32), 'Wo': jax.random.normal(ks[8], (D, D), dtype=jnp.float32) * std, 'bo': jnp.zeros((D,), dtype=jnp.float32), 'W1': jax.random.normal(ks[9], (D, F), dtype=jnp.float32) * std, 'b1': jnp.zeros((F,), dtype=jnp.float32), 'W2': jax.random.normal(ks[10], (F, D), dtype=jnp.float32) * std, 'b2': jnp.zeros((D,), dtype=jnp.float32), 'g2': jnp.ones((D,), dtype=jnp.float32), 'beta2': jnp.zeros((D,), dtype=jnp.float32)}
        return inp
    _L1_cond_all = _L1_cond_setup()
    _L1_cond_in = {k: v for k, v in _L1_cond_all.items() if k in ('W_ada', 'b_ada', 'Wq', 'bq', 'Wk', 'bk', 'Wv', 'bv', 'Wo', 'bo', 'W1', 'b1', 'W2', 'b2', 'g2', 'beta2')}
    del _L1_cond_all

    def _L2_cond_setup():
        import jax, jax.numpy as jnp
        import numpy as np
        E, H, I = (8, 128, 512)
        B, S = (4, 128)
        LN_EPS = 1e-12
        key = jax.random.key(seed)
        ks = jax.random.split(key, 8)
        x = jax.random.normal(ks[0], (B, S, H), dtype=jnp.float32)
        expert_idx = jax.random.randint(ks[1], (B,), 0, E, dtype=jnp.int64)
        Wi = jax.random.normal(ks[2], (E, H, I), dtype=jnp.float32) * 0.02
        bi = jnp.zeros((E, I), dtype=jnp.float32)
        Wo = jax.random.normal(ks[3], (E, I, H), dtype=jnp.float32) * 0.02
        bo = jnp.zeros((E, H), dtype=jnp.float32)
        gamma = jnp.ones((E, H), dtype=jnp.float32)
        beta = jnp.zeros((E, H), dtype=jnp.float32)
        return {'input_tensor': x, 'expert_idx': expert_idx, 'Wi': Wi, 'bi': bi, 'Wo': Wo, 'bo': bo, 'gamma': gamma, 'beta': beta}
    _L2_cond_all = _L2_cond_setup()
    _L2_cond_in = {k: v for k, v in _L2_cond_all.items() if k in ('Wi', 'bi', 'Wo', 'bo', 'gamma', 'beta')}
    del _L2_cond_all

    def _L3_cond_setup():
        import jax, jax.numpy as jnp
        import numpy as np
        D = 128
        E = 8
        FF = 512
        TOPK = 2
        S = 32
        SE = 64
        SH = 128
        B, T = (2, 256)

        def _forward(x, subject_ids, ln_g, ln_b, subj_emb, hyp_w1, hyp_b1, hyp_w2, hyp_b2, sty_w1, sty_b1, sty_w2, sty_b2, router_w, exp_w1, exp_b1, exp_w2, exp_b2):
            mu = x.mean(-1, keepdims=True)
            var = x.var(-1, keepdims=True)
            h = (x - mu) * jax.lax.rsqrt(var + 1e-05) * ln_g + ln_b
            m_t = h.mean(1, keepdims=True)
            v_t = h.var(1, keepdims=True)
            h_norm = (h - m_t) * jax.lax.rsqrt(v_t + 1e-08)
            se = subj_emb[subject_ids]
            hyp = jax.nn.relu(se @ hyp_w1 + hyp_b1) @ hyp_w2 + hyp_b2
            sty = jax.nn.relu(hyp @ sty_w1 + sty_b1) @ sty_w2 + sty_b2
            gamma, beta = jnp.split(sty, 2, axis=-1)
            gamma = jax.nn.softplus(gamma) + 1e-08
            h = h_norm * gamma[:, None, :] + beta[:, None, :]
            h_flat = h.reshape(-1, D)
            probs = jax.nn.softmax(h_flat @ router_w, axis=-1)
            gates, idx = jax.lax.top_k(probs, TOPK)
            gates = gates / gates.sum(-1, keepdims=True)
            N = h_flat.shape[0]
            combine = jnp.zeros((N, E), h_flat.dtype).at[jnp.arange(N)[:, None], idx].add(gates)
            hid = jax.nn.relu(jnp.einsum('nd,edf->nef', h_flat, exp_w1) + exp_b1)
            eout = jnp.einsum('nef,efd->ned', hid, exp_w2) + exp_b2
            y = jnp.einsum('ned,ne->nd', eout, combine)
            return x + y.reshape(x.shape)
        key = jax.random.key(seed)
        ks = jax.random.split(key, 16)
        n = lambda k, sh, s=0.02: jax.random.normal(k, sh, dtype=jnp.float32) * s
        return {'x': jax.random.normal(ks[0], (B, T, D), dtype=jnp.float32), 'subject_ids': jax.random.randint(ks[1], (B,), 0, S), 'ln_g': jnp.ones((D,), jnp.float32), 'ln_b': jnp.zeros((D,), jnp.float32), 'subj_emb': n(ks[2], (S, SE)), 'hyp_w1': n(ks[3], (SE, SH), 1.0 / np.sqrt(SE)), 'hyp_b1': jnp.zeros((SH,), jnp.float32), 'hyp_w2': n(ks[4], (SH, SH), 1.0 / np.sqrt(SH)), 'hyp_b2': jnp.zeros((SH,), jnp.float32), 'sty_w1': n(ks[5], (SH, SH // 2), 1.0 / np.sqrt(SH)), 'sty_b1': jnp.zeros((SH // 2,), jnp.float32), 'sty_w2': n(ks[6], (SH // 2, 2 * D), 1.0 / np.sqrt(SH // 2)), 'sty_b2': jnp.zeros((2 * D,), jnp.float32), 'router_w': n(ks[7], (D, E), 1.0 / np.sqrt(D)), 'exp_w1': n(ks[8], (E, D, FF), 1.0 / np.sqrt(D)), 'exp_b1': jnp.zeros((E, FF), jnp.float32), 'exp_w2': n(ks[9], (E, FF, D), 1.0 / np.sqrt(FF)), 'exp_b2': jnp.zeros((E, D), jnp.float32)}
    _L3_cond_all = _L3_cond_setup()
    _L3_cond_in = {k: v for k, v in _L3_cond_all.items() if k in ('ln_g', 'ln_b', 'subj_emb', 'hyp_w1', 'hyp_b1', 'hyp_w2', 'hyp_b2', 'sty_w1', 'sty_b1', 'sty_w2', 'sty_b2', 'router_w', 'exp_w1', 'exp_b1', 'exp_w2', 'exp_b2')}
    del _L3_cond_all
    return {'x': x, 'itok_B_0_15': itok_B_0_15, 'itok_B_34_63': itok_B_34_63, 'fside_Bx16xSxS_0': fside_Bx16xSxS_0, 'itok_B_0_7': itok_B_0_7, 'itok_B_6_14': itok_B_6_14, 'mask_Bx1xSxS_bk0': mask_Bx1xSxS_bk0, 'L0_cond_down_W': _L0_cond_in['down_W'], 'L0_cond_down_b': _L0_cond_in['down_b'], 'L0_cond_up_W': _L0_cond_in['up_W'], 'L0_cond_up_b': _L0_cond_in['up_b'], 'L0_cond_expert_W': _L0_cond_in['expert_W'], 'L0_cond_expert_b': _L0_cond_in['expert_b'], 'L0_cond_domain_emb': _L0_cond_in['domain_emb'], 'L0_cond_ln_gamma': _L0_cond_in['ln_gamma'], 'L0_cond_ln_beta': _L0_cond_in['ln_beta'], 'L1_cond_W_ada': _L1_cond_in['W_ada'], 'L1_cond_b_ada': _L1_cond_in['b_ada'], 'L1_cond_Wq': _L1_cond_in['Wq'], 'L1_cond_bq': _L1_cond_in['bq'], 'L1_cond_Wk': _L1_cond_in['Wk'], 'L1_cond_bk': _L1_cond_in['bk'], 'L1_cond_Wv': _L1_cond_in['Wv'], 'L1_cond_bv': _L1_cond_in['bv'], 'L1_cond_Wo': _L1_cond_in['Wo'], 'L1_cond_bo': _L1_cond_in['bo'], 'L1_cond_W1': _L1_cond_in['W1'], 'L1_cond_b1': _L1_cond_in['b1'], 'L1_cond_W2': _L1_cond_in['W2'], 'L1_cond_b2': _L1_cond_in['b2'], 'L1_cond_g2': _L1_cond_in['g2'], 'L1_cond_beta2': _L1_cond_in['beta2'], 'L2_cond_Wi': _L2_cond_in['Wi'], 'L2_cond_bi': _L2_cond_in['bi'], 'L2_cond_Wo': _L2_cond_in['Wo'], 'L2_cond_bo': _L2_cond_in['bo'], 'L2_cond_gamma': _L2_cond_in['gamma'], 'L2_cond_beta': _L2_cond_in['beta'], 'L3_cond_ln_g': _L3_cond_in['ln_g'], 'L3_cond_ln_b': _L3_cond_in['ln_b'], 'L3_cond_subj_emb': _L3_cond_in['subj_emb'], 'L3_cond_hyp_w1': _L3_cond_in['hyp_w1'], 'L3_cond_hyp_b1': _L3_cond_in['hyp_b1'], 'L3_cond_hyp_w2': _L3_cond_in['hyp_w2'], 'L3_cond_hyp_b2': _L3_cond_in['hyp_b2'], 'L3_cond_sty_w1': _L3_cond_in['sty_w1'], 'L3_cond_sty_b1': _L3_cond_in['sty_b1'], 'L3_cond_sty_w2': _L3_cond_in['sty_w2'], 'L3_cond_sty_b2': _L3_cond_in['sty_b2'], 'L3_cond_router_w': _L3_cond_in['router_w'], 'L3_cond_exp_w1': _L3_cond_in['exp_w1'], 'L3_cond_exp_b1': _L3_cond_in['exp_b1'], 'L3_cond_exp_w2': _L3_cond_in['exp_w2'], 'L3_cond_exp_b2': _L3_cond_in['exp_b2']}

def reference(x, itok_B_0_15, itok_B_34_63, fside_Bx16xSxS_0, itok_B_0_7, itok_B_6_14, mask_Bx1xSxS_bk0, L0_cond_down_W, L0_cond_down_b, L0_cond_up_W, L0_cond_up_b, L0_cond_expert_W, L0_cond_expert_b, L0_cond_domain_emb, L0_cond_ln_gamma, L0_cond_ln_beta, L1_cond_W_ada, L1_cond_b_ada, L1_cond_Wq, L1_cond_bq, L1_cond_Wk, L1_cond_bk, L1_cond_Wv, L1_cond_bv, L1_cond_Wo, L1_cond_bo, L1_cond_W1, L1_cond_b1, L1_cond_W2, L1_cond_b2, L1_cond_g2, L1_cond_beta2, L2_cond_Wi, L2_cond_bi, L2_cond_Wo, L2_cond_bo, L2_cond_gamma, L2_cond_beta, L3_cond_ln_g, L3_cond_ln_b, L3_cond_subj_emb, L3_cond_hyp_w1, L3_cond_hyp_b1, L3_cond_hyp_w2, L3_cond_hyp_b2, L3_cond_sty_w1, L3_cond_sty_b1, L3_cond_sty_w2, L3_cond_sty_b2, L3_cond_router_w, L3_cond_exp_w1, L3_cond_exp_b1, L3_cond_exp_w2, L3_cond_exp_b2):
    import jax
    import jax.numpy as jnp

    def _L0_cond_ref(hidden_states, domain_id, down_W, down_b, up_W, up_b, expert_W, expert_b, domain_emb, ln_gamma, ln_beta):
        import jax, jax.numpy as jnp
        import numpy as np
        B, S, D = (32, 128, 128)
        A = 32
        E = 16
        LN_EPS = 1e-05
        residual = hidden_states
        hidden = jnp.einsum('bsd,ad->bsa', hidden_states, down_W) + down_b
        hidden = jax.nn.gelu(hidden, approximate=False)
        valid = (domain_id >= 0) & (domain_id < E)
        idx = jnp.clip(domain_id, 0, E - 1)
        Wsel = expert_W[idx]
        bsel = expert_b[idx]
        expert_out = jnp.einsum('bsa,boa->bso', hidden, Wsel) + bsel[:, None, :]
        domain_output = jnp.where(valid[:, None, None], expert_out, hidden)
        hidden = domain_output + domain_emb[idx][:, None, :]
        hidden = jnp.einsum('bsa,da->bsd', hidden, up_W) + up_b
        x = hidden + residual
        mu = jnp.mean(x, axis=-1, keepdims=True)
        var = jnp.mean(jnp.square(x - mu), axis=-1, keepdims=True)
        return (x - mu) * jax.lax.rsqrt(var + LN_EPS) * ln_gamma + ln_beta

    def _L1_cond_ref(src, src_mask, timestep, attention_bias, W_ada, b_ada, Wq, bq, Wk, bk, Wv, bv, Wo, bo, W1, b1, W2, b2, g2, beta2):
        import jax, jax.numpy as jnp
        import numpy as np
        import math
        D_MODEL = 128
        N_HEAD = 16
        HEAD_DIM = D_MODEL // N_HEAD
        D_FF = 512
        NUM_STEPS = 100.0
        RESCALE = 4000.0
        EPS = 1e-05

        def _sin_emb(t):
            half = D_MODEL // 2
            x = t.astype(jnp.float32) / NUM_STEPS * RESCALE
            freqs = jnp.exp(jnp.arange(half, dtype=jnp.float32) * (-math.log(10000.0) / (half - 1)))
            e = x[:, None] * freqs[None, :]
            return jnp.concatenate([jnp.sin(e), jnp.cos(e)], axis=-1)

        def _ln(x):
            m = jnp.mean(x, axis=-1, keepdims=True)
            v = jnp.var(x, axis=-1, keepdims=True)
            return (x - m) / jnp.sqrt(v + EPS)

        def _gelu2(x):
            return x * jax.nn.sigmoid(1.702 * x)
        B, S, D = src.shape
        emb = jax.nn.silu(_sin_emb(timestep)) @ W_ada + b_ada
        scale, shift = jnp.split(emb[:, None, :], 2, axis=-1)
        x = _ln(src) * (1.0 + scale) + shift
        q = (x @ Wq + bq).reshape(B, S, N_HEAD, HEAD_DIM).transpose(0, 2, 1, 3)
        k = (x @ Wk + bk).reshape(B, S, N_HEAD, HEAD_DIM).transpose(0, 2, 1, 3)
        v = (x @ Wv + bv).reshape(B, S, N_HEAD, HEAD_DIM).transpose(0, 2, 1, 3)
        scores = jnp.einsum('bhqd,bhkd->bhqk', q / math.sqrt(HEAD_DIM), k)
        scores = scores + attention_bias
        scores = jnp.where(src_mask, -jnp.inf, scores.astype(jnp.float32))
        probs = jax.nn.softmax(scores, axis=-1).astype(v.dtype)
        ctx = jnp.einsum('bhqk,bhkd->bhqd', probs, v)
        ctx = ctx.transpose(0, 2, 1, 3).reshape(B, S, D)
        x = x + (ctx @ Wo + bo)
        h = _ln(x) * g2 + beta2
        ff = _gelu2(h @ W1 + b1) @ W2 + b2
        return x + ff

    def _L2_cond_ref(input_tensor, expert_idx, Wi, bi, Wo, bo, gamma, beta):
        import jax, jax.numpy as jnp
        import numpy as np
        E, H, I = (8, 128, 512)
        B, S = (4, 128)
        LN_EPS = 1e-12
        Wi_b = Wi[expert_idx]
        bi_b = bi[expert_idx]
        Wo_b = Wo[expert_idx]
        bo_b = bo[expert_idx]
        g_b = gamma[expert_idx]
        be_b = beta[expert_idx]
        h = jax.nn.gelu(jnp.einsum('bsh,bhi->bsi', input_tensor, Wi_b) + bi_b[:, None, :], approximate=False)
        o = jnp.einsum('bsi,bih->bsh', h, Wo_b) + bo_b[:, None, :]
        r = o + input_tensor
        mu = jnp.mean(r, axis=-1, keepdims=True)
        var = jnp.mean(jnp.square(r - mu), axis=-1, keepdims=True)
        y = (r - mu) * jax.lax.rsqrt(var + LN_EPS)
        return y * g_b[:, None, :] + be_b[:, None, :]

    def _L3_cond_ref(x, subject_ids, ln_g, ln_b, subj_emb, hyp_w1, hyp_b1, hyp_w2, hyp_b2, sty_w1, sty_b1, sty_w2, sty_b2, router_w, exp_w1, exp_b1, exp_w2, exp_b2):
        import jax, jax.numpy as jnp
        import numpy as np
        D = 128
        E = 8
        FF = 512
        TOPK = 2
        S = 32
        SE = 64
        SH = 128
        B, T = (2, 256)

        def _forward(x, subject_ids, ln_g, ln_b, subj_emb, hyp_w1, hyp_b1, hyp_w2, hyp_b2, sty_w1, sty_b1, sty_w2, sty_b2, router_w, exp_w1, exp_b1, exp_w2, exp_b2):
            mu = x.mean(-1, keepdims=True)
            var = x.var(-1, keepdims=True)
            h = (x - mu) * jax.lax.rsqrt(var + 1e-05) * ln_g + ln_b
            m_t = h.mean(1, keepdims=True)
            v_t = h.var(1, keepdims=True)
            h_norm = (h - m_t) * jax.lax.rsqrt(v_t + 1e-08)
            se = subj_emb[subject_ids]
            hyp = jax.nn.relu(se @ hyp_w1 + hyp_b1) @ hyp_w2 + hyp_b2
            sty = jax.nn.relu(hyp @ sty_w1 + sty_b1) @ sty_w2 + sty_b2
            gamma, beta = jnp.split(sty, 2, axis=-1)
            gamma = jax.nn.softplus(gamma) + 1e-08
            h = h_norm * gamma[:, None, :] + beta[:, None, :]
            h_flat = h.reshape(-1, D)
            probs = jax.nn.softmax(h_flat @ router_w, axis=-1)
            gates, idx = jax.lax.top_k(probs, TOPK)
            gates = gates / gates.sum(-1, keepdims=True)
            N = h_flat.shape[0]
            combine = jnp.zeros((N, E), h_flat.dtype).at[jnp.arange(N)[:, None], idx].add(gates)
            hid = jax.nn.relu(jnp.einsum('nd,edf->nef', h_flat, exp_w1) + exp_b1)
            eout = jnp.einsum('nef,efd->ned', hid, exp_w2) + exp_b2
            y = jnp.einsum('ned,ne->nd', eout, combine)
            return x + y.reshape(x.shape)
        return _forward(x, subject_ids, ln_g, ln_b, subj_emb, hyp_w1, hyp_b1, hyp_w2, hyp_b2, sty_w1, sty_b1, sty_w2, sty_b2, router_w, exp_w1, exp_b1, exp_w2, exp_b2)
    x = _L0_cond_ref(x, itok_B_0_15, L0_cond_down_W, L0_cond_down_b, L0_cond_up_W, L0_cond_up_b, L0_cond_expert_W, L0_cond_expert_b, L0_cond_domain_emb, L0_cond_ln_gamma, L0_cond_ln_beta)
    x = _L1_cond_ref(x, mask_Bx1xSxS_bk0, itok_B_34_63, fside_Bx16xSxS_0, L1_cond_W_ada, L1_cond_b_ada, L1_cond_Wq, L1_cond_bq, L1_cond_Wk, L1_cond_bk, L1_cond_Wv, L1_cond_bv, L1_cond_Wo, L1_cond_bo, L1_cond_W1, L1_cond_b1, L1_cond_W2, L1_cond_b2, L1_cond_g2, L1_cond_beta2)
    x = _L2_cond_ref(x, itok_B_0_7, L2_cond_Wi, L2_cond_bi, L2_cond_Wo, L2_cond_bo, L2_cond_gamma, L2_cond_beta)
    x = _L3_cond_ref(x, itok_B_6_14, L3_cond_ln_g, L3_cond_ln_b, L3_cond_subj_emb, L3_cond_hyp_w1, L3_cond_hyp_b1, L3_cond_hyp_w2, L3_cond_hyp_b2, L3_cond_sty_w1, L3_cond_sty_b1, L3_cond_sty_w2, L3_cond_sty_b2, L3_cond_router_w, L3_cond_exp_w1, L3_cond_exp_b1, L3_cond_exp_w2, L3_cond_exp_b2)
    return x

_drawn_inputs = setup_inputs


def setup_inputs(seed=0):
    import zlib

    import numpy as np

    out = dict(_drawn_inputs(seed))
    spreads = {'L0_cond_ln_gamma': (1.0, 0.2),
     'L0_cond_ln_beta': (0.0, 0.1),
     'L1_cond_b_ada': (0.0, 0.1),
     'L1_cond_bq': (0.0, 0.762),
     'L1_cond_bk': (0.0, 0.8),
     'L1_cond_bv': (0.0, 0.335),
     'L1_cond_bo': (0.0, 0.1),
     'L1_cond_b1': (0.0, 0.1),
     'L1_cond_b2': (0.0, 0.1),
     'L1_cond_g2': (1.0, 0.2),
     'L1_cond_beta2': (0.0, 0.39),
     'L2_cond_bi': (0.0, 0.1),
     'L2_cond_bo': (0.0, 0.1),
     'L2_cond_gamma': (1.0, 0.2),
     'L2_cond_beta': (0.0, 0.1),
     'L3_cond_ln_g': (1.0, 0.6),
     'L3_cond_ln_b': (0.0, 0.8),
     'L3_cond_hyp_b1': (0.0, 0.1),
     'L3_cond_hyp_b2': (0.0, 0.1),
     'L3_cond_sty_b1': (0.0, 0.1),
     'L3_cond_sty_b2': (0.0, 0.1),
     'L3_cond_exp_b1': (0.0, 0.1),
     'L3_cond_exp_b2': (0.0, 0.1)}
    factors = {'L1_cond_Wq': 7.359, 'L1_cond_Wk': 8.0}
    for name, (base, spread) in spreads.items():
        noise = np.random.default_rng([zlib.crc32(name.encode()), seed]).standard_normal(out[name].shape)
        drawn = base * np.exp(spread * noise) if base else spread * noise
        out[name] = jnp.asarray(drawn.astype(out[name].dtype))
    for name, factor in factors.items():
        out[name] = (out[name] * factor).astype(out[name].dtype)
    return out
```

```python
from contextlib import ExitStack

import numpy as np

import concourse.bass as bass
from concourse import mybir

F32, BF16 = mybir.dt.float32, mybir.dt.bfloat16
I32, U32, U8 = mybir.dt.int32, mybir.dt.uint32, mybir.dt.uint8
ALU = mybir.AluOpType
ACT = mybir.ActivationFunctionType
AX = mybir.AxisListType.X

B, S, D = 16, 128, 128
GB = 4
NG, GT = B // GB, GB * S
A0, E0 = 32, 16
H, DH = 16, 8
HQ = 4
NQ = H // HQ
FF, FC = 512, 4
E2, E3 = 8, 8
SUB, SE = 32, 64
CW = 32
MASKED = -1.0e30
Q_PIECES = (0, 0, 1, 1, 0, 2)
K_PIECES = (0, 1, 0, 1, 2, 0)
TWO_PI_PARTS = (6.28125, 0.0019340515136718750, 1.2556659146e-06)
ROUNDER = 12582912.0


SETUP_ID2 = 11
SETUP_ONEHOT = 14
SETUP_ANGLE = 22
SETUP_WSEL = 24
SETUP_ADA = 29


def wait_apart(eng, sem, value, met, met_value):
    value = value if isinstance(value, int) else eng.to_reg(value)
    eng.wait_ge(met, met_value)
    eng.wait_ge(sem, value)


class Chain:

    def __init__(self, eng, sem, base=0):
        self.eng, self.sem, self.base, self.n = eng, sem, base, 0

    def did(self, ins):
        ins.then_inc(self.sem, 1)
        self.n += 1

    def join(self):
        self.eng.wait_ge(self.sem, self.base + self.n)

    def join_apart(self, met, met_value):
        wait_apart(self.eng, self.sem, self.base + self.n, met, met_value)

    def step(self, ins):
        self.did(ins)
        self.join()


def program(nc, t, out):
    ctx = ExitStack()
    with ctx:
        build(nc, ctx, t, out)


def build(nc, ctx, dram, out):
    def sb(name, shape, dt=F32):
        return ctx.enter_context(nc.sbuf_tensor(name, shape, dt))

    def sem(name):
        return ctx.enter_context(nc.semaphore(name))

    x_in = sb("x_in", [S, B, D])
    x2 = x_in
    l0_area = sb("l0_area", [128, 8192])
    xT = l0_area[:, 0:2048]
    hT = l0_area[0:A0, 2048:4096]
    eT = l0_area[0:A0 + 1, 4096:6144]
    x1 = l0_area[:, 6144:8192].rearrange("p (b d) -> p b d", b=B)
    w1e = l0_area[:, 0:4096].rearrange("p (e f) -> p e f", e=E3)
    w2e = l0_area[:, 4096:8192].rearrange("p (e c d) -> p e c d", e=E3, c=FC)
    xn1 = sb("xn1", [S, B, D])
    x4 = xn1
    v_rows = sb("v_rows", [S, B, D])
    hcols = v_rows[:, :, :].rearrange("p b d -> p (b d)")
    y_rows = sb("y_rows", [S, B, D])
    biasx = sb("biasx", [S, GB, H, S])
    stack_area = sb("stack_area", [128, 2 * 2 * H * GT], BF16)
    qst = stack_area[:, 0:2 * H * GT].rearrange("p (r h t) -> p r h t", r=2, h=H)
    kst = stack_area[:, 2 * H * GT:].rearrange("p (r h t) -> p r h t", r=2, h=H)
    ff_area = stack_area[:, :].bitcast(F32)
    ffT = [ff_area[:, 2048 * p:2048 * p + 2048].rearrange("p (c t) -> p c t", c=FC) for p in range(2)]
    xs = [ff_area[:, 4096 + 512 * p:4608 + 512 * p].rearrange("p (b d) -> p b d", b=GB) for p in range(2)]
    hf = [ff_area[:, 5120 + 512 * p:5632 + 512 * p] for p in range(2)]
    x3 = [ff_area[:, 6144 + 512 * p:6656 + 512 * p].rearrange("p (b d) -> p b d", b=GB) for p in range(2)]
    h2T = [ff_area[:, 7168 + 512 * p:7680 + 512 * p].rearrange("p (c t) -> p c t", c=FC) for p in range(2)]
    r3 = ff_area[:, 8192:8704].rearrange("p (b d) -> p b d", b=GB)
    xb3 = ff_area[:, 8704:9216].rearrange("p (b d) -> p b d", b=GB)
    hl = ff_area[:, 9216:9728].rearrange("p (b d) -> p b d", b=GB)
    hfs = ff_area[:, 9728:10240].rearrange("p (b d) -> p b d", b=GB)
    w2slot = [biasx[:, j, 0:8, :].rearrange("p a b -> p (a b)") for j in range(GB)]
    rows2 = [biasx[:, j, 8:11, :] for j in range(GB)]
    combT = ff_area[0:E3, 10240:10752]
    early = y_rows[:, :, :].rearrange("p b d -> p (b d)")
    bi_sb = early[0:E2, 0:512]
    w_h1 = early[0:SE, 512:640]
    w_h2 = early[:, 640:768]
    w_s1 = early[:, 768:832]
    w_s2 = early[0:64, 832:1088]
    sel_small = early[0:SUB, 1088:1216]
    w_down = early[:, 1216:1248]
    w_up = early[0:A0 + 1, 1248:1376]
    w_ada = early[:, 1376:1632]
    p_area = sb("p_area", [128, 1024])
    pT = [p_area[:, 512 * p:512 * p + 512].rearrange("p (h q) -> p h q", h=HQ) for p in range(2)]
    ew0 = p_area[0:E0 + 1, :]
    wsel = sb("wsel", [A0, B, A0])
    yT = [sb(f"yT{p}", [D, GB, S]) for p in range(2)]
    qkf = [sb(f"qkf{p}", [D, GT]) for p in range(2)]
    pieces = [sb(f"pieces{p}", [D, 3, GT], BF16) for p in range(2)]
    vaug = [sb(f"vaug{p}", [S, H, CW]) for p in range(2)]
    mneg = [sb(f"mneg{p}", [S, S], BF16) for p in range(2)]
    mask = sb("mask", [S, B, S], U8)
    msel = sb("msel", [128, H], BF16)
    mx = sb("mx", [S, 2, H])
    mres = sb("mres", [S, H])
    mp = sb("mp", [S, 128], BF16)
    mT = sb("mT", [128, S], BF16)
    ctxs = sb("ctxs", [128, NQ, S])
    ctxn = sb("ctxn", [S, D])
    ctx2T = sb("ctx2T", [D, S])
    den = sb("den", [S, H])
    rden = sb("rden", [S, H])
    nanfix = sb("nanfix", [S, B])
    ident = sb("ident", [128, 128])
    identb = sb("identb", [128, 128], BF16)
    maskedb = sb("maskedb", [128, 128], BF16)
    cst = sb("cst", [128, 32])
    ids = sb("ids", [128, 4, B], I32)
    idf = sb("idf", [128, 8, B])
    oh = sb("oh", [128, 5, B])
    id2 = sb("id2", [1, B], I32)
    cols = sb("cols", [128, 64])
    rows = sb("rows", [128, 5, D])
    tmp = sb("tmp", [128, 8, B])
    ada = sb("ada", [D, 2, B])
    domb = sb("domb", [A0, B])
    bi2 = sb("bi2", [128, FC, B])
    sty = sb("sty", [D, 4, B])
    hyp = sb("hyp", [128, 4, B])
    w_q = sb("w_q", [D, D])
    w_k = sb("w_k", [D, D])
    w_vi = sb("w_vi", [D, 2 * D])
    w_o = sb("w_o", [D, D])
    w_1 = sb("w_1", [D, FF])
    w_2 = sb("w_2", [128, FC, D])
    w_r = sb("w_r", [D, E3])
    be2 = sb("be2", [E3, D])
    b1e = sb("b1e", [128, E3 * FC])
    st = sb("st", [128, GB, 6])
    mv = sb("mv", [128, GB, 2])
    rs = sb("rs", [128, 4, GB])
    top = sb("top", [S, GB, 8])
    topi = sb("topi", [S, GB, 8], U32)
    topf = sb("topf", [S, GB, 8])
    gate = sb("gate", [S, 4, GB])
    comb = sb("comb", [S, B, E3])
    comb2 = sb("comb2", [S, GB, E3])
    combs = sb("combs", [S, GB, E3])
    iota8 = sb("iota8", [128, 8])
    ps = ctx.enter_context(nc.psum_tensor("ps", [128, 8, 512], F32))
    scr = nc.dram_tensor("qk_pieces", [2, 3, 128, B * S], BF16).ap()

    def bank4(n):
        return ps[:, n, :].rearrange("p (a b) -> p a b", a=4)

    IOTA, FREQ, PHASE, TURN = (cst[:, i:i + 1] for i in range(4))
    hsel = cst[:, 8:24]
    (C_DOWN, C_ADA0, C_ADA1, C_BQ, C_BK, C_G2, C_BETA2, C_LNG, C_LNB, C_HB1, C_HB2, C_SB1, C_SG, C_SB,
     C_B1) = range(15)

    def col(i, n=128):
        return cols[0:n, i:i + 1]

    x_loaded = [sem(f"x_loaded{g}") for g in range(NG)]
    small_loaded = sem("small_loaded")
    bias_loaded = [sem(f"bias_loaded{j}") for j in range(GB)]
    memsets = sem("memsets")
    setup_v = sem("setup_v")
    setup_pe = sem("setup_pe")
    setup_a = sem("setup_a")
    xT_psum, xT_ready = sem("xT_psum"), sem("xT_ready")
    down_psum, gelu_ready = sem("down_psum"), sem("gelu_ready")
    exp_psum, eT_ready = sem("exp_psum"), sem("eT_ready")
    up_psum, up_read = sem("up_psum"), sem("up_read")
    xa_ready, x1_ready, pool_own = sem("xa_ready"), sem("x1_ready"), sem("pool_own")
    xn1_ready, yT_psum, yT_ready = sem("xn1_ready"), sem("yT_psum"), sem("yT_ready")
    qk_psum, qkf_ready, vy_psum, vy_read = sem("qk_psum"), sem("qkf_ready"), sem("vy_psum"), sem("vy_read")
    piece1, rest1, piece2, piece3 = sem("piece1"), sem("rest1"), sem("piece2"), sem("piece3")
    pieces_out = [sem(f"pieces_out{p}") for p in range(2)]
    stack_in = sem("stack_in")
    vaug_ready, mneg_ready = sem("vaug_ready"), sem("mneg_ready")
    scores_ready, scores_read = sem("scores_ready"), sem("scores_read")
    mp_ready, mT_psum, mT_ready = sem("mp_ready"), sem("mT_psum"), sem("mT_ready")
    xt_ready, exp_ready = sem("xt_ready"), sem("exp_ready")
    pv_done, ctxs_ready, ctxn_psum, ctxn_ready = (sem("pv_done"), sem("ctxs_ready"), sem("ctxn_psum"),
                                                  sem("ctxn_ready"))
    ctx2_psum, ctx2_ready, wo_psum, x2_ready = sem("ctx2_psum"), sem("ctx2_ready"), sem("wo_psum"), sem("x2_ready")
    l_act, den_v, pool_l2 = sem("l_act"), sem("den_v"), sem("pool_l2")
    att_v, l0_v, ffn_v, pre_v, moe_v = (sem("att_v"), sem("l0_v"), sem("ffn_v"), sem("pre_v"), sem("moe_v"))
    w2_loaded = [sem(f"w2_loaded{j}") for j in range(GB)]
    rows2_loaded = [sem(f"rows2_loaded{j}") for j in range(GB)]
    experts_loaded = sem("experts_loaded")
    xs_ready, xs_psum, hf_ready = sem("xs_ready"), sem("xs_psum"), sem("hf_ready")
    w1_psum, ff_ready, w2_psum, x3_ready, x2b_ready = (sem("w1_psum"), sem("ff_ready"), sem("w2_psum"),
                                                       sem("x3_ready"), sem("x2b_ready"))
    x3T_psum, x3T_ready = sem("x3T_psum"), sem("x3T_ready")
    wi_psum, h2_ready, wo2_psum, r3_ready = sem("wi_psum"), sem("h2_ready"), sem("wo2_psum"), sem("r3_ready")
    r3_sum, x4_ready = sem("r3_sum"), sem("x4_ready")
    e_xs, e_psum, e_hl, e_hfs, e_hcols = (sem(n) for n in ("e_xs", "e_psum", "e_hl", "e_hfs", "e_hcols"))
    e_logit, e_top, e_gate, e_comb, e_combT, e_cT, e_b2, e_acc = (
        sem(n) for n in ("e_logit", "e_top", "e_gate", "e_comb", "e_combT", "e_cT", "e_b2", "e_acc"))
    m_w1, m_hid, m_w2, m_acc, m_read = (sem(n) for n in ("m_w1", "m_hid", "m_w2", "m_acc", "m_read"))
    stored = sem("stored")

    block = ctx.enter_context(nc.Block())

    small = [
        (ident[:, :], dram["c_ident"]), (cst[:, :], dram["c_cols"]), (iota8[:, :], dram["c_iota8"].partition_broadcast(128)),
        (ids[:, 0, :], dram["itok_B_0_15"].partition_broadcast(128)),
        (ids[:, 1, :], dram["itok_B_34_63"].partition_broadcast(128)),
        (ids[:, 2, :], dram["itok_B_0_7"].partition_broadcast(128)),
        (ids[:, 3, :], dram["itok_B_6_14"].partition_broadcast(128)),
        (ew0[0:E0, :], dram["expert_W"]), (ew0[E0:E0 + 1, :], dram["c_eye_row"]),
        (sel_small[0:E0, 64:96], dram["expert_b"]), (sel_small[0:E0, 96:128], dram["domain_emb"]),
        (w_down[:, :], dram["down_WT"]), (w_up[:, :], dram["up_WTb"]),
        (cols[:, 0:C_B1 + FC], dram["cols"]), (w_ada[:, :], dram["W_ada"]),
        (rows[:, :, :], dram["rows"].partition_broadcast(128)),
        (w_q[:, :], dram["Wq"]), (w_k[:, :], dram["Wk"]), (w_vi[:, 0:D], dram["Wv"]), (w_vi[:, D:2 * D], dram["c_ident"]),
        (w_o[:, :], dram["Wo"]), (w_1[:, :], dram["W1"]), (w_2[:, :, :], dram["W2"]),
        (sel_small[0:SUB, 0:64], dram["subj_emb"]), (bi_sb[:, :], dram["bi"]),
        (w_h1[:, :], dram["hyp_w1"]), (w_h2[:, :], dram["hyp_w2"]), (w_s1[:, :], dram["sty_w1"]),
        (w_s2[:, :], dram["sty_w2"]), (w_r[:, :], dram["router_w"]), (be2[:, :], dram["exp_b2"]),
        (b1e[:, :], dram["exp_b1T"]), (mask[:, :, :], dram["mask"]),
    ]
    N_SMALL = 16 * len(small)

    @block.sync
    def _(sp):
        x_dram = dram["x"].rearrange("b s d -> s b d")

        def load_bias(b, j):
            sp.dma_start(biasx[:, j, :, :], dram["attn_bias"][b]).then_inc(bias_loaded[j], 16)

        for g in range(NG):
            sp.dma_start(x_in[:, g * GB:(g + 1) * GB, :], x_dram[:, g * GB:(g + 1) * GB, :]).then_inc(x_loaded[g], 16)
        for dst, src in small:
            sp.dma_start(dst, src).then_inc(small_loaded, 16)
        for j in range(GB):
            load_bias(j, j)

        def store_pieces(g, which):
            sp.wait_ge(piece3, 2 * g + which + 1)
            sp.dma_start(scr[which, :, :, g * GT:(g + 1) * GT].rearrange("p d t -> d p t"),
                         pieces[which][:, :, :]).then_inc(pieces_out[which], 16)

        def load_stack(g, par):
            for which, st_, pcs in ((0, qst, Q_PIECES), (1, kst, K_PIECES)):
                for c, p in enumerate(pcs):
                    sp.dma_start(st_[DH * c:DH * c + DH, par, :, :],
                                 scr[which, p, :, bass.ts(g, GT)].rearrange("(h r) t -> r h t", r=DH)
                                 ).then_inc(stack_in, 16)

        for g in range(NG):
            for which in range(2):
                store_pieces(g, which)
            if g == 0:
                sp.wait_ge(memsets, 2)
                sp.wait_ge(pieces_out[0], 16)
                sp.wait_ge(pieces_out[1], 16)
                load_stack(0, 0)
        sp.wait_ge(pieces_out[0], 16 * NG)
        sp.wait_ge(pieces_out[1], 16 * NG)
        with sp.Fori(0, NG - 1) as g:
            sp.wait_ge(scores_ready, g * GB * NQ)
            sp.wait_ge(stack_in, (g + 1) * 12 * 16)
            load_stack(g + 1, (g + 1) % 2)
            for j in range(GB):
                sp.wait_ge(xt_ready, (g * GB + j + 1) * NQ)
                load_bias((g + 1) * GB + j, j)
        sp.wait_ge(xn1_ready, NG)
        sp.dma_start(w1e, dram["exp_w1"].rearrange("e d f -> d e f")).then_inc(experts_loaded, 16)
        sp.dma_start(w2e, dram["exp_w2"]).then_inc(experts_loaded, 16)

        def load_l2(b, j):
            e = sp.value_load(id2[0:1, bass.ds(b, 1)], min_val=0, max_val=E2 - 1)
            sp.dma_start(w2slot[j], dram["l2_w"][e]).then_inc(w2_loaded[j], 16)

        def load_rows2(b, j):
            e = sp.value_load(id2[0:1, bass.ds(b, 1)], min_val=0, max_val=E2 - 1)
            sp.dma_start(rows2[j], dram["l2_rows"][e].partition_broadcast(128)).then_inc(rows2_loaded[j], 16)

        sp.wait_ge(setup_v, SETUP_ID2)
        for j in range(GB):
            sp.wait_ge(xt_ready, (B - GB + j + 1) * NQ)
            load_l2(j, j)
            load_rows2(j, j)
        with sp.Fori(1, NG) as g:
            for j in range(GB):
                wait_apart(sp, wo2_psum, (g - 1) * GB + j + 1, setup_v, SETUP_ID2)
                load_l2(g * GB + j, j)
            wait_apart(sp, x4_ready, g, setup_v, SETUP_ID2)
            for j in range(GB):
                load_rows2(g * GB + j, j)
        out_rows = out.rearrange("b s d -> s b d")
        with sp.Fori(0, NG) as g:
            sp.wait_ge(m_acc, (g + 1) * E3 * GB)
            sp.dma_start(out_rows[:, bass.ts(g, GB), :], x4[:, bass.ts(g, GB), :]).then_inc(stored, 16)
        sp.wait_ge(stored, 16 * NG)

    @block.tensor
    def _(pe):
        def mm(o, l, r, start=True, stop=True, **kw):
            return pe.matmul(o, l, r, start=start, stop=stop, **kw)

        pe.wait_ge(small_loaded, N_SMALL)
        pe.wait_ge(setup_v, SETUP_ONEHOT)
        for o in range(A0):
            ins = mm(ps[0:A0, 4, o * B:(o + 1) * B], ew0[:, o * A0:(o + 1) * A0], oh[0:E0 + 1, 0, :])
        ins.then_inc(setup_pe, 1)
        mm(ps[0:A0, 5, 0:B], sel_small[0:E0, 64:96], oh[0:E0, 0, :], stop=False)
        mm(ps[0:A0, 5, 0:B], sel_small[0:E0, 96:128], oh[0:E0, 1, :], start=False).then_inc(setup_pe, 1)
        for c in range(FC):
            ins = mm(ps[:, 6, 32 + c * B:32 + (c + 1) * B], bi_sb[:, c * 128:(c + 1) * 128], oh[0:E2, 2, :])
        mm(ps[0:SE, 7, 0:B], sel_small[0:SUB, 0:64], oh[0:SUB, 3, :]).then_inc(setup_pe, 1)
        pe.wait_ge(setup_a, 1)
        for i in range(2):
            ins = mm(ps[:, 6, i * B:(i + 1) * B], w_ada[:, i * D:(i + 1) * D], tmp[:, 7, :])
        ins.then_inc(setup_pe, 1)

        for g in range(NG):
            pe.wait_ge(x_loaded[g], 16)
            if g >= 2:
                pe.wait_ge(xT_ready, g - 1)
            for j in range(GB):
                ins = pe.transpose(bank4(g % 2)[:, j, :], x_in[:, g * GB + j, :], ident[:, :])
            ins.then_inc(xT_psum, 1)
        pe.wait_ge(setup_a, 2)
        mm(ps[:, 7, 16:32], w_h1[:, :], hyp[0:SE, 0, :]).then_inc(setup_pe, 1)
        for g in range(NG):
            pe.wait_ge(xT_ready, g + 1)
            if g >= 2:
                pe.wait_ge(gelu_ready, g - 1)
            mm(ps[0:A0, 2 + g % 2, :], w_down[:, :], xT[:, g * GT:(g + 1) * GT]).then_inc(down_psum, 1)
        pe.wait_ge(setup_a, 3)
        mm(ps[:, 7, 32:48], w_h2[:, :], hyp[:, 1, :]).then_inc(setup_pe, 1)
        pe.wait_ge(setup_v, SETUP_WSEL)
        for g in range(NG):
            pe.wait_ge(gelu_ready, g + 1)
            if g >= 2:
                pe.wait_ge(eT_ready, g - 1)
            for j in range(GB):
                b = g * GB + j
                ins = mm(ps[0:A0, 4 + g % 2, j * S:(j + 1) * S], wsel[:, b, :], hT[:, b * S:(b + 1) * S])
            ins.then_inc(exp_psum, 1)
        pe.wait_ge(setup_a, 4)
        mm(ps[0:64, 7, 48:64], w_s1[:, :], hyp[:, 2, :]).then_inc(setup_pe, 1)
        pe.wait_ge(setup_a, 5)
        mm(ps[:, 7, 64:80], w_s2[:, 0:128], hyp[0:64, 3, :])
        mm(ps[:, 7, 80:96], w_s2[:, 128:256], hyp[0:64, 3, :]).then_inc(setup_pe, 1)
        pe.wait_ge(setup_a, 6)
        pe.wait_ge(memsets, 1)
        pe.wait_ge(setup_v, SETUP_ADA)
        for g in range(NG):
            pe.wait_ge(eT_ready, g + 1)
            if g >= 2:
                pe.wait_ge(up_read, g - 1)
            for j in range(GB):
                b = g * GB + j
                ins = mm(bank4(6 + g % 2)[:, j, :], eT[:, b * S:(b + 1) * S], w_up[:, :])
            ins.then_inc(up_psum, 1)

        for g in range(NG):
            pe.wait_ge(xn1_ready, g + 1)
            if g >= 2:
                pe.wait_ge(yT_ready, g - 1)
            for j in range(GB):
                ins = pe.transpose(bank4(g % 2)[:, j, :], xn1[:, g * GB + j, :], ident[:, :])
            ins.then_inc(yT_psum, 1)
            pe.wait_ge(yT_ready, g + 1)
            y = yT[g % 2][:, :, :].rearrange("p b s -> p (b s)")
            for which, w in ((0, w_q), (1, w_k)):
                if g >= 1:
                    pe.wait_ge(qkf_ready, 2 * g - 1 + which)
                mm(ps[:, 2 + which, :], w[:, :], y).then_inc(qk_psum, 1)
            if g == 0:
                pe.wait_ge(up_read, NG)
            if g >= 2:
                pe.wait_ge(vy_read, g - 1)
            for j in range(GB):
                bank = 4 + 2 * (g % 2) + j // 2
                ins = mm(ps[:, bank, (j % 2) * 256:(j % 2) * 256 + 256], yT[g % 2][:, j, :], w_vi[:, :])
            ins.then_inc(vy_psum, 1)

        def scores(tn, gn, jn, q):
            if q == 0:
                pe.wait_ge(mneg_ready, tn + 1)
                if jn == 0:
                    pe.wait_ge(stack_in, (gn + 1) * 12 * 16)
            if not (isinstance(tn, int) and 4 * tn + q < 2):
                pe.wait_ge(scores_read, NQ * tn + q - 1)
            par = gn % 2
            for i in range(HQ):
                h = q * HQ + i
                mm(bank4(q % 2)[:, i, :], qst[:, par, h, jn * S:(jn + 1) * S],
                         kst[:, par, h, jn * S:(jn + 1) * S], start=(i == 0), stop=False,
                         skip_group_check=True)
            mm(bank4(q % 2), maskedb[:, :], mneg[jn % 2][:, :].unsqueeze(1).to_broadcast([128, HQ, S]),
               start=False, skip_group_check=True).then_inc(scores_ready, 1)

        def turn(t, j, q):
            if not (isinstance(t, int) and 4 * t + q < 2):
                pe.wait_ge(exp_ready, NQ * t + q - 1)
            for i in range(HQ):
                pe.matmul(bank4(2 + q % 2)[:, i, :], biasx[:, j, q * HQ + i, :], ident[:, :], start=(i == 0),
                          stop=False, is_transpose=True, skip_group_check=True)
            for i in range(HQ):
                ins = mm(bank4(2 + q % 2)[:, i, :], msel[:, q * HQ + i:q * HQ + i + 1].to_broadcast([128, S]), mT[:, :], start=False,
                         stop=True, skip_group_check=True)
            ins.then_inc(xt_ready, 1)

        def values(t, j, q):
            pe.wait_ge(exp_ready, NQ * t + q + 1)
            if q == 0:
                pe.wait_ge(vaug_ready, t + 1)
                if not (isinstance(t, int) and t == 0):
                    pe.wait_ge(ctxs_ready, t)
            for i in range(HQ):
                ins = mm(ps[CW * i:CW * i + CW, 4, q * S:(q + 1) * S], vaug[j % 2][:, q * HQ + i, :],
                         pT[q % 2][:, i, :], tile_position=(0, CW * i))
            ins.then_inc(pv_done, 1)

        def project_a(t):
            pe.wait_ge(ctxs_ready, t + 1)
            if not (isinstance(t, int) and t == 0):
                pe.wait_ge(ctxn_ready, t)
            for q in range(NQ):
                ins = pe.transpose(bank4(6)[:, q, :], ctxs[:, q, :], ident[:, :])
            ins.then_inc(ctxn_psum, 1)

        def project_b(t):
            pe.wait_ge(ctxn_ready, t + 1)
            if not (isinstance(t, int) and t == 0):
                pe.wait_ge(x2_ready, t)
            pe.transpose(ps[:, 7, 0:128], ctxn[:, :], ident[:, :]).then_inc(ctx2_psum, 1)

        def project_c(t):
            pe.wait_ge(ctx2_ready, t + 1)
            mm(ps[:, 7, 128:256], ctx2T[:, :], w_o[:, :]).then_inc(wo_psum, 1)

        def attend(t, g, j, first, last):
            nxt = (t + 1, g if j < GB - 1 else g + 1, (j + 1) % GB)
            if not last:
                scores(*nxt, 0)
                scores(*nxt, 1)
            pe.wait_ge(mp_ready, t + 1)
            if not first:
                pe.wait_ge(mT_ready, t)
            pe.transpose(ps[:, 5, 0:64].bitcast(BF16), mp[:, :], identb[:, :]).then_inc(mT_psum, 1)
            if not first:
                project_a(t - 1)
            pe.wait_ge(mT_ready, t + 1)
            turn(t, j, 0)
            if not first:
                project_b(t - 1)
            turn(t, j, 1)
            if not last:
                scores(*nxt, 2)
            values(t, j, 0)
            if not first:
                project_c(t - 1)
            turn(t, j, 2)
            if not last:
                scores(*nxt, 3)
            values(t, j, 1)
            turn(t, j, 3)
            values(t, j, 2)
            values(t, j, 3)

        pe.wait_ge(memsets, 5)
        pe.wait_ge(yT_ready, NG)
        pe.wait_ge(qkf_ready, 2 * NG)
        pe.wait_ge(vy_read, NG)
        for q in range(NQ):
            scores(0, 0, 0, q)
        for j in range(GB):
            attend(j, 0, j, j == 0, False)
        with pe.Fori(1, NG - 1) as g:
            for j in range(GB):
                attend(g * GB + j, g, j, False, False)
        for j in range(GB):
            attend(B - GB + j, NG - 1, j, False, j == GB - 1)
        project_a(B - 1)
        project_b(B - 1)
        project_c(B - 1)

        pe.wait_ge(x2_ready, B)
        pe.wait_ge(exp_ready, NQ * B)
        with pe.Fori(0, NG // 2) as it:
            def ff_hidden(p):
                n = 2 * it + p
                pe.wait_ge(xs_ready, n + 1)
                for j in range(GB):
                    ins = pe.transpose(bank4(p)[:, j, :], xs[p][:, j, :], ident[:, :])
                ins.then_inc(xs_psum, 1)
                pe.wait_ge(hf_ready, n + 1)
                for c in range(FC):
                    if p == 0:
                        pe.wait_ge(h2_ready, 8 * it)
                    else:
                        pe.wait_ge(ff_ready, FC * (n - 1) + c + 1)
                    mm(ps[:, 2 + c, :], w_1[:, c * 128:(c + 1) * 128], hf[p]).then_inc(w1_psum, 1)

            def ff_out(p):
                n = 2 * it + p
                pe.wait_ge(ff_ready, FC * (n + 1))
                pe.wait_ge(r3_sum, 2 * it)
                for j in range(GB):
                    for c in range(FC):
                        ins = mm(bank4(6 + p)[:, j, :], ffT[p][:, c, j * S:(j + 1) * S], w_2[:, c, :],
                                 start=(c == 0), stop=(c == FC - 1))
                ins.then_inc(w2_psum, 1)

            def l2_turn(p):
                pe.wait_ge(x3_ready, 2 * it + p + 1)
                for j in range(GB):
                    ins = pe.transpose(bank4(p)[:, j, :], x3[p][:, j, :], ident[:, :])
                ins.then_inc(x3T_psum, 1)

            def l2_hidden(p, j):
                b = 8 * it + 4 * p + j
                if j == 0:
                    pe.wait_ge(x3T_ready, 2 * it + p + 1)
                pe.wait_ge(w2_loaded[j], 16 * (2 * it + p + 1))
                if 4 * p + j >= 4:
                    pe.wait_ge(h2_ready, b - 3)
                for c in range(FC):
                    ins = mm(bank4(2 + j)[:, c, :], w2slot[j][:, c * 128:(c + 1) * 128],
                             hf[p][:, j * S:(j + 1) * S])
                ins.then_inc(wi_psum, 1)

            def l2_out(p, j):
                b = 8 * it + 4 * p + j
                pe.wait_ge(h2_ready, b + 1)
                for c in range(FC):
                    ins = mm(bank4(6 + p)[:, j, :], h2T[j % 2][:, c, :],
                             w2slot[j][:, 512 + c * 128:512 + (c + 1) * 128], start=(c == 0), stop=(c == FC - 1))
                ins.then_inc(wo2_psum, 1)

            ff_hidden(0)
            ff_hidden(1)
            ff_out(0)
            ff_out(1)
            l2_turn(0)
            pe.wait_ge(ff_ready, FC * (2 * it + 2))
            for n in range(8):
                p, j = n // 4, n % 4
                l2_hidden(p, j)
                if n == 3:
                    l2_turn(1)
                if n:
                    l2_out((n - 1) // 4, (n - 1) % 4)
            l2_out(1, 3)

        pe.wait_ge(r3_sum, NG)
        pe.wait_ge(h2_ready, B)
        with pe.Fori(0, NG) as g:
            pe.wait_ge(e_xs, g + 1)
            for j in range(GB):
                ins = pe.transpose(bank4(0)[:, j, :], xs[0][:, j, :], ident[:, :])
            ins.then_inc(e_psum, 1)
            pe.wait_ge(e_hfs, g + 1)
            for j in range(GB):
                ins = mm(ps[:, 1, j * E3:(j + 1) * E3], hfs[:, j, :], w_r[:, :])
            ins.then_inc(e_logit, 1)
            pe.wait_ge(e_comb, g + 1)
            for j in range(GB):
                ins = pe.transpose(ps[0:E3, 2, j * S:(j + 1) * S], combs[:, j, :], ident[:, :])
            ins.then_inc(e_combT, 1)
            pe.wait_ge(e_cT, g + 1)
            for j in range(GB):
                ins = mm(bank4(3)[:, j, :], combT[:, j * S:(j + 1) * S], be2[:, :])
            ins.then_inc(e_b2, 1)

        pe.wait_ge(experts_loaded, 32)
        pe.wait_ge(e_acc, NG)
        with pe.Fori(0, NG) as g:
            def hidden(e):
                n = g * E3 + e
                if e == 0:
                    pe.wait_ge(e_hcols, g + 1)
                for c in range(FC):
                    pe.wait_ge(m_hid, FC * n + c - FC + 1) if e else pe.wait_ge(m_hid, FC * n)
                    mm(ps[:, c, :], w1e[:, e, c * 128:(c + 1) * 128], hcols[:, bass.ts(g, GT)]).then_inc(m_w1, 1)

            def output(e):
                n = g * E3 + e
                pe.wait_ge(m_hid, FC * (n + 1))
                if e >= 2:
                    pe.wait_ge(m_acc, GB * (n - 1))
                else:
                    pe.wait_ge(m_acc, GB * E3 * g)
                for j in range(GB):
                    for c in range(FC):
                        ins = mm(bank4(4 + e % 2)[:, j, :], ffT[e % 2][:, c, j * S:(j + 1) * S], w2e[:, e, c, :],
                                 start=(c == 0), stop=(c == FC - 1))
                ins.then_inc(m_w2, 1)

            hidden(0)
            for e in range(1, E3):
                hidden(e)
                output(e - 1)
            output(E3 - 1)

    @block.scalar
    def _(act):
        def affine(o, i, scale, bias):
            return act.activation(o, i, ACT.Identity, scale=scale, bias=bias)

        act.wait_ge(setup_v, SETUP_ANGLE)
        act.activation(tmp[:, 6, :], tmp[:, 5, :], ACT.Sin).then_inc(l_act, 1)
        act.wait_ge(l_act, 1)
        act.activation(tmp[:, 7, :], tmp[:, 6, :], ACT.Silu).then_inc(setup_a, 1)
        act.preload_act_table(ACT.Gelu)
        act.wait_ge(setup_pe, 3)
        act.activation(hyp[0:SE, 0, :], ps[0:SE, 7, 0:B], ACT.Copy).then_inc(setup_a, 1)
        for g in range(NG):
            act.wait_ge(xT_psum, g + 1)
            act.activation(xT[:, g * GT:(g + 1) * GT], ps[:, g % 2, :], ACT.Copy).then_inc(xT_ready, 1)
        act.wait_ge(setup_pe, 5)
        act.activation(hyp[:, 1, :], ps[:, 7, 16:32], ACT.Relu, bias=col(C_HB1)).then_inc(setup_a, 1)
        for g in range(NG):
            act.wait_ge(down_psum, g + 1)
            act.activation(hT[:, g * GT:(g + 1) * GT], ps[0:A0, 2 + g % 2, :], ACT.Gelu,
                           bias=col(C_DOWN, A0)).then_inc(gelu_ready, 1)
        act.wait_ge(setup_pe, 6)
        affine(hyp[:, 2, :], ps[:, 7, 32:48], 1.0, col(C_HB2)).then_inc(setup_a, 1)
        act.wait_ge(setup_pe, 7)
        act.activation(hyp[0:64, 3, :], ps[0:64, 7, 48:64], ACT.Relu, bias=col(C_SB1, 64)).then_inc(setup_a, 1)
        act.wait_ge(setup_pe, 8)
        affine(sty[:, 2, :], ps[:, 7, 64:80], 1.0, col(C_SG)).then_inc(l_act, 1)
        affine(sty[:, 1, :], ps[:, 7, 80:96], 1.0, col(C_SB)).then_inc(setup_a, 1)

        act.wait_ge(setup_v, SETUP_ADA)
        act.preload_act_table(ACT.Exp)
        for g in range(NG):
            act.wait_ge(yT_psum, g + 1)
            if g >= 2:
                act.wait_ge(vy_psum, g - 1)
            for j in range(GB):
                b = g * GB + j
                ins = affine(yT[g % 2][:, j, :], bank4(g % 2)[:, j, :], ada[:, 0, b:b + 1], ada[:, 1, b:b + 1])
            ins.then_inc(yT_ready, 1)
            for which, cb, sc in ((0, C_BQ, DH ** -0.5), (1, C_BK, 1.0)):
                act.wait_ge(qk_psum, 2 * g + which + 1)
                if g >= 1:
                    act.wait_ge(piece3, 2 * g - 1 + which)
                affine(qkf[which][:, :], ps[:, 2 + which, :], sc, col(cb)).then_inc(qkf_ready, 1)

        def context_out(t):
            act.wait_ge(pv_done, NQ * (t + 1))
            if not (isinstance(t, int) and t == 0):
                act.wait_ge(ctxn_psum, t)
            act.activation(ctxs[:, :, :], bank4(4), ACT.Copy).then_inc(ctxs_ready, 1)

        def context_turned(t):
            act.wait_ge(ctx2_psum, t + 1)
            if not (isinstance(t, int) and t == 0):
                act.wait_ge(wo_psum, t)
            act.activation(ctx2T[:, :], ps[:, 7, 0:128], ACT.Copy).then_inc(ctx2_ready, 1)

        def exponent(t, q):
            act.wait_ge(xt_ready, NQ * t + q + 1)
            if not (isinstance(t, int) and 4 * t + q < 2):
                act.wait_ge(pv_done, NQ * t + q - 1)
            act.activation(pT[q % 2], bank4(2 + q % 2), ACT.Exp).then_inc(exp_ready, 1)

        def attend(t, first):
            if not first:
                context_out(t - 1)
            act.wait_ge(mT_psum, t + 1)
            if not first:
                act.wait_ge(xt_ready, NQ * t)
            act.activation(mT[:, :], ps[:, 5, 0:64].bitcast(BF16), ACT.Copy).then_inc(mT_ready, 1)
            exponent(t, 0)
            if not first:
                context_turned(t - 1)
            for q in range(1, NQ):
                exponent(t, q)

        for j in range(GB):
            attend(j, j == 0)
        with act.Fori(1, NG) as g:
            for j in range(GB):
                attend(g * GB + j, False)
        context_out(B - 1)
        context_turned(B - 1)

        with act.Fori(0, NG // 2) as it:
            for p in range(2):
                n = 2 * it + p
                act.wait_ge(xs_psum, n + 1)
                if p == 0:
                    act.wait_ge(wi_psum, 8 * it)
                else:
                    act.wait_ge(wi_psum, 8 * it)
                affine(hf[p], ps[:, p, :], col(C_G2), col(C_BETA2)).then_inc(hf_ready, 1)
                act.wait_ge(w2_psum, 2 * it)
                for c in range(FC):
                    act.wait_ge(w1_psum, FC * n + c + 1)
                    act.activation(ffT[p][:, c, :], ps[:, 2 + c, :], ACT.Gelu_apprx_sigmoid,
                                   bias=col(C_B1 + c)).then_inc(ff_ready, 1)
            for p in range(2):
                def turned(p=p):
                    act.wait_ge(x3T_psum, 2 * it + p + 1)
                    act.wait_ge(w1_psum, FC * (2 * it + 2))
                    act.activation(hf[p], ps[:, p, :], ACT.Copy).then_inc(x3T_ready, 1)
                if p == 0:
                    turned()
                for j in range(GB):
                    b = 8 * it + 4 * p + j
                    act.wait_ge(wi_psum, b + 1)
                    if 4 * p + j >= 2:
                        act.wait_ge(wo2_psum, b - 1)
                    else:
                        act.wait_ge(wo2_psum, 8 * it)
                    for c in range(FC):
                        ins = act.activation(h2T[j % 2][:, c, :], bank4(2 + j)[:, c, :], ACT.Gelu,
                                             bias=bi2[:, c, bass.ds(b, 1)])
                    ins.then_inc(h2_ready, 1)
                    if p == 0 and j == 3:
                        turned(1)

        act.wait_ge(l_act, 2)
        act.activation(sty[:, 3, :], sty[:, 2, :], ACT.Abs).then_inc(l_act, 1)
        act.wait_ge(l_act, 3)
        act.activation(sty[:, 3, :], sty[:, 3, :], ACT.Exp, scale=-1.0).then_inc(l_act, 1)
        act.wait_ge(l_act, 4)
        act.activation(sty[:, 3, :], sty[:, 3, :], ACT.Ln, bias=1.0).then_inc(l_act, 1)
        act.preload_act_table(ACT.Exp)
        with act.Fori(0, NG) as g:
            act.wait_ge(e_psum, g + 1)
            act.wait_ge(e_hfs, g)
            affine(hl, bank4(0), col(C_LNG), col(C_LNB)).then_inc(e_hl, 1)
            act.wait_ge(e_top, g + 1)
            act.activation(gate[:, 1, :], gate[:, 0, :], ACT.Exp).then_inc(e_gate, 1)
            act.wait_ge(e_combT, g + 1)
            act.wait_ge(e_b2, g)
            act.activation(combT[:, :], ps[0:E3, 2, :], ACT.Copy).then_inc(e_cT, 1)
        with act.Fori(0, NG) as g:
            for e in range(E3):
                n = g * E3 + e
                if e >= 2:
                    act.wait_ge(m_w2, n - 1)
                else:
                    act.wait_ge(m_w2, E3 * g)
                for c in range(FC):
                    act.wait_ge(m_w1, FC * n + c + 1)
                    act.activation(ffT[e % 2][:, c, :], ps[:, c, :], ACT.Relu,
                                   bias=b1e[:, e * FC + c:e * FC + c + 1]).then_inc(m_hid, 1)

    def rsqrt(ch, v, var, eps, n):
        ve, a, y = rs[:, 0, 0:n], rs[:, 1, 0:n], rs[:, 3, 0:n]
        ch.step(v.tensor_scalar(ve, var, eps, None, ALU.add))
        ch.step(v.tensor_scalar(a.bitcast(I32), ve.bitcast(I32), 1, None, ALU.logical_shift_right))
        ch.step(v.tensor_scalar(y.bitcast(I32), a.bitcast(I32), -1.0, float(0x5F3759DF), ALU.mult, ALU.add))
        for _ in range(3):
            ch.step(v.tensor_tensor(a, y, y, ALU.mult))
            ch.step(v.scalar_tensor_tensor(out=a, in0=a, scalar=-0.5, in1=ve, op0=ALU.mult, op1=ALU.mult))
            ch.step(v.scalar_tensor_tensor(out=y, in0=a, scalar=1.5, in1=y, op0=ALU.add, op1=ALU.mult))

    def norm_stats(ch, v, src, eps):
        for j in range(GB):
            ch.did(v.bn_stats(st[:, j, :], src(j)))
        ch.join_apart(small_loaded, N_SMALL)
        for j in range(GB):
            ch.did(v.bn_aggr(mv[:, j, :], st[:, j, :]))
        ch.join()
        rsqrt(ch, v, mv[:, :, 1], eps, GB)

    def apply_norm(v, o, i, j):
        return v.tensor_scalar(o, i, mv[:, j, 0:1], rs[:, 3, j:j + 1], ALU.subtract, ALU.mult)

    @block.vector
    def _(v):
        ch = Chain(v, setup_v)
        v.wait_ge(small_loaded, N_SMALL)
        ch.step(v.tensor_copy(idf[:, 0:4, :], ids[:, :, :]))
        id0, tim, i2, i3 = (idf[:, i, :] for i in range(4))
        ch.did(v.tensor_scalar(idf[:, 4, :], id0, 0.0, float(E0 - 1), ALU.max, ALU.min))
        ch.did(v.tensor_scalar(idf[:, 7, :], id0, -float(E0), None, ALU.add))
        ch.did(v.tensor_scalar(tmp[:, 0, :], tim, 40.0, FREQ, ALU.mult, ALU.mult))
        ch.did(v.tensor_scalar(i2, i2, 0.0, float(E2 - 1), ALU.max, ALU.min))
        ch.did(v.tensor_scalar(i3, i3, 0.0, float(SUB - 1), ALU.max, ALU.min))
        ch.join()
        ch.did(v.tensor_tensor(idf[:, 5, :], idf[:, 4, :], id0, ALU.is_equal))
        ch.did(v.tensor_scalar(oh[:, 1, :], idf[:, 4, :], IOTA, None, ALU.is_equal))
        ch.did(v.tensor_scalar(oh[:, 2, :], i2, IOTA, None, ALU.is_equal))
        ch.did(v.tensor_scalar(oh[:, 3, :], i3, IOTA, None, ALU.is_equal))
        ch.did(v.tensor_copy(id2[:, :], i2[0:1, :]))
        ch.join()
        assert ch.n == SETUP_ID2, ch.n
        ch.step(v.tensor_tensor(idf[:, 6, :], idf[:, 7, :], idf[:, 5, :], ALU.mult))
        ch.step(v.tensor_scalar(idf[:, 6, :], idf[:, 6, :], float(E0), None, ALU.add))
        ch.step(v.tensor_scalar(oh[:, 0, :], idf[:, 6, :], IOTA, None, ALU.is_equal))
        assert ch.n == SETUP_ONEHOT, ch.n
        ch.step(v.tensor_scalar(tmp[:, 1, :], tmp[:, 0, :], 1.0 / (2.0 * np.pi), TURN, ALU.mult, ALU.add))
        ch.step(v.tensor_scalar(tmp[:, 2, :], tmp[:, 1, :], ROUNDER, None, ALU.add))
        ch.step(v.tensor_scalar(tmp[:, 2, :], tmp[:, 2, :], -ROUNDER, None, ALU.add))
        for part in TWO_PI_PARTS:
            ch.step(v.scalar_tensor_tensor(out=tmp[:, 0, :], in0=tmp[:, 2, :], scalar=-part, in1=tmp[:, 0, :],
                                           op0=ALU.mult, op1=ALU.add))
        ch.step(v.tensor_scalar(tmp[:, 0, :], tmp[:, 0, :], PHASE, float(np.float32(3.1415925)), ALU.add, ALU.min))
        ch.step(v.tensor_scalar(tmp[:, 5, :], tmp[:, 0, :], -float(np.float32(3.1415925)), None, ALU.max))
        assert ch.n == SETUP_ANGLE, ch.n
        v.wait_ge(setup_pe, 1)
        ch.did(v.tensor_copy(wsel[:, :, :], ps[0:A0, 4, :].rearrange("p (o b) -> p b o", o=A0)))
        v.wait_ge(setup_pe, 2)
        ch.did(v.tensor_copy(domb[:, :], ps[0:A0, 5, 0:B]))
        assert ch.n == SETUP_WSEL, ch.n
        v.wait_ge(setup_pe, 4)
        ch.did(v.tensor_copy(bi2[:, :, :], ps[:, 6, 32:32 + FC * B].rearrange("p (c b) -> p c b", c=FC)))
        ch.did(v.tensor_scalar(ada[:, 0, :], ps[:, 6, 0:B], col(C_ADA0), 1.0, ALU.add, ALU.add))
        ch.did(v.tensor_scalar(ada[:, 1, :], ps[:, 6, B:2 * B], col(C_ADA1), None, ALU.add))
        ch.did(v.tensor_reduce(nanfix[:, :], mask[:, :, :], AX, ALU.min))
        ch.did(v.tensor_scalar(col(C_BQ), col(C_BQ), DH ** -0.5, None, ALU.mult))
        ch.join()
        assert ch.n == SETUP_ADA, ch.n
        ch.step(v.tensor_scalar(nanfix[:, :], nanfix[:, :], 3.0e38, 3.0e38, ALU.mult, ALU.mult))
        ch.step(v.tensor_scalar(nanfix[:, :], nanfix[:, :], 0.0, None, ALU.mult))

        lc = Chain(v, l0_v)
        for g in range(NG):
            v.wait_ge(exp_psum, g + 1)
            v.tensor_tensor(eT[0:A0, g * GT:(g + 1) * GT].rearrange("p (b s) -> p b s", b=GB),
                            ps[0:A0, 4 + g % 2, :].rearrange("p (b s) -> p b s", b=GB),
                            domb[:, g * GB:(g + 1) * GB].unsqueeze(2).to_broadcast([A0, GB, S]),
                            ALU.add).then_inc(eT_ready, 1)

        def l0_first(g):
            sl = slice(g * GB, (g + 1) * GB)
            v.wait_ge(up_psum, g + 1)
            v.tensor_tensor(x1[:, sl, :], bank4(6 + g % 2), x_in[:, sl, :], ALU.add).then_inc(up_read, 1)
            v.wait_ge(up_read, g + 1)
            norm_stats(lc, v, lambda j: x1[:, g * GB + j, :], 1e-5)
            for j in range(GB):
                ins = apply_norm(v, xn1[:, g * GB + j, :], x1[:, g * GB + j, :], j)
            ins.then_inc(xa_ready, 1)
            v.wait_ge(xa_ready, g + 1)

        def l0_second(g):
            v.wait_ge(x1_ready, g + 1)
            norm_stats(lc, v, lambda j: x1[:, g * GB + j, :], 1e-5)
            for j in range(GB):
                ins = apply_norm(v, xn1[:, g * GB + j, :], x1[:, g * GB + j, :], j)
                if j < GB - 1:
                    lc.did(ins)
            ins.then_inc(xn1_ready, 1)

        def project_in(g):
            for which in range(2):
                v.wait_ge(qkf_ready, 2 * g + which + 1)
                if g:
                    v.wait_ge(pieces_out[which], 16 * g)
                v.tensor_copy(pieces[which][:, 0, :], qkf[which][:, :]).then_inc(piece1, 1)
                v.wait_ge(rest1, 2 * g + which + 1)
                v.tensor_copy(pieces[which][:, 1, :], qkf[which][:, :]).then_inc(piece2, 1)
            sl = slice(g * GB, (g + 1) * GB)
            v.wait_ge(vy_psum, g + 1)
            b0 = 4 + 2 * (g % 2)
            vy = ps[:, b0:b0 + 2, :].rearrange("p n (j c) -> p (n j) c", j=2)
            lc.did(v.tensor_tensor(v_rows[:, sl, :], vy[:, :, 0:D], rows[:, 2:3, :].to_broadcast([S, GB, D]), ALU.add))
            v.tensor_tensor(y_rows[:, sl, :], vy[:, :, D:2 * D], rows[:, 3:4, :].to_broadcast([S, GB, D]),
                            ALU.add).then_inc(vy_read, 1)

        for g in range(NG):
            l0_first(g)
            if g:
                l0_second(g - 1)
        project_in(0)
        l0_second(NG - 1)
        for g in range(1, NG):
            project_in(g)

        v.wait_ge(memsets, 6)
        NATT = 3
        def attend(t, j, first):
            for q in range(NQ):
                if q == 0:
                    g1 = (t - j + GB)
                    v.wait_ge(bias_loaded[j], 4 * g1)
                wait_apart(v, scores_ready, NQ * t + q + 1, small_loaded, N_SMALL)
                for i in range(HQ):
                    h = q * HQ + i
                    ins = v.tensor_tensor_reduce(biasx[:, j, h, :], bank4(q % 2)[:, i, :], biasx[:, j, h, :], 1.0,
                                                 -3.0e38, ALU.add, ALU.max, mx[:, j % 2, h:h + 1])
                ins.then_inc(scores_read, 1)
                if q == 1 and not (isinstance(t, int) and t < 2):
                        finish(t - 2)
            v.wait_ge(scores_read, NQ * (t + 1))
            if not first:
                v.wait_ge(mT_psum, t)
            m, n = mx[:, j % 2, :], NATT * t
            v.tensor_scalar(mp[:, 0:16], m, -1.0, None, ALU.mult).then_inc(att_v, 1)
            v.wait_ge(att_v, n + 1)
            v.scalar_tensor_tensor(out=mres[:, :], in0=m, scalar=-1.0, in1=mp[:, 0:16], op0=ALU.mult,
                                   op1=ALU.subtract).then_inc(att_v, 1)
            v.wait_ge(att_v, n + 2)
            v.tensor_copy(mp[:, 16:32], mres[:, :]).then_inc(att_v, 1)
            v.wait_ge(att_v, n + 3)
            v.tensor_tensor(mp[:, 32:48], mres[:, :], mp[:, 16:32], ALU.subtract).then_inc(mp_ready, 1)
            v.wait_ge(mp_ready, t + 1)
            if not first:
                divide(t - 1)

        def divide(t):
            v.wait_ge(ctxn_psum, t + 1)
            if not (isinstance(t, int) and t == 0):
                v.wait_ge(ctx2_psum, t)
            nat = bank4(6).rearrange("p q (i r) -> p (q i) r", i=HQ)
            v.tensor_scalar(den[:, :], nat[:, :, DH], nanfix[:, bass.ds(t, 1)], None, ALU.add).then_inc(den_v, 1)
            v.wait_ge(den_v, 2 * t + 1)
            v.reciprocal(rden[:, :], den[:, :]).then_inc(den_v, 1)
            v.wait_ge(den_v, 2 * t + 2)
            v.tensor_tensor(ctxn[:, :].rearrange("p (h r) -> p h r", h=H), nat[:, :, 0:DH],
                            rden[:, :].unsqueeze(2).to_broadcast([S, H, DH]), ALU.mult).then_inc(ctxn_ready, 1)

        def finish(t):
            v.wait_ge(wo_psum, t + 1)
            v.tensor_tensor(x2[:, bass.ds(t, 1), :].rearrange("p a d -> p (a d)"), ps[:, 7, 128:256],
                            y_rows[:, bass.ds(t, 1), :].rearrange("p a d -> p (a d)"), ALU.add).then_inc(x2_ready, 1)

        for j in range(GB):
            attend(j, j, j == 0)
        with v.Fori(1, NG) as g:
            for j in range(GB):
                attend(g * GB + j, j, False)
        finish(B - 2)
        divide(B - 1)
        finish(B - 1)

        NFF = 100
        with v.Fori(0, NG // 2) as it:
            fc = Chain(v, ffn_v, it * NFF)
            for p in range(2):
                g = 2 * it + p
                v.wait_ge(x2_ready, GB * (g + 1))
                if p == 0:
                    v.wait_ge(ffn_v, it * NFF)
                norm_stats(fc, v, lambda j: x2[:, bass.ds(g * GB + j, 1), :].rearrange("p a d -> p (a d)"), 1e-5)
                v.wait_ge(xs_psum, 2 * it)
                for j in range(GB):
                    ins = apply_norm(v, xs[p][:, j, :], x2[:, bass.ds(g * GB + j, 1), :].rearrange("p a d -> p (a d)"), j)
                    if j < GB - 1:
                        fc.did(ins)
                ins.then_inc(xs_ready, 1)
                v.wait_ge(xs_ready, g + 1)
            for p in range(2):
                g = 2 * it + p
                v.wait_ge(w2_psum, g + 1)
                v.wait_ge(x2b_ready, g + 1)
                v.wait_ge(r3_ready, 2 * it)
                v.tensor_tensor(x3[p], bank4(6 + p), x2[:, bass.ts(g, GB), :], ALU.add).then_inc(x3_ready, 1)
            for p in range(2):
                g = 2 * it + p
                v.wait_ge(wo2_psum, GB * (g + 1))
                v.wait_ge(x3_ready, g + 1)
                v.tensor_tensor(r3, bank4(6 + p), x3[p], ALU.add).then_inc(r3_sum, 1)
                v.wait_ge(r3_sum, g + 1)
                for j in range(GB):
                    v.wait_ge(rows2_loaded[j], 16 * (g + 1))
                    fc.did(v.tensor_tensor(r3[:, j, :], r3[:, j, :], rows2[j][:, 0, :], ALU.add))
                fc.join()
                norm_stats(fc, v, lambda j: r3[:, j, :], 1e-12)
                v.wait_ge(x4_ready, g)
                for j in range(GB):
                    ins = apply_norm(v, xb3[:, j, :], r3[:, j, :], j)
                    if j < GB - 1:
                        fc.did(ins)
                ins.then_inc(r3_ready, 1)
                v.wait_ge(r3_ready, g + 1)
            assert fc.n == NFF, (fc.n, NFF)

        v.wait_ge(l_act, 5)
        sc = Chain(v, moe_v)
        sc.step(v.scalar_tensor_tensor(out=sty[:, 0, :], in0=sty[:, 2, :], scalar=0.0, in1=sty[:, 3, :],
                                       op0=ALU.max, op1=ALU.add))
        sc.step(v.tensor_scalar(sty[:, 0, :], sty[:, 0, :], 1e-8, None, ALU.add))
        NPRE = 70
        with v.Fori(0, NG) as g:
            pc = Chain(v, pre_v, g * NPRE)
            v.wait_ge(x4_ready, g + 1)
            norm_stats(pc, v, lambda j: x4[:, bass.ds(g * GB + j, 1), :].rearrange("p a d -> p (a d)"), 1e-5)
            for j in range(GB):
                ins = apply_norm(v, xs[0][:, j, :], x4[:, bass.ds(g * GB + j, 1), :].rearrange("p a d -> p (a d)"), j)
                if j < GB - 1:
                    pc.did(ins)
            ins.then_inc(e_xs, 1)
            v.wait_ge(e_xs, g + 1)
            v.wait_ge(e_hl, g + 1)
            norm_stats(pc, v, lambda j: hl[:, j, :], 1e-8)
            sl = bass.ts(g, GB)
            pc.step(v.tensor_tensor(rs[:, 3, :], rs[:, 3, :], sty[:, 0, sl], ALU.mult))
            pc.step(v.tensor_tensor(rs[:, 1, :], mv[:, :, 0], rs[:, 3, :], ALU.mult))
            pc.step(v.tensor_tensor(rs[:, 2, :], sty[:, 1, sl], rs[:, 1, :], ALU.subtract))
            v.wait_ge(e_hcols, g)
            for j in range(GB):
                ins = v.tensor_scalar(hfs[:, j, :], hl[:, j, :], rs[:, 3, j:j + 1], rs[:, 2, j:j + 1], ALU.mult, ALU.add)
                if j < GB - 1:
                    pc.did(ins)
            ins.then_inc(e_hfs, 1)
            wait_apart(v, e_logit, g + 1, small_loaded, N_SMALL)
            for j in range(GB):
                pc.did(v.max(top[:, j, :], ps[:, 1, j * E3:(j + 1) * E3]))
            pc.join_apart(small_loaded, N_SMALL)
            for j in range(GB):
                ins = v.max_index(topi[:, j, :], top[:, j, :], ps[:, 1, j * E3:(j + 1) * E3])
                if j < GB - 1:
                    pc.did(ins)
                else:
                    pc.step(ins)
            pc.did(v.tensor_copy(topf[:, :, :], topi[:, :, :]))
            v.tensor_tensor(gate[:, 0, :], top[:, :, 1], top[:, :, 0], ALU.subtract).then_inc(e_top, 1)
            v.wait_ge(e_gate, g + 1)
            pc.step(v.tensor_scalar(gate[:, 2, :], gate[:, 1, :], 1.0, None, ALU.add))
            pc.step(v.reciprocal(gate[:, 2, :], gate[:, 2, :]))
            pc.step(v.tensor_tensor(gate[:, 3, :], gate[:, 1, :], gate[:, 2, :], ALU.mult))
            for j in range(GB):
                pc.did(v.tensor_scalar(combs[:, j, :], iota8[:, :], topf[:, j, 0:1], gate[:, 2, j:j + 1],
                                       ALU.is_equal, ALU.mult))
                pc.did(v.tensor_scalar(comb2[:, j, :], iota8[:, :], topf[:, j, 1:2], gate[:, 3, j:j + 1],
                                       ALU.is_equal, ALU.mult))
            pc.join()
            v.tensor_tensor(combs[:, :, :], combs[:, :, :], comb2[:, :, :], ALU.add).then_inc(e_comb, 1)
            v.wait_ge(e_comb, g + 1)
            pc.did(v.tensor_copy(comb[:, bass.ts(g, GB), :], combs[:, :, :]))
            v.wait_ge(e_b2, g + 1)
            v.tensor_tensor(x4[:, bass.ts(g, GB), :], bank4(3), x4[:, bass.ts(g, GB), :], ALU.add).then_inc(e_acc, 1)
            pc.join()
            assert pc.n == NPRE, (pc.n, NPRE)

        v.wait_ge(e_acc, NG)
        with v.Fori(0, NG) as g:
            for e in range(E3):
                n = g * E3 + e
                v.wait_ge(m_w2, n + 1)
                v.wait_ge(m_acc, GB * n)
                for j in range(GB):
                    b = g * GB + j
                    row = x4[:, bass.ds(b, 1), :].rearrange("p a d -> p (a d)")
                    v.scalar_tensor_tensor(out=row, in0=bank4(4 + e % 2)[:, j, :],
                                           scalar=comb[:, bass.ds(b, 1), e], in1=row,
                                           op0=ALU.mult, op1=ALU.add).then_inc(m_acc, 1)

    @block.gpsimd
    def _(pool):
        ms = Chain(pool, memsets)
        ms.step(pool.memset(l0_area[32:33, 4096:6144], 1.0))
        ms.step(pool.memset(stack_area[:, :].bitcast(U32), 0))
        pool.wait_ge(small_loaded, N_SMALL)
        ms.step(pool.tensor_copy(identb[:, :], ident[:, :]))
        ms.step(pool.tensor_scalar(maskedb[:, :], ident[:, :], MASKED, None, ALU.mult))
        ms.step(pool.tensor_copy(msel[:, :], hsel))
        ms.step(pool.memset(mp[:, :], 0.0))
        for p in range(2):
            ms.step(pool.memset(vaug[p][:, :, :], 0.0))
            ms.step(pool.memset(vaug[p][:, :, DH:DH + 1], 1.0))
        po = Chain(pool, pool_own)
        for g in range(2 * NG):
            if g < NG:
                pool.wait_ge(xa_ready, g + 1)
                sl = slice(g * GB, (g + 1) * GB)
                po.step(pool.tensor_tensor(x1[:, sl, :], xn1[:, sl, :], rows[:, 0:1, :].to_broadcast([S, GB, D]), ALU.mult))
                pool.tensor_tensor(x1[:, sl, :], x1[:, sl, :], rows[:, 1:2, :].to_broadcast([S, GB, D]),
                                   ALU.add).then_inc(x1_ready, 1)
                pool.wait_ge(x1_ready, g + 1)
            else:
                for which in range(2):
                    k = 2 * (g - NG) + which
                    pool.wait_ge(piece1, k + 1)
                    pool.tensor_tensor(qkf[which][:, :], qkf[which][:, :], pieces[which][:, 0, :],
                                       ALU.subtract).then_inc(rest1, 1)
                    pool.wait_ge(rest1, k + 1)
                    pool.wait_ge(piece2, k + 1)
                    pool.tensor_tensor(pieces[which][:, 2, :], qkf[which][:, :], pieces[which][:, 1, :],
                                       ALU.subtract).then_inc(piece3, 1)
                    pool.wait_ge(piece3, k + 1)
        pool.wait_ge(memsets, 10)
        pool.wait_ge(vy_read, NG)

        def prepare(t, j, early):
            if not early:
                pool.wait_ge(pv_done, NQ * (t - 1))
                pool.wait_ge(scores_ready, NQ * (t - 1))
            pool.tensor_copy(mneg[j % 2][:, :], mask[:, bass.ds(t, 1), :].rearrange("p a k -> p (a k)")
                             ).then_inc(mneg_ready, 1)
            pool.wait_ge(mneg_ready, t + 1)
            pool.tensor_copy(vaug[j % 2][:, :, 0:DH],
                             v_rows[:, bass.ds(t, 1), :].rearrange("p a (h r) -> p (a h) r", h=H)).then_inc(vaug_ready, 1)
            pool.wait_ge(vaug_ready, t + 1)

        for j in range(GB):
            prepare(j, j, j < 2)
        with pool.Fori(1, NG) as g:
            for j in range(GB):
                prepare(g * GB + j, j, False)
        with pool.Fori(0, NG // 2) as it:
            for p in range(2):
                g = 2 * it + p
                pool.wait_ge(xs_ready, g + 1)
                pool.tensor_tensor(x2[:, bass.ts(g, GB), :], x2[:, bass.ts(g, GB), :],
                                   rows[:, 4:5, :].to_broadcast([S, GB, D]), ALU.add).then_inc(x2b_ready, 1)
                pool.wait_ge(x2b_ready, g + 1)
            for p in range(2):
                g = 2 * it + p
                pool.wait_ge(r3_ready, g + 1)
                l2c = Chain(pool, pool_l2, g * (2 * GB - 1))
                for j in range(GB):
                    b = g * GB + j
                    l2c.step(pool.tensor_tensor(xb3[:, j, :], xb3[:, j, :], rows2[j][:, 1, :], ALU.mult))
                    ins = pool.tensor_tensor(x4[:, bass.ds(b, 1), :].rearrange("p a d -> p (a d)"), xb3[:, j, :],
                                             rows2[j][:, 2, :], ALU.add)
                    if j < GB - 1:
                        l2c.step(ins)
                ins.then_inc(x4_ready, 1)
                pool.wait_ge(x4_ready, g + 1)
        with pool.Fori(0, NG) as g:
            pool.wait_ge(e_hfs, g + 1)
            pool.tensor_copy(hcols[:, bass.ts(g, GT)].rearrange("p (b s) -> p b s", b=GB), hfs).then_inc(e_hcols, 1)
            pool.wait_ge(e_hcols, g + 1)


CONSTS = ["c_ident", "c_cols", "c_iota8", "c_eye_row"]
OUT_SHAPE = (B, S, D)


def kernel(**inputs):
    import concourse.bacc as bacc
    from concourse.bass_utils import run_bass_kernel_spmd

    def arr(name):
        return np.asarray(inputs[name])

    def column(v):
        n = v.shape[0]
        if n > 128:
            return v.reshape(-1, 128).T
        c = np.zeros((128, 1), v.dtype)
        c[:n, 0] = v
        return c

    l0, l1, l2, l3 = "L0_cond_", "L1_cond_", "L2_cond_", "L3_cond_"
    half = D // 2
    freq = np.exp(np.arange(half, dtype=np.float32) * np.float32(-np.log(10000.0) / (half - 1))).astype(np.float32)
    cc = np.zeros((128, 32), np.float32)
    cc[:, 0] = np.arange(128)
    cc[:, 1] = np.concatenate([freq, freq])
    cc[half:, 2] = np.float32(np.pi / 2)
    cc[half:, 3] = 0.25
    for p in range(3):
        cc[p * H:(p + 1) * H, 8:8 + H] = np.eye(H)

    data = {
        "x": arr("x"),
        "attn_bias": arr("fside_Bx16xSxS_0").transpose(0, 2, 1, 3),
        "mask": np.ascontiguousarray(arr("mask_Bx1xSxS_bk0")[:, 0].transpose(1, 0, 2)),
        "expert_W": arr(l0 + "expert_W").reshape(E0, A0 * A0),
        "expert_b": arr(l0 + "expert_b"), "domain_emb": arr(l0 + "domain_emb"),
        "down_WT": arr(l0 + "down_W").T,
        "up_WTb": np.concatenate([arr(l0 + "up_W").T, arr(l0 + "up_b")[None]], 0),
        "W_ada": arr(l1 + "W_ada"), "Wq": arr(l1 + "Wq"), "Wk": arr(l1 + "Wk"), "Wv": arr(l1 + "Wv"),
        "Wo": arr(l1 + "Wo"), "W1": arr(l1 + "W1"),
        "W2": arr(l1 + "W2").reshape(FC, 128, D).transpose(1, 0, 2),
        "subj_emb": arr(l3 + "subj_emb"), "bi": arr(l2 + "bi"),
        "hyp_w1": arr(l3 + "hyp_w1"), "hyp_w2": arr(l3 + "hyp_w2"), "sty_w1": arr(l3 + "sty_w1"),
        "sty_w2": arr(l3 + "sty_w2"), "router_w": arr(l3 + "router_w"), "exp_b2": arr(l3 + "exp_b2"),
        "exp_b1T": arr(l3 + "exp_b1").reshape(E3 * FC, 128).T,
        "exp_w1": arr(l3 + "exp_w1"),
        "exp_w2": arr(l3 + "exp_w2").reshape(E3, FC, 128, D).transpose(2, 0, 1, 3),
        "l2_w": np.concatenate([arr(l2 + "Wi"), arr(l2 + "Wo").reshape(E2, FC, 128, D).transpose(0, 2, 1, 3)
                                .reshape(E2, 128, FC * D)], 2),
        "l2_rows": np.stack([arr(l2 + "bo"), arr(l2 + "gamma"), arr(l2 + "beta")], 1),
        "rows": np.stack([arr(l0 + "ln_gamma"), arr(l0 + "ln_beta"), arr(l1 + "bv"), arr(l1 + "bo"), arr(l1 + "b2")], 0),
        "cols": np.concatenate([column(c) for c in (
            arr(l0 + "down_b"), arr(l1 + "b_ada")[:D], arr(l1 + "b_ada")[D:], arr(l1 + "bq"), arr(l1 + "bk"),
            arr(l1 + "g2"), arr(l1 + "beta2"), arr(l3 + "ln_g"), arr(l3 + "ln_b"), arr(l3 + "hyp_b1"),
            arr(l3 + "hyp_b2"), arr(l3 + "sty_b1"), arr(l3 + "sty_b2")[:D], arr(l3 + "sty_b2")[D:], arr(l1 + "b1"))], 1),
        "c_ident": np.eye(128, dtype=np.float32), "c_cols": cc,
        "c_iota8": np.arange(8, dtype=np.float32), "c_eye_row": np.eye(A0, dtype=np.float32).reshape(1, -1),
    }
    for name in ("itok_B_0_15", "itok_B_34_63", "itok_B_0_7", "itok_B_6_14"):
        data[name] = arr(name)

    nc = bacc.Bacc("TRN2", target_bir_lowering=False, num_devices=1)
    arrays, aps = {}, {}
    for name, a in data.items():
        a = np.ascontiguousarray(a)
        arrays[f"in_{name}"] = a
        aps[name] = nc.dram_tensor(f"in_{name}", a.shape, mybir.dt.from_np(a.dtype), kind="ExternalInput").ap()
    out = nc.dram_tensor("out_0", OUT_SHAPE, F32, kind="ExternalOutput").ap()
    program(nc, aps, out)
    return run_bass_kernel_spmd(nc, [arrays], core_ids=[0]).results[0]["out_0"]
```

```python
from contextlib import ExitStack

import numpy as np

import concourse.bass as bass
from concourse import mybir

F32, BF16 = mybir.dt.float32, mybir.dt.bfloat16
I32, U32, U8 = mybir.dt.int32, mybir.dt.uint32, mybir.dt.uint8
ALU = mybir.AluOpType
ACT = mybir.ActivationFunctionType
AX = mybir.AxisListType.X

B, S, D = 16, 128, 128
GB = 4
NG, GT = B // GB, GB * S
A0, E0 = 32, 16
H, DH = 16, 8
HQ = 4
NQ = H // HQ
FF, FC = 512, 4
E2, E3 = 8, 8
SUB, SE = 32, 64
CW = 32
MASKED = -1.0e30
Q_PIECES = (0, 0, 1, 1, 0, 2)
K_PIECES = (0, 1, 0, 1, 2, 0)
TWO_PI_PARTS = (6.28125, 0.0019340515136718750, 1.2556659146e-06)
ROUNDER = 12582912.0


SETUP_ID2 = 11
SETUP_ONEHOT = 14
SETUP_ANGLE = 22
SETUP_WSEL = 24
SETUP_ADA = 29


def wait_apart(eng, sem, value, met, met_value):
    value = value if isinstance(value, int) else eng.to_reg(value)
    eng.wait_ge(met, met_value)
    eng.wait_ge(sem, value)


def after_start(eng, sem, value):
    if not (isinstance(value, int) and value <= 0):
        eng.wait_ge(sem, value)


class Chain:

    def __init__(self, eng, sem, base=0):
        self.eng, self.sem, self.base, self.n = eng, sem, base, 0

    def did(self, ins):
        ins.then_inc(self.sem, 1)
        self.n += 1

    def join(self):
        self.eng.wait_ge(self.sem, self.base + self.n)

    def join_apart(self, met, met_value):
        wait_apart(self.eng, self.sem, self.base + self.n, met, met_value)

    def step(self, ins):
        self.did(ins)
        self.join()


def program(nc, t, out):
    ctx = ExitStack()
    with ctx:
        build(nc, ctx, t, out)


def build(nc, ctx, dram, out):
    def sb(name, shape, dt=F32):
        return ctx.enter_context(nc.sbuf_tensor(name, shape, dt))

    def sem(name):
        return ctx.enter_context(nc.semaphore(name))

    x_in = sb("x_in", [S, B, D])
    x2 = x_in
    l0_area = sb("l0_area", [128, 8192])
    xT = l0_area[:, 0:2048]
    hT = l0_area[0:A0, 2048:4096]
    eT = l0_area[0:A0 + 1, 4096:6144]
    x1 = l0_area[:, 6144:8192].rearrange("p (b d) -> p b d", b=B)
    w1e = l0_area[:, 0:4096].rearrange("p (e f) -> p e f", e=E3)
    w2e = l0_area[:, 4096:8192].rearrange("p (e c d) -> p e c d", e=E3, c=FC)
    xn1 = sb("xn1", [S, B, D])
    x4 = xn1
    v_rows = sb("v_rows", [S, B, D])
    hcols = v_rows[:, :, :].rearrange("p b d -> p (b d)")
    y_rows = sb("y_rows", [S, B, D])
    biasx = sb("biasx", [S, GB, H, S])
    stack_area = sb("stack_area", [128, 2 * 2 * H * GT], BF16)
    qst = stack_area[:, 0:2 * H * GT].rearrange("p (r h t) -> p r h t", r=2, h=H)
    kst = stack_area[:, 2 * H * GT:].rearrange("p (r h t) -> p r h t", r=2, h=H)
    ff_area = stack_area[:, :].bitcast(F32)
    ffT = [ff_area[:, 2048 * p:2048 * p + 2048].rearrange("p (c t) -> p c t", c=FC) for p in range(2)]
    ff1T = ff_area[:, 4096:6144].rearrange("p (c t) -> p c t", c=FC)
    h2T = [ff_area[:, 6144 + 512 * p:6656 + 512 * p].rearrange("p (c t) -> p c t", c=FC) for p in range(2)]
    xs1, (hf, x3T, x3, r3, xs3, hl, hfs) = ff_area[:, 7168:9216].rearrange("p (b d) -> p b d", b=B), (
        ff_area[:, a:a + 512].rearrange("p (b d) -> p b d", b=GB) for a in range(9216, 12800, 512))
    combT = ff_area[0:E3, 12800:13312]
    xs_slot = ff_area[:, 13312:13824].rearrange("p (b d) -> p b d", b=GB)
    w2slot = [biasx[:, j, 0:8, :].rearrange("p a b -> p (a b)") for j in range(GB)]
    rows2 = biasx[:, :, 8:11, :]
    early = y_rows[:, :, :].rearrange("p b d -> p (b d)")
    bi_sb = early[0:E2, 0:512]
    w_h1 = early[0:SE, 512:640]
    w_h2 = early[:, 640:768]
    w_s1 = early[:, 768:832]
    w_s2 = early[0:64, 832:1088]
    sel_small = early[0:SUB, 1088:1216]
    w_down = early[:, 1216:1248]
    w_up = early[0:A0 + 1, 1248:1376]
    w_ada = early[:, 1376:1632]
    p_area = sb("p_area", [128, 1024])
    pT = [p_area[:, 512 * p:512 * p + 512].rearrange("p (h q) -> p h q", h=HQ) for p in range(2)]
    ew0 = p_area[0:E0 + 1, :]
    wsel = sb("wsel", [A0, B, A0])
    yT = [sb(f"yT{p}", [D, GB, S]) for p in range(2)]
    qkf = [sb(f"qkf{p}", [D, GT]) for p in range(2)]
    pieces = [sb(f"pieces{p}", [D, 3, GT], BF16) for p in range(2)]
    vaug = [sb(f"vaug{p}", [S, H, CW]) for p in range(2)]
    mneg = [sb(f"mneg{p}", [S, S], BF16) for p in range(2)]
    mask = sb("mask", [S, B, S], U8)
    msel = sb("msel", [128, H], BF16)
    mx = sb("mx", [S, 2, H])
    mres = sb("mres", [S, H])
    mp = sb("mp", [S, 128], BF16)
    mT = sb("mT", [128, S], BF16)
    ctxs = sb("ctxs", [128, NQ, S])
    ctxn = sb("ctxn", [S, D])
    ctx2T = sb("ctx2T", [D, S])
    den = sb("den", [S, H])
    rden = sb("rden", [S, H])
    nanfix = sb("nanfix", [S, B])
    ident = sb("ident", [128, 128])
    identb = sb("identb", [128, 128], BF16)
    maskedb = sb("maskedb", [128, 128], BF16)
    cst = sb("cst", [128, 32])
    ids = sb("ids", [128, 4, B], I32)
    idf = sb("idf", [128, 8, B])
    oh = sb("oh", [128, 5, B])
    id2 = sb("id2", [1, B], I32)
    cols = sb("cols", [128, 64])
    rows = sb("rows", [128, 5, D])
    tmp = sb("tmp", [128, 8, B])
    ada = sb("ada", [D, 2, B])
    domb = sb("domb", [A0, B])
    bi2 = sb("bi2", [128, FC, B])
    sty = sb("sty", [D, 4, B])
    hyp = sb("hyp", [128, 4, B])
    w_q = sb("w_q", [D, D])
    w_k = sb("w_k", [D, D])
    w_vi = sb("w_vi", [D, 2 * D])
    w_o = sb("w_o", [D, D])
    w_1 = sb("w_1", [D, FF])
    w_2 = sb("w_2", [128, FC, D])
    w_r = sb("w_r", [D, E3])
    be2 = sb("be2", [E3, D])
    b1e = sb("b1e", [128, E3 * FC])
    st = sb("st", [128, B, 6])
    mv = sb("mv", [128, B, 2])
    rs = sb("rs", [128, 4, B])
    top = sb("top", [S, GB, 8])
    topi = sb("topi", [S, GB, 8], U32)
    topf = sb("topf", [S, GB, 8])
    gate = sb("gate", [S, 4, GB])
    comb = sb("comb", [S, B, E3])
    comb2 = sb("comb2", [S, GB, E3])
    combs = sb("combs", [S, GB, E3])
    iota8 = sb("iota8", [128, 8])
    ps = ctx.enter_context(nc.psum_tensor("ps", [128, 8, 512], F32))
    scr = nc.dram_tensor("qk_pieces", [2, 3, 128, B * S], BF16).ap()

    def bank4(n):
        return ps[:, n, :].rearrange("p (a b) -> p a b", a=4)

    IOTA, FREQ, PHASE, TURN = (cst[:, i:i + 1] for i in range(4))
    hsel = cst[:, 8:24]
    (C_DOWN, C_ADA0, C_ADA1, C_BQ, C_BK, C_G2, C_BETA2, C_LNG, C_LNB, C_HB1, C_HB2, C_SB1, C_SG, C_SB,
     C_B1) = range(15)

    def flat(x):
        return x.rearrange("p b d -> p (b d)")

    def col(i, n=128):
        return cols[0:n, i:i + 1]

    x_loaded = [sem(f"x_loaded{g}") for g in range(NG)]
    small_loaded = sem("small_loaded")
    bias_loaded = [sem(f"bias_loaded{j}") for j in range(GB)]
    memsets = sem("memsets")
    setup_v = sem("setup_v")
    setup_pe = sem("setup_pe")
    setup_a = sem("setup_a")
    xT_psum, xT_ready = sem("xT_psum"), sem("xT_ready")
    down_psum, gelu_ready = sem("down_psum"), sem("gelu_ready")
    exp_psum, eT_ready = sem("exp_psum"), sem("eT_ready")
    up_psum, up_read = sem("up_psum"), sem("up_read")
    xa_ready, x1_ready, pool_own = sem("xa_ready"), sem("x1_ready"), sem("pool_own")
    xn1_ready, yT_psum, yT_ready = sem("xn1_ready"), sem("yT_psum"), sem("yT_ready")
    qk_psum, qkf_ready, vy_psum, vy_read = sem("qk_psum"), sem("qkf_ready"), sem("vy_psum"), sem("vy_read")
    piece1, rest1, piece2, piece3 = sem("piece1"), sem("rest1"), sem("piece2"), sem("piece3")
    pieces_out = [sem(f"pieces_out{p}") for p in range(2)]
    stack_in = sem("stack_in")
    vaug_ready, mneg_ready = sem("vaug_ready"), sem("mneg_ready")
    scores_ready, scores_read = sem("scores_ready"), sem("scores_read")
    mp_ready, mT_psum, mT_ready = sem("mp_ready"), sem("mT_psum"), sem("mT_ready")
    xt_ready, exp_ready = sem("xt_ready"), sem("exp_ready")
    pv_done, ctxs_ready, ctxn_psum, ctxn_ready = (sem("pv_done"), sem("ctxs_ready"), sem("ctxn_psum"),
                                                  sem("ctxn_ready"))
    ctx2_psum, ctx2_ready, wo_psum, x2_ready = sem("ctx2_psum"), sem("ctx2_ready"), sem("wo_psum"), sem("x2_ready")
    l_act, den_v = sem("l_act"), sem("den_v")
    att_v, l0_v, ffn_v, side_v = sem("att_v"), sem("l0_v"), sem("ffn_v"), sem("side_v")
    w2_loaded = [sem(f"w2_loaded{j}") for j in range(GB)]
    rows2_loaded = sem("rows2_loaded")
    experts_loaded, xs_staged = sem("experts_loaded"), sem("xs_staged")
    xs_ready, xs_psum, hf_ready = sem("xs_ready"), sem("xs_psum"), sem("hf_ready")
    w1_psum, ff_ready, w2_psum, x3_ready, x2b_ready = (sem("w1_psum"), sem("ff_ready"), sem("w2_psum"),
                                                       sem("x3_ready"), sem("x2b_ready"))
    x3T_psum, x3T_ready = sem("x3T_psum"), sem("x3T_ready")
    wi_psum, h2_ready, wo2_psum = sem("wi_psum"), sem("h2_ready"), sem("wo2_psum")
    r3_sum, x4_ready = sem("r3_sum"), sem("x4_ready")
    e_xs, e_psum, e_hl, e_hfs, e_hcols = (sem(n) for n in ("e_xs", "e_psum", "e_hl", "e_hfs", "e_hcols"))
    e_logit, e_top, e_gate, e_comb, e_combT, e_cT, e_b2, e_acc = (
        sem(n) for n in ("e_logit", "e_top", "e_gate", "e_comb", "e_combT", "e_cT", "e_b2", "e_acc"))
    m_w1, m_hid, m_w2, m_acc = (sem(n) for n in ("m_w1", "m_hid", "m_w2", "m_acc"))
    stored = sem("stored")

    block = ctx.enter_context(nc.Block())

    small = [
        (ident[:, :], dram["c_ident"]), (cst[:, :], dram["c_cols"]), (iota8[:, :], dram["c_iota8"].partition_broadcast(128)),
        (ids[:, 0, :], dram["itok_B_0_15"].partition_broadcast(128)),
        (ids[:, 1, :], dram["itok_B_34_63"].partition_broadcast(128)),
        (ids[:, 2, :], dram["itok_B_0_7"].partition_broadcast(128)),
        (ids[:, 3, :], dram["itok_B_6_14"].partition_broadcast(128)),
        (ew0[0:E0, :], dram["expert_W"]), (ew0[E0:E0 + 1, :], dram["c_eye_row"]),
        (sel_small[0:E0, 64:96], dram["expert_b"]), (sel_small[0:E0, 96:128], dram["domain_emb"]),
        (w_down[:, :], dram["down_WT"]), (w_up[:, :], dram["up_WTb"]),
        (cols[:, 0:C_B1 + FC], dram["cols"]), (w_ada[:, :], dram["W_ada"]),
        (rows[:, :, :], dram["rows"].partition_broadcast(128)),
        (w_q[:, :], dram["Wq"]), (w_k[:, :], dram["Wk"]), (w_vi[:, 0:D], dram["Wv"]), (w_vi[:, D:2 * D], dram["c_ident"]),
        (w_o[:, :], dram["Wo"]), (w_1[:, :], dram["W1"]), (w_2[:, :, :], dram["W2"]),
        (sel_small[0:SUB, 0:64], dram["subj_emb"]), (bi_sb[:, :], dram["bi"]),
        (w_h1[:, :], dram["hyp_w1"]), (w_h2[:, :], dram["hyp_w2"]), (w_s1[:, :], dram["sty_w1"]),
        (w_s2[:, :], dram["sty_w2"]), (w_r[:, :], dram["router_w"]), (be2[:, :], dram["exp_b2"]),
        (b1e[:, :], dram["exp_b1T"]), (mask[:, :, :], dram["mask"]),
    ]
    N_SMALL = 16 * len(small)

    @block.sync
    def _(sp):
        x_dram = dram["x"].rearrange("b s d -> s b d")

        def load_bias(b, j):
            sp.dma_start(biasx[:, j, :, :], dram["attn_bias"][b]).then_inc(bias_loaded[j], 16)

        for g in range(NG):
            sp.dma_start(x_in[:, g * GB:(g + 1) * GB, :], x_dram[:, g * GB:(g + 1) * GB, :]).then_inc(x_loaded[g], 16)
        for dst, src in small:
            sp.dma_start(dst, src).then_inc(small_loaded, 16)
        for j in range(GB):
            load_bias(j, j)

        def store_pieces(g, which):
            sp.wait_ge(piece3, 2 * g + which + 1)
            sp.dma_start(scr[which, :, :, g * GT:(g + 1) * GT].rearrange("p d t -> d p t"),
                         pieces[which][:, :, :]).then_inc(pieces_out[which], 16)

        def load_stack(g, par):
            for which, st_, pcs in ((0, qst, Q_PIECES), (1, kst, K_PIECES)):
                for c, p in enumerate(pcs):
                    sp.dma_start(st_[DH * c:DH * c + DH, par, :, :],
                                 scr[which, p, :, bass.ts(g, GT)].rearrange("(h r) t -> r h t", r=DH)
                                 ).then_inc(stack_in, 16)

        for g in range(NG):
            for which in range(2):
                store_pieces(g, which)
            if g == 0:
                sp.wait_ge(memsets, 2)
                sp.wait_ge(pieces_out[0], 16)
                sp.wait_ge(pieces_out[1], 16)
                load_stack(0, 0)
        sp.wait_ge(pieces_out[0], 16 * NG)
        sp.wait_ge(pieces_out[1], 16 * NG)

        def load_group(g):
            if not (isinstance(g, int) and g == 1):
                sp.wait_ge(scores_ready, (g - 1) * GB * NQ)
            sp.wait_ge(stack_in, g * 12 * 16)
            load_stack(g, g % 2)
            for j in range(GB):
                sp.wait_ge(xt_ready, ((g - 1) * GB + j + 1) * NQ)
                load_bias(g * GB + j, j)

        load_group(1)
        with sp.Fori(2, NG) as g:
            load_group(g)
        sp.wait_ge(xn1_ready, NG)
        sp.dma_start(w1e, dram["exp_w1"].rearrange("e d f -> d e f")).then_inc(experts_loaded, 16)
        sp.dma_start(w2e, dram["exp_w2"]).then_inc(experts_loaded, 16)

        def load_l2(b, j):
            e = sp.value_load(id2[0:1, bass.ds(b, 1)], min_val=0, max_val=E2 - 1)
            sp.dma_start(w2slot[j], dram["l2_w"][e]).then_inc(w2_loaded[j], 16)

        def load_rows2(b, j):
            e = sp.value_load(id2[0:1, bass.ds(b, 1)], min_val=0, max_val=E2 - 1)
            sp.dma_start(rows2[:, j, :, :], dram["l2_rows"][e].partition_broadcast(128)).then_inc(rows2_loaded, 16)

        sp.wait_ge(setup_v, SETUP_ID2)
        for j in range(GB):
            sp.wait_ge(xt_ready, (B - GB + j + 1) * NQ)
            load_l2(j, j)
            load_rows2(j, j)

        def refill(g):
            for j in range(GB):
                wait_apart(sp, wo2_psum, (g - 1) * GB + j + 1, setup_v, SETUP_ID2)
                load_l2(g * GB + j, j)
            wait_apart(sp, x4_ready, g, setup_v, SETUP_ID2)
            for j in range(GB):
                load_rows2(g * GB + j, j)

        out_rows = out.rearrange("b s d -> s b d")

        def store(g):
            sp.wait_ge(m_acc, (g + 1) * E3 * GB)
            sp.dma_start(out_rows[:, bass.ts(g, GB), :], x4[:, bass.ts(g, GB), :]).then_inc(stored, 16)

        refill(1)
        with sp.Fori(2, NG) as g:
            refill(g)
            store(g - 2)
        store(NG - 2)
        store(NG - 1)
        sp.wait_ge(stored, 16 * NG)

    @block.tensor
    def _(pe):
        def mm(o, l, r, start=True, stop=True, **kw):
            return pe.matmul(o, l, r, start=start, stop=stop, **kw)

        pe.wait_ge(small_loaded, N_SMALL)
        pe.wait_ge(setup_v, SETUP_ONEHOT)
        for o in range(A0):
            ins = mm(ps[0:A0, 4, o * B:(o + 1) * B], ew0[:, o * A0:(o + 1) * A0], oh[0:E0 + 1, 0, :])
        ins.then_inc(setup_pe, 1)
        mm(ps[0:A0, 5, 0:B], sel_small[0:E0, 64:96], oh[0:E0, 0, :], stop=False)
        mm(ps[0:A0, 5, 0:B], sel_small[0:E0, 96:128], oh[0:E0, 1, :], start=False).then_inc(setup_pe, 1)
        for c in range(FC):
            ins = mm(ps[:, 6, 32 + c * B:32 + (c + 1) * B], bi_sb[:, c * 128:(c + 1) * 128], oh[0:E2, 2, :])
        mm(ps[0:SE, 7, 0:B], sel_small[0:SUB, 0:64], oh[0:SUB, 3, :]).then_inc(setup_pe, 1)
        pe.wait_ge(setup_a, 1)
        for i in range(2):
            ins = mm(ps[:, 6, i * B:(i + 1) * B], w_ada[:, i * D:(i + 1) * D], tmp[:, 7, :])
        ins.then_inc(setup_pe, 1)

        for g in range(NG):
            pe.wait_ge(x_loaded[g], 16)
            if g >= 2:
                pe.wait_ge(xT_ready, g - 1)
            for j in range(GB):
                ins = pe.transpose(bank4(g % 2)[:, j, :], x_in[:, g * GB + j, :], ident[:, :])
            ins.then_inc(xT_psum, 1)
        pe.wait_ge(setup_a, 2)
        mm(ps[:, 7, 16:32], w_h1[:, :], hyp[0:SE, 0, :]).then_inc(setup_pe, 1)
        for g in range(NG):
            pe.wait_ge(xT_ready, g + 1)
            if g >= 2:
                pe.wait_ge(gelu_ready, g - 1)
            mm(ps[0:A0, 2 + g % 2, :], w_down[:, :], xT[:, g * GT:(g + 1) * GT]).then_inc(down_psum, 1)
        pe.wait_ge(setup_a, 3)
        mm(ps[:, 7, 32:48], w_h2[:, :], hyp[:, 1, :]).then_inc(setup_pe, 1)
        pe.wait_ge(setup_v, SETUP_WSEL)
        for g in range(NG):
            pe.wait_ge(gelu_ready, g + 1)
            if g >= 2:
                pe.wait_ge(eT_ready, g - 1)
            for j in range(GB):
                b = g * GB + j
                ins = mm(ps[0:A0, 4 + g % 2, j * S:(j + 1) * S], wsel[:, b, :], hT[:, b * S:(b + 1) * S])
            ins.then_inc(exp_psum, 1)
        pe.wait_ge(setup_a, 4)
        mm(ps[0:64, 7, 48:64], w_s1[:, :], hyp[:, 2, :]).then_inc(setup_pe, 1)
        pe.wait_ge(setup_a, 5)
        mm(ps[:, 7, 64:80], w_s2[:, 0:128], hyp[0:64, 3, :])
        mm(ps[:, 7, 80:96], w_s2[:, 128:256], hyp[0:64, 3, :]).then_inc(setup_pe, 1)
        pe.wait_ge(setup_a, 6)
        pe.wait_ge(memsets, 1)
        pe.wait_ge(setup_v, SETUP_ADA)
        for g in range(NG):
            pe.wait_ge(eT_ready, g + 1)
            if g >= 2:
                pe.wait_ge(up_read, g - 1)
            for j in range(GB):
                b = g * GB + j
                ins = mm(bank4(6 + g % 2)[:, j, :], eT[:, b * S:(b + 1) * S], w_up[:, :])
            ins.then_inc(up_psum, 1)

        for g in range(NG):
            pe.wait_ge(xn1_ready, g + 1)
            if g >= 2:
                pe.wait_ge(yT_ready, g - 1)
            for j in range(GB):
                ins = pe.transpose(bank4(g % 2)[:, j, :], xn1[:, g * GB + j, :], ident[:, :])
            ins.then_inc(yT_psum, 1)
            pe.wait_ge(yT_ready, g + 1)
            y = yT[g % 2][:, :, :].rearrange("p b s -> p (b s)")
            for which, w in ((0, w_q), (1, w_k)):
                if g >= 1:
                    pe.wait_ge(qkf_ready, 2 * g - 1 + which)
                mm(ps[:, 2 + which, :], w[:, :], y).then_inc(qk_psum, 1)
            if g == 0:
                pe.wait_ge(up_read, NG)
            if g >= 2:
                pe.wait_ge(vy_read, g - 1)
            for j in range(GB):
                bank = 4 + 2 * (g % 2) + j // 2
                ins = mm(ps[:, bank, (j % 2) * 256:(j % 2) * 256 + 256], yT[g % 2][:, j, :], w_vi[:, :])
            ins.then_inc(vy_psum, 1)

        def scores(tn, gn, jn, q):
            if q == 0:
                pe.wait_ge(mneg_ready, tn + 1)
                if jn == 0:
                    pe.wait_ge(stack_in, (gn + 1) * 12 * 16)
            if not (isinstance(tn, int) and 4 * tn + q < 2):
                pe.wait_ge(scores_read, NQ * tn + q - 1)
            par = gn % 2
            for i in range(HQ):
                h = q * HQ + i
                mm(bank4(q % 2)[:, i, :], qst[:, par, h, jn * S:(jn + 1) * S],
                         kst[:, par, h, jn * S:(jn + 1) * S], start=(i == 0), stop=False,
                         skip_group_check=True)
            mm(bank4(q % 2), maskedb[:, :], mneg[jn % 2][:, :].unsqueeze(1).to_broadcast([128, HQ, S]),
               start=False, skip_group_check=True).then_inc(scores_ready, 1)

        def turn(t, j, q):
            if not (isinstance(t, int) and 4 * t + q < 2):
                pe.wait_ge(exp_ready, NQ * t + q - 1)
            for i in range(HQ):
                pe.matmul(bank4(2 + q % 2)[:, i, :], biasx[:, j, q * HQ + i, :], ident[:, :], start=(i == 0),
                          stop=False, is_transpose=True, skip_group_check=True)
            for i in range(HQ):
                ins = mm(bank4(2 + q % 2)[:, i, :], msel[:, q * HQ + i:q * HQ + i + 1].to_broadcast([128, S]), mT[:, :], start=False,
                         stop=True, skip_group_check=True)
            ins.then_inc(xt_ready, 1)

        def values(t, j, q):
            pe.wait_ge(exp_ready, NQ * t + q + 1)
            if q == 0:
                pe.wait_ge(vaug_ready, t + 1)
                if not (isinstance(t, int) and t == 0):
                    pe.wait_ge(ctxs_ready, t)
            for i in range(HQ):
                ins = mm(ps[CW * i:CW * i + CW, 4, q * S:(q + 1) * S], vaug[j % 2][:, q * HQ + i, :],
                         pT[q % 2][:, i, :], tile_position=(0, CW * i))
            ins.then_inc(pv_done, 1)

        def project_a(t):
            pe.wait_ge(ctxs_ready, t + 1)
            if not (isinstance(t, int) and t == 0):
                pe.wait_ge(ctxn_ready, t)
            for q in range(NQ):
                ins = pe.transpose(bank4(6)[:, q, :], ctxs[:, q, :], ident[:, :])
            ins.then_inc(ctxn_psum, 1)

        def project_b(t):
            pe.wait_ge(ctxn_ready, t + 1)
            if not (isinstance(t, int) and t == 0):
                pe.wait_ge(x2_ready, t)
            pe.transpose(ps[:, 7, 0:128], ctxn[:, :], ident[:, :]).then_inc(ctx2_psum, 1)

        def project_c(t):
            pe.wait_ge(ctx2_ready, t + 1)
            mm(ps[:, 7, 128:256], ctx2T[:, :], w_o[:, :]).then_inc(wo_psum, 1)

        def attend(t, g, j, first, last):
            nxt = (t + 1, g if j < GB - 1 else g + 1, (j + 1) % GB)
            if not last:
                scores(*nxt, 0)
                scores(*nxt, 1)
            pe.wait_ge(mp_ready, t + 1)
            if not first:
                pe.wait_ge(mT_ready, t)
            pe.transpose(ps[:, 5, 0:64].bitcast(BF16), mp[:, :], identb[:, :]).then_inc(mT_psum, 1)
            if not first:
                project_a(t - 1)
            pe.wait_ge(mT_ready, t + 1)
            turn(t, j, 0)
            if not first:
                project_b(t - 1)
            turn(t, j, 1)
            if not last:
                scores(*nxt, 2)
            values(t, j, 0)
            if not first:
                project_c(t - 1)
            turn(t, j, 2)
            if not last:
                scores(*nxt, 3)
            values(t, j, 1)
            turn(t, j, 3)
            values(t, j, 2)
            values(t, j, 3)

        pe.wait_ge(memsets, 5)
        pe.wait_ge(yT_ready, NG)
        pe.wait_ge(qkf_ready, 2 * NG)
        pe.wait_ge(vy_read, NG)
        for q in range(NQ):
            scores(0, 0, 0, q)
        for j in range(GB):
            attend(j, 0, j, j == 0, False)
        with pe.Fori(1, NG - 1) as g:
            for j in range(GB):
                attend(g * GB + j, g, j, False, False)
        for j in range(GB):
            attend(B - GB + j, NG - 1, j, False, j == GB - 1)
        project_a(B - 1)
        project_b(B - 1)
        project_c(B - 1)

        pe.wait_ge(x2_ready, B)
        pe.wait_ge(exp_ready, NQ * B)

        def turn_x2(n):
            if isinstance(n, int):
                pe.wait_ge(xs_ready, n + 1)
            else:
                pe.wait_ge(xs_staged, n - 1)
            for j in range(GB):
                x = xs1[:, n * GB + j, :] if isinstance(n, int) else xs_slot[:, j, :]
                ins = pe.transpose(bank4(6)[:, j, :], x, ident[:, :])
            ins.then_inc(xs_psum, 1)

        def ff_hidden(n, chunks):
            pe.wait_ge(hf_ready, n + 1)
            for c in chunks:
                if c >= 2:
                    pe.wait_ge(ff_ready, FC * n + c - 1)
                mm(ps[:, 4 + c % 2, :], w_1[:, c * 128:(c + 1) * 128], flat(hf)).then_inc(w1_psum, 1)

        def ff_out(n):
            pe.wait_ge(ff_ready, FC * (n + 1))
            after_start(pe, e_acc, n)
            for j in range(GB):
                for c in range(FC):
                    ins = mm(bank4(7)[:, j, :], ff1T[:, c, j * S:(j + 1) * S], w_2[:, c, :],
                             start=(c == 0), stop=(c == FC - 1))
            ins.then_inc(w2_psum, 1)

        def turn_x3(n):
            pe.wait_ge(x3_ready, n + 1)
            for j in range(GB):
                ins = pe.transpose(bank4(6)[:, j, :], x3[:, j, :], ident[:, :])
            ins.then_inc(x3T_psum, 1)

        def l2_hidden(n, j):
            if j == 0:
                pe.wait_ge(x3T_ready, n + 1)
            pe.wait_ge(w2_loaded[j], 16 * (n + 1))
            if j >= 2:
                pe.wait_ge(h2_ready, GB * n + j - 1)
            for c in range(FC):
                ins = mm(bank4(4 + j % 2)[:, c, :], w2slot[j][:, c * 128:(c + 1) * 128], x3T[:, j, :])
            ins.then_inc(wi_psum, 1)

        def l2_out(n, j):
            pe.wait_ge(h2_ready, GB * n + j + 1)
            for c in range(FC):
                ins = mm(bank4(7)[:, j, :], h2T[j % 2][:, c, :], w2slot[j][:, 512 + c * 128:512 + (c + 1) * 128],
                         start=(c == 0), stop=(c == FC - 1))
            ins.then_inc(wo2_psum, 1)

        def turn_x4(n):
            pe.wait_ge(e_xs, n + 1)
            for j in range(GB):
                ins = pe.transpose(bank4(6)[:, j, :], xs3[:, j, :], ident[:, :])
            ins.then_inc(e_psum, 1)

        def router(n):
            pe.wait_ge(e_hfs, n + 1)
            for j in range(GB):
                ins = mm(ps[:, 7, j * E3:(j + 1) * E3], hfs[:, j, :], w_r[:, :])
            ins.then_inc(e_logit, 1)

        def turn_gates(n):
            pe.wait_ge(e_comb, n + 1)
            for j in range(GB):
                ins = pe.transpose(ps[0:E3, 6, j * S:(j + 1) * S], combs[:, j, :], ident[:, :])
            ins.then_inc(e_combT, 1)

        def gated_bias(n):
            pe.wait_ge(e_cT, n + 1)
            for j in range(GB):
                ins = mm(bank4(7)[:, j, :], combT[:, j * S:(j + 1) * S], be2[:, :])
            ins.then_inc(e_b2, 1)

        def hidden(m, e):
            if e == 0:
                pe.wait_ge(e_hcols, m + 1)
            for c in range(FC):
                after_start(pe, m_hid, FC * (m * E3 + e) + c - 1)
                mm(ps[:, c % 2, :], w1e[:, e, c * 128:(c + 1) * 128], hcols[:, bass.ts(m, GT)]).then_inc(m_w1, 1)

        def output(m, e):
            pe.wait_ge(m_hid, FC * (m * E3 + e + 1))
            after_start(pe, m_acc, GB * (m * E3 + e - 1))
            for j in range(GB):
                for c in range(FC):
                    ins = mm(bank4(2 + e % 2)[:, j, :], ffT[e % 2][:, c, j * S:(j + 1) * S], w2e[:, e, c, :],
                             start=(c == 0), stop=(c == FC - 1))
            ins.then_inc(m_w2, 1)

        def side_by_side(n, m):
            side = n is not None
            hidden(m, 0)
            router(m)
            if side:
                turn_x2(n)
                pe.wait_ge(hf_ready, n + 1)
            hidden(m, 1)
            turn_gates(m)
            if side:
                ff_hidden(n, (0, 1))
            output(m, 0)
            if side:
                ff_hidden(n, (2, 3))
            gated_bias(m)
            hidden(m, 2)
            if side:
                ff_out(n)
            output(m, 1)
            if side:
                turn_x3(n)
            hidden(m, 3)
            if side:
                l2_hidden(n, 0)
                l2_hidden(n, 1)
            output(m, 2)
            if side:
                l2_out(n, 0)
                l2_hidden(n, 2)
                l2_out(n, 1)
                l2_hidden(n, 3)
            hidden(m, 4)
            if side:
                l2_out(n, 2)
                l2_out(n, 3)
            output(m, 3)
            hidden(m, 5)
            output(m, 4)
            hidden(m, 6)
            output(m, 5)
            if side:
                turn_x4(n)
            hidden(m, 7)
            output(m, 6)
            output(m, 7)

        turn_x2(0)
        ff_hidden(0, range(FC))
        ff_out(0)
        turn_x3(0)
        l2_hidden(0, 0)
        for j in range(1, GB):
            l2_hidden(0, j)
            l2_out(0, j - 1)
        l2_out(0, GB - 1)
        turn_x4(0)
        pe.wait_ge(experts_loaded, 32)
        side_by_side(1, 0)
        with pe.Fori(2, NG) as n:
            side_by_side(n, n - 1)
        side_by_side(None, NG - 1)

    @block.scalar
    def _(act):
        def affine(o, i, scale, bias):
            return act.activation(o, i, ACT.Identity, scale=scale, bias=bias)

        act.wait_ge(setup_v, SETUP_ANGLE)
        act.activation(tmp[:, 6, :], tmp[:, 5, :], ACT.Sin).then_inc(l_act, 1)
        act.wait_ge(l_act, 1)
        act.activation(tmp[:, 7, :], tmp[:, 6, :], ACT.Silu).then_inc(setup_a, 1)
        act.preload_act_table(ACT.Gelu)
        act.wait_ge(setup_pe, 3)
        act.activation(hyp[0:SE, 0, :], ps[0:SE, 7, 0:B], ACT.Copy).then_inc(setup_a, 1)
        for g in range(NG):
            act.wait_ge(xT_psum, g + 1)
            act.activation(xT[:, g * GT:(g + 1) * GT], ps[:, g % 2, :], ACT.Copy).then_inc(xT_ready, 1)
        act.wait_ge(setup_pe, 5)
        act.activation(hyp[:, 1, :], ps[:, 7, 16:32], ACT.Relu, bias=col(C_HB1)).then_inc(setup_a, 1)
        for g in range(NG):
            act.wait_ge(down_psum, g + 1)
            act.activation(hT[:, g * GT:(g + 1) * GT], ps[0:A0, 2 + g % 2, :], ACT.Gelu,
                           bias=col(C_DOWN, A0)).then_inc(gelu_ready, 1)
        act.wait_ge(setup_pe, 6)
        affine(hyp[:, 2, :], ps[:, 7, 32:48], 1.0, col(C_HB2)).then_inc(setup_a, 1)
        act.wait_ge(setup_pe, 7)
        act.activation(hyp[0:64, 3, :], ps[0:64, 7, 48:64], ACT.Relu, bias=col(C_SB1, 64)).then_inc(setup_a, 1)
        act.wait_ge(setup_pe, 8)
        affine(sty[:, 2, :], ps[:, 7, 64:80], 1.0, col(C_SG)).then_inc(l_act, 1)
        affine(sty[:, 1, :], ps[:, 7, 80:96], 1.0, col(C_SB)).then_inc(setup_a, 1)

        act.wait_ge(setup_v, SETUP_ADA)
        act.preload_act_table(ACT.Exp)
        for g in range(NG):
            act.wait_ge(yT_psum, g + 1)
            if g >= 2:
                act.wait_ge(vy_psum, g - 1)
            for j in range(GB):
                b = g * GB + j
                ins = affine(yT[g % 2][:, j, :], bank4(g % 2)[:, j, :], ada[:, 0, b:b + 1], ada[:, 1, b:b + 1])
            ins.then_inc(yT_ready, 1)
            for which, cb, sc in ((0, C_BQ, DH ** -0.5), (1, C_BK, 1.0)):
                act.wait_ge(qk_psum, 2 * g + which + 1)
                if g >= 1:
                    act.wait_ge(piece3, 2 * g - 1 + which)
                affine(qkf[which][:, :], ps[:, 2 + which, :], sc, col(cb)).then_inc(qkf_ready, 1)

        def context_out(t):
            act.wait_ge(pv_done, NQ * (t + 1))
            if not (isinstance(t, int) and t == 0):
                act.wait_ge(ctxn_psum, t)
            act.activation(ctxs[:, :, :], bank4(4), ACT.Copy).then_inc(ctxs_ready, 1)

        def context_turned(t):
            act.wait_ge(ctx2_psum, t + 1)
            if not (isinstance(t, int) and t == 0):
                act.wait_ge(wo_psum, t)
            act.activation(ctx2T[:, :], ps[:, 7, 0:128], ACT.Copy).then_inc(ctx2_ready, 1)

        def exponent(t, q):
            act.wait_ge(xt_ready, NQ * t + q + 1)
            if not (isinstance(t, int) and 4 * t + q < 2):
                act.wait_ge(pv_done, NQ * t + q - 1)
            act.activation(pT[q % 2], bank4(2 + q % 2), ACT.Exp).then_inc(exp_ready, 1)

        def attend(t, first):
            if not first:
                context_out(t - 1)
            act.wait_ge(mT_psum, t + 1)
            if not first:
                act.wait_ge(xt_ready, NQ * t)
            act.activation(mT[:, :], ps[:, 5, 0:64].bitcast(BF16), ACT.Copy).then_inc(mT_ready, 1)
            exponent(t, 0)
            if not first:
                context_turned(t - 1)
            for q in range(1, NQ):
                exponent(t, q)

        for j in range(GB):
            attend(j, j == 0)
        with act.Fori(1, NG) as g:
            for j in range(GB):
                attend(g * GB + j, False)
        context_out(B - 1)
        context_turned(B - 1)

        act.wait_ge(l_act, 2)
        act.activation(sty[:, 3, :], sty[:, 2, :], ACT.Abs).then_inc(l_act, 1)
        act.wait_ge(l_act, 3)
        act.activation(sty[:, 3, :], sty[:, 3, :], ACT.Exp, scale=-1.0).then_inc(l_act, 1)
        act.wait_ge(l_act, 4)
        act.activation(sty[:, 3, :], sty[:, 3, :], ACT.Ln, bias=1.0).then_inc(l_act, 1)

        def x2_turned(n):
            act.wait_ge(xs_psum, n + 1)
            affine(hf, bank4(6), col(C_G2), col(C_BETA2)).then_inc(hf_ready, 1)

        def ff_hidden(n, chunks):
            for c in chunks:
                act.wait_ge(w1_psum, FC * n + c + 1)
                act.activation(ff1T[:, c, :], ps[:, 4 + c % 2, :], ACT.Gelu_apprx_sigmoid,
                               bias=col(C_B1 + c)).then_inc(ff_ready, 1)

        def x3_turned(n):
            act.wait_ge(x3T_psum, n + 1)
            act.activation(x3T, bank4(6), ACT.Copy).then_inc(x3T_ready, 1)

        def l2_hidden(n, j):
            act.wait_ge(wi_psum, GB * n + j + 1)
            if j >= 2:
                act.wait_ge(wo2_psum, GB * n + j - 1)
            for c in range(FC):
                ins = act.activation(h2T[j % 2][:, c, :], bank4(4 + j % 2)[:, c, :], ACT.Gelu,
                                     bias=bi2[:, c, bass.ds(n * GB + j, 1)])
            ins.then_inc(h2_ready, 1)

        def x4_turned(n):
            act.wait_ge(e_psum, n + 1)
            affine(hl, bank4(6), col(C_LNG), col(C_LNB)).then_inc(e_hl, 1)

        def gate_exp(n):
            act.wait_ge(e_top, n + 1)
            act.activation(gate[:, 1, :], gate[:, 0, :], ACT.Exp).then_inc(e_gate, 1)

        def gates_turned(n):
            act.wait_ge(e_combT, n + 1)
            act.activation(combT[:, :], ps[0:E3, 6, :], ACT.Copy).then_inc(e_cT, 1)

        def hidden(m, e):
            after_start(act, m_w2, m * E3 + e - 1)
            for c in range(FC):
                act.wait_ge(m_w1, FC * (m * E3 + e) + c + 1)
                act.activation(ffT[e % 2][:, c, :], ps[:, c % 2, :], ACT.Relu,
                               bias=b1e[:, e * FC + c:e * FC + c + 1]).then_inc(m_hid, 1)

        def side_by_side(n, m):
            side = n is not None
            hidden(m, 0)
            if side:
                x2_turned(n)
            gate_exp(m)
            hidden(m, 1)
            gates_turned(m)
            if side:
                ff_hidden(n, range(FC))
            hidden(m, 2)
            if side:
                x3_turned(n)
            hidden(m, 3)
            if side:
                for j in range(GB):
                    l2_hidden(n, j)
            for e in range(4, 7):
                hidden(m, e)
            if side:
                x4_turned(n)
            hidden(m, 7)

        x2_turned(0)
        ff_hidden(0, range(FC))
        x3_turned(0)
        for j in range(GB):
            l2_hidden(0, j)
        x4_turned(0)
        side_by_side(1, 0)
        with act.Fori(2, NG) as n:
            side_by_side(n, n - 1)
        side_by_side(None, NG - 1)

    def rsqrt(ch, v, var, eps, n):
        ve, a, y = rs[:, 0, 0:n], rs[:, 1, 0:n], rs[:, 3, 0:n]
        ch.step(v.tensor_scalar(ve, var, eps, None, ALU.add))
        ch.step(v.tensor_scalar(a.bitcast(I32), ve.bitcast(I32), 1, None, ALU.logical_shift_right))
        ch.step(v.tensor_scalar(y.bitcast(I32), a.bitcast(I32), -1.0, float(0x5F3759DF), ALU.mult, ALU.add))
        for _ in range(3):
            ch.step(v.tensor_tensor(a, y, y, ALU.mult))
            ch.step(v.scalar_tensor_tensor(out=a, in0=a, scalar=-0.5, in1=ve, op0=ALU.mult, op1=ALU.mult))
            ch.step(v.scalar_tensor_tensor(out=y, in0=a, scalar=1.5, in1=y, op0=ALU.add, op1=ALU.mult))

    def norm_stats(ch, v, src, eps, n=GB):
        for j in range(n):
            ch.did(v.bn_stats(st[:, j, :], src(j)))
        ch.join_apart(small_loaded, N_SMALL)
        for j in range(n):
            ch.did(v.bn_aggr(mv[:, j, :], st[:, j, :]))
        ch.join()
        rsqrt(ch, v, mv[:, 0:n, 1], eps, n)

    def apply_norm(v, o, i, j):
        return v.tensor_scalar(o, i, mv[:, j, 0:1], rs[:, 3, j:j + 1], ALU.subtract, ALU.mult)

    @block.vector
    def _(v):
        ch = Chain(v, setup_v)
        v.wait_ge(small_loaded, N_SMALL)
        ch.step(v.tensor_copy(idf[:, 0:4, :], ids[:, :, :]))
        id0, tim, i2, i3 = (idf[:, i, :] for i in range(4))
        ch.did(v.tensor_scalar(idf[:, 4, :], id0, 0.0, float(E0 - 1), ALU.max, ALU.min))
        ch.did(v.tensor_scalar(idf[:, 7, :], id0, -float(E0), None, ALU.add))
        ch.did(v.tensor_scalar(tmp[:, 0, :], tim, 40.0, FREQ, ALU.mult, ALU.mult))
        ch.did(v.tensor_scalar(i2, i2, 0.0, float(E2 - 1), ALU.max, ALU.min))
        ch.did(v.tensor_scalar(i3, i3, 0.0, float(SUB - 1), ALU.max, ALU.min))
        ch.join()
        ch.did(v.tensor_tensor(idf[:, 5, :], idf[:, 4, :], id0, ALU.is_equal))
        ch.did(v.tensor_scalar(oh[:, 1, :], idf[:, 4, :], IOTA, None, ALU.is_equal))
        ch.did(v.tensor_scalar(oh[:, 2, :], i2, IOTA, None, ALU.is_equal))
        ch.did(v.tensor_scalar(oh[:, 3, :], i3, IOTA, None, ALU.is_equal))
        ch.did(v.tensor_copy(id2[:, :], i2[0:1, :]))
        ch.join()
        assert ch.n == SETUP_ID2, ch.n
        ch.step(v.tensor_tensor(idf[:, 6, :], idf[:, 7, :], idf[:, 5, :], ALU.mult))
        ch.step(v.tensor_scalar(idf[:, 6, :], idf[:, 6, :], float(E0), None, ALU.add))
        ch.step(v.tensor_scalar(oh[:, 0, :], idf[:, 6, :], IOTA, None, ALU.is_equal))
        assert ch.n == SETUP_ONEHOT, ch.n
        ch.step(v.tensor_scalar(tmp[:, 1, :], tmp[:, 0, :], 1.0 / (2.0 * np.pi), TURN, ALU.mult, ALU.add))
        ch.step(v.tensor_scalar(tmp[:, 2, :], tmp[:, 1, :], ROUNDER, None, ALU.add))
        ch.step(v.tensor_scalar(tmp[:, 2, :], tmp[:, 2, :], -ROUNDER, None, ALU.add))
        for part in TWO_PI_PARTS:
            ch.step(v.scalar_tensor_tensor(out=tmp[:, 0, :], in0=tmp[:, 2, :], scalar=-part, in1=tmp[:, 0, :],
                                           op0=ALU.mult, op1=ALU.add))
        ch.step(v.tensor_scalar(tmp[:, 0, :], tmp[:, 0, :], PHASE, float(np.float32(3.1415925)), ALU.add, ALU.min))
        ch.step(v.tensor_scalar(tmp[:, 5, :], tmp[:, 0, :], -float(np.float32(3.1415925)), None, ALU.max))
        assert ch.n == SETUP_ANGLE, ch.n
        v.wait_ge(setup_pe, 1)
        ch.did(v.tensor_copy(wsel[:, :, :], ps[0:A0, 4, :].rearrange("p (o b) -> p b o", o=A0)))
        v.wait_ge(setup_pe, 2)
        ch.did(v.tensor_copy(domb[:, :], ps[0:A0, 5, 0:B]))
        assert ch.n == SETUP_WSEL, ch.n
        v.wait_ge(setup_pe, 4)
        ch.did(v.tensor_copy(bi2[:, :, :], ps[:, 6, 32:32 + FC * B].rearrange("p (c b) -> p c b", c=FC)))
        ch.did(v.tensor_scalar(ada[:, 0, :], ps[:, 6, 0:B], col(C_ADA0), 1.0, ALU.add, ALU.add))
        ch.did(v.tensor_scalar(ada[:, 1, :], ps[:, 6, B:2 * B], col(C_ADA1), None, ALU.add))
        ch.did(v.tensor_reduce(nanfix[:, :], mask[:, :, :], AX, ALU.min))
        ch.did(v.tensor_scalar(col(C_BQ), col(C_BQ), DH ** -0.5, None, ALU.mult))
        ch.join()
        assert ch.n == SETUP_ADA, ch.n
        ch.step(v.tensor_scalar(nanfix[:, :], nanfix[:, :], 3.0e38, 3.0e38, ALU.mult, ALU.mult))
        ch.step(v.tensor_scalar(nanfix[:, :], nanfix[:, :], 0.0, None, ALU.mult))

        lc = Chain(v, l0_v)
        for g in range(NG):
            v.wait_ge(exp_psum, g + 1)
            v.tensor_tensor(eT[0:A0, g * GT:(g + 1) * GT].rearrange("p (b s) -> p b s", b=GB),
                            ps[0:A0, 4 + g % 2, :].rearrange("p (b s) -> p b s", b=GB),
                            domb[:, g * GB:(g + 1) * GB].unsqueeze(2).to_broadcast([A0, GB, S]),
                            ALU.add).then_inc(eT_ready, 1)

        def l0_first(g):
            sl = slice(g * GB, (g + 1) * GB)
            v.wait_ge(up_psum, g + 1)
            v.tensor_tensor(x1[:, sl, :], bank4(6 + g % 2), x_in[:, sl, :], ALU.add).then_inc(up_read, 1)
            v.wait_ge(up_read, g + 1)
            norm_stats(lc, v, lambda j: x1[:, g * GB + j, :], 1e-5)
            for j in range(GB):
                ins = apply_norm(v, xn1[:, g * GB + j, :], x1[:, g * GB + j, :], j)
            ins.then_inc(xa_ready, 1)
            v.wait_ge(xa_ready, g + 1)

        def l0_second(g):
            v.wait_ge(x1_ready, g + 1)
            norm_stats(lc, v, lambda j: x1[:, g * GB + j, :], 1e-5)
            for j in range(GB):
                ins = apply_norm(v, xn1[:, g * GB + j, :], x1[:, g * GB + j, :], j)
                if j < GB - 1:
                    lc.did(ins)
            ins.then_inc(xn1_ready, 1)

        def project_in(g):
            for which in range(2):
                v.wait_ge(qkf_ready, 2 * g + which + 1)
                if g:
                    v.wait_ge(pieces_out[which], 16 * g)
                v.tensor_copy(pieces[which][:, 0, :], qkf[which][:, :]).then_inc(piece1, 1)
                v.wait_ge(rest1, 2 * g + which + 1)
                v.tensor_copy(pieces[which][:, 1, :], qkf[which][:, :]).then_inc(piece2, 1)
            sl = slice(g * GB, (g + 1) * GB)
            v.wait_ge(vy_psum, g + 1)
            b0 = 4 + 2 * (g % 2)
            vy = ps[:, b0:b0 + 2, :].rearrange("p n (j c) -> p (n j) c", j=2)
            lc.did(v.tensor_tensor(v_rows[:, sl, :], vy[:, :, 0:D], rows[:, 2:3, :].to_broadcast([S, GB, D]), ALU.add))
            v.tensor_tensor(y_rows[:, sl, :], vy[:, :, D:2 * D], rows[:, 3:4, :].to_broadcast([S, GB, D]),
                            ALU.add).then_inc(vy_read, 1)

        for g in range(NG):
            l0_first(g)
            if g:
                l0_second(g - 1)
        project_in(0)
        l0_second(NG - 1)
        for g in range(1, NG):
            project_in(g)

        v.wait_ge(memsets, 6)
        NATT = 3
        def attend(t, j, first):
            for q in range(NQ):
                if q == 0:
                    g1 = (t - j + GB)
                    v.wait_ge(bias_loaded[j], 4 * g1)
                wait_apart(v, scores_ready, NQ * t + q + 1, small_loaded, N_SMALL)
                for i in range(HQ):
                    h = q * HQ + i
                    ins = v.tensor_tensor_reduce(biasx[:, j, h, :], bank4(q % 2)[:, i, :], biasx[:, j, h, :], 1.0,
                                                 -3.0e38, ALU.add, ALU.max, mx[:, j % 2, h:h + 1])
                ins.then_inc(scores_read, 1)
                if q == 1 and not (isinstance(t, int) and t < 2):
                        finish(t - 2)
            v.wait_ge(scores_read, NQ * (t + 1))
            if not first:
                v.wait_ge(mT_psum, t)
            m, n = mx[:, j % 2, :], NATT * t
            v.tensor_scalar(mp[:, 0:16], m, -1.0, None, ALU.mult).then_inc(att_v, 1)
            v.wait_ge(att_v, n + 1)
            v.scalar_tensor_tensor(out=mres[:, :], in0=m, scalar=-1.0, in1=mp[:, 0:16], op0=ALU.mult,
                                   op1=ALU.subtract).then_inc(att_v, 1)
            v.wait_ge(att_v, n + 2)
            v.tensor_copy(mp[:, 16:32], mres[:, :]).then_inc(att_v, 1)
            v.wait_ge(att_v, n + 3)
            v.tensor_tensor(mp[:, 32:48], mres[:, :], mp[:, 16:32], ALU.subtract).then_inc(mp_ready, 1)
            v.wait_ge(mp_ready, t + 1)
            if not first:
                divide(t - 1)

        def divide(t):
            v.wait_ge(ctxn_psum, t + 1)
            if not (isinstance(t, int) and t == 0):
                v.wait_ge(ctx2_psum, t)
            nat = bank4(6).rearrange("p q (i r) -> p (q i) r", i=HQ)
            v.tensor_scalar(den[:, :], nat[:, :, DH], nanfix[:, bass.ds(t, 1)], None, ALU.add).then_inc(den_v, 1)
            v.wait_ge(den_v, 2 * t + 1)
            v.reciprocal(rden[:, :], den[:, :]).then_inc(den_v, 1)
            v.wait_ge(den_v, 2 * t + 2)
            v.tensor_tensor(ctxn[:, :].rearrange("p (h r) -> p h r", h=H), nat[:, :, 0:DH],
                            rden[:, :].unsqueeze(2).to_broadcast([S, H, DH]), ALU.mult).then_inc(ctxn_ready, 1)

        def finish(t):
            v.wait_ge(wo_psum, t + 1)
            v.tensor_tensor(x2[:, bass.ds(t, 1), :].rearrange("p a d -> p (a d)"), ps[:, 7, 128:256],
                            y_rows[:, bass.ds(t, 1), :].rearrange("p a d -> p (a d)"), ALU.add).then_inc(x2_ready, 1)

        for j in range(GB):
            attend(j, j, j == 0)
        with v.Fori(1, NG) as g:
            for j in range(GB):
                attend(g * GB + j, j, False)
        finish(B - 2)
        divide(B - 1)
        finish(B - 1)

        fc = Chain(v, ffn_v)
        for first, count in ((0, GB), (GB, B - GB)):
            v.wait_ge(x2_ready, first + count)
            norm_stats(fc, v, lambda j: x2[:, first + j, :], 1e-5, count)
            for j in range(count):
                ins = apply_norm(v, xs1[:, first + j, :], x2[:, first + j, :], j)
                if j < count - 1:
                    fc.did(ins)
            ins.then_inc(xs_ready, 1)
            v.wait_ge(xs_ready, 1 if first == 0 else 2)
        v.wait_ge(l_act, 5)
        fc.step(v.scalar_tensor_tensor(out=sty[:, 0, :], in0=sty[:, 2, :], scalar=0.0, in1=sty[:, 3, :],
                                       op0=ALU.max, op1=ALU.add))
        fc.step(v.tensor_scalar(sty[:, 0, :], sty[:, 0, :], 1e-8, None, ALU.add))

        def residual3(n):
            v.wait_ge(w2_psum, n + 1)
            v.wait_ge(x2b_ready, n + 1)
            v.tensor_tensor(x3, bank4(7), x2[:, bass.ts(n, GB), :], ALU.add).then_inc(x3_ready, 1)

        def norm4(sc, n):
            v.wait_ge(wo2_psum, GB * (n + 1))
            v.wait_ge(x3_ready, n + 1)
            v.tensor_tensor(r3, bank4(7), x3, ALU.add).then_inc(r3_sum, 1)
            v.wait_ge(r3_sum, n + 1)
            v.wait_ge(rows2_loaded, 16 * GB * (n + 1))
            sc.step(v.tensor_tensor(r3, r3, rows2[:, :, 0, :], ALU.add))
            norm_stats(sc, v, lambda j: r3[:, j, :], 1e-12)
            for j in range(GB):
                sc.did(apply_norm(v, r3[:, j, :], r3[:, j, :], j))
            sc.join()
            sc.step(v.tensor_tensor(r3, r3, rows2[:, :, 1, :], ALU.mult))
            v.tensor_tensor(x4[:, bass.ts(n, GB), :], r3, rows2[:, :, 2, :], ALU.add).then_inc(x4_ready, 1)
            v.wait_ge(x4_ready, n + 1)

        def norm_l3(sc, n):
            row = lambda j: x4[:, bass.ds(n * GB + j, 1), :].rearrange("p a d -> p (a d)")
            norm_stats(sc, v, row, 1e-5)
            for j in range(GB):
                ins = apply_norm(v, xs3[:, j, :], row(j), j)
                if j < GB - 1:
                    sc.did(ins)
            ins.then_inc(e_xs, 1)
            v.wait_ge(e_xs, n + 1)

        def token_norm(sc, n):
            v.wait_ge(e_hl, n + 1)
            norm_stats(sc, v, lambda j: hl[:, j, :], 1e-8)
            sl = bass.ts(n, GB)
            sc.step(v.tensor_tensor(rs[:, 3, 0:GB], rs[:, 3, 0:GB], sty[:, 0, sl], ALU.mult))
            sc.step(v.tensor_tensor(rs[:, 1, 0:GB], mv[:, 0:GB, 0], rs[:, 3, 0:GB], ALU.mult))
            sc.step(v.tensor_tensor(rs[:, 2, 0:GB], sty[:, 1, sl], rs[:, 1, 0:GB], ALU.subtract))
            for j in range(GB):
                ins = v.tensor_scalar(hfs[:, j, :], hl[:, j, :], rs[:, 3, j:j + 1], rs[:, 2, j:j + 1], ALU.mult, ALU.add)
                if j < GB - 1:
                    sc.did(ins)
            ins.then_inc(e_hfs, 1)

        def pick(sc, n):
            wait_apart(v, e_logit, n + 1, small_loaded, N_SMALL)
            for j in range(GB):
                sc.did(v.max(top[:, j, :], ps[:, 7, j * E3:(j + 1) * E3]))
            sc.join_apart(small_loaded, N_SMALL)
            for j in range(GB):
                sc.did(v.max_index(topi[:, j, :], top[:, j, :], ps[:, 7, j * E3:(j + 1) * E3]))
            sc.join()
            sc.did(v.tensor_copy(topf[:, :, :], topi[:, :, :]))
            v.tensor_tensor(gate[:, 0, :], top[:, :, 1], top[:, :, 0], ALU.subtract).then_inc(e_top, 1)
            v.wait_ge(e_gate, n + 1)
            sc.step(v.tensor_scalar(gate[:, 2, :], gate[:, 1, :], 1.0, None, ALU.add))
            sc.step(v.reciprocal(gate[:, 2, :], gate[:, 2, :]))
            sc.step(v.tensor_tensor(gate[:, 3, :], gate[:, 1, :], gate[:, 2, :], ALU.mult))
            for j in range(GB):
                sc.did(v.tensor_scalar(combs[:, j, :], iota8[:, :], topf[:, j, 0:1], gate[:, 2, j:j + 1],
                                       ALU.is_equal, ALU.mult))
                sc.did(v.tensor_scalar(comb2[:, j, :], iota8[:, :], topf[:, j, 1:2], gate[:, 3, j:j + 1],
                                       ALU.is_equal, ALU.mult))
            sc.join()
            v.tensor_tensor(combs[:, :, :], combs[:, :, :], comb2[:, :, :], ALU.add).then_inc(e_comb, 1)
            v.wait_ge(e_comb, n + 1)
            sc.step(v.tensor_copy(comb[:, bass.ts(n, GB), :], combs[:, :, :]))

        def add_bias(n):
            v.wait_ge(e_b2, n + 1)
            v.tensor_tensor(x4[:, bass.ts(n, GB), :], bank4(7), x4[:, bass.ts(n, GB), :], ALU.add).then_inc(e_acc, 1)
            v.wait_ge(e_acc, n + 1)

        def add_expert(m, e):
            v.wait_ge(m_w2, m * E3 + e + 1)
            if e:
                v.wait_ge(m_acc, GB * (m * E3 + e))
            for j in range(GB):
                b = m * GB + j
                row = x4[:, bass.ds(b, 1), :].rearrange("p a d -> p (a d)")
                v.scalar_tensor_tensor(out=row, in0=bank4(2 + e % 2)[:, j, :],
                                       scalar=comb[:, bass.ds(b, 1), e], in1=row,
                                       op0=ALU.mult, op1=ALU.add).then_inc(m_acc, 1)

        N_NORMS, N_PICK = 75, 21
        def side_by_side(n, m):
            side = n is not None
            sc = Chain(v, side_v, N_NORMS + (N_NORMS + N_PICK) * m)
            pick(sc, m)
            assert sc.n == N_PICK, sc.n
            add_bias(m)
            add_expert(m, 0)
            if side:
                residual3(n)
            add_expert(m, 1)
            add_expert(m, 2)
            if side:
                norm4(sc, n)
            add_expert(m, 3)
            if side:
                norm_l3(sc, n)
            add_expert(m, 4)
            add_expert(m, 5)
            if side:
                token_norm(sc, n)
                assert sc.n == N_PICK + N_NORMS, sc.n
            add_expert(m, 6)
            add_expert(m, 7)

        sc = Chain(v, side_v)
        residual3(0)
        norm4(sc, 0)
        norm_l3(sc, 0)
        token_norm(sc, 0)
        assert sc.n == N_NORMS, sc.n
        side_by_side(1, 0)
        with v.Fori(2, NG) as n:
            side_by_side(n, n - 1)
        side_by_side(None, NG - 1)

    @block.gpsimd
    def _(pool):
        ms = Chain(pool, memsets)
        ms.step(pool.memset(l0_area[32:33, 4096:6144], 1.0))
        ms.step(pool.memset(stack_area[:, :].bitcast(U32), 0))
        pool.wait_ge(small_loaded, N_SMALL)
        ms.step(pool.tensor_copy(identb[:, :], ident[:, :]))
        ms.step(pool.tensor_scalar(maskedb[:, :], ident[:, :], MASKED, None, ALU.mult))
        ms.step(pool.tensor_copy(msel[:, :], hsel))
        ms.step(pool.memset(mp[:, :], 0.0))
        for p in range(2):
            ms.step(pool.memset(vaug[p][:, :, :], 0.0))
            ms.step(pool.memset(vaug[p][:, :, DH:DH + 1], 1.0))
        po = Chain(pool, pool_own)
        for g in range(2 * NG):
            if g < NG:
                pool.wait_ge(xa_ready, g + 1)
                sl = slice(g * GB, (g + 1) * GB)
                po.step(pool.tensor_tensor(x1[:, sl, :], xn1[:, sl, :], rows[:, 0:1, :].to_broadcast([S, GB, D]), ALU.mult))
                pool.tensor_tensor(x1[:, sl, :], x1[:, sl, :], rows[:, 1:2, :].to_broadcast([S, GB, D]),
                                   ALU.add).then_inc(x1_ready, 1)
                pool.wait_ge(x1_ready, g + 1)
            else:
                for which in range(2):
                    k = 2 * (g - NG) + which
                    pool.wait_ge(piece1, k + 1)
                    pool.tensor_tensor(qkf[which][:, :], qkf[which][:, :], pieces[which][:, 0, :],
                                       ALU.subtract).then_inc(rest1, 1)
                    pool.wait_ge(rest1, k + 1)
                    pool.wait_ge(piece2, k + 1)
                    pool.tensor_tensor(pieces[which][:, 2, :], qkf[which][:, :], pieces[which][:, 1, :],
                                       ALU.subtract).then_inc(piece3, 1)
                    pool.wait_ge(piece3, k + 1)
        pool.wait_ge(memsets, 10)
        pool.wait_ge(vy_read, NG)

        def mask_score(t, j, early):
            if not early:
                pool.wait_ge(scores_ready, NQ * (t - 1))
            pool.tensor_copy(mneg[j % 2][:, :], mask[:, bass.ds(t, 1), :].rearrange("p a k -> p (a k)")
                             ).then_inc(mneg_ready, 1)
            pool.wait_ge(mneg_ready, t + 1)

        def values(t, j, early):
            if not early:
                pool.wait_ge(pv_done, NQ * (t - 1))
            pool.tensor_copy(vaug[j % 2][:, :, 0:DH],
                             v_rows[:, bass.ds(t, 1), :].rearrange("p a (h r) -> p (a h) r", h=H)).then_inc(vaug_ready, 1)
            pool.wait_ge(vaug_ready, t + 1)

        mask_score(0, 0, True)
        for j in range(1, GB):
            mask_score(j, j, j < 2)
            values(j - 1, j - 1, j < 3)
        with pool.Fori(1, NG) as g:
            for j in range(GB):
                mask_score(g * GB + j, j, False)
                values(g * GB + j - 1, (j - 1) % GB, False)
        values(B - 1, B - 1, False)

        def residual_bias(n):
            pool.wait_ge(xs_ready, 1 if isinstance(n, int) and n == 0 else 2)
            pool.tensor_tensor(x2[:, bass.ts(n, GB), :], x2[:, bass.ts(n, GB), :],
                               rows[:, 4:5, :].to_broadcast([S, GB, D]), ALU.add).then_inc(x2b_ready, 1)
            pool.wait_ge(x2b_ready, n + 1)

        def keep_columns(n):
            pool.wait_ge(e_hfs, n + 1)
            pool.tensor_copy(hcols[:, bass.ts(n, GT)].rearrange("p (b s) -> p b s", b=GB), hfs).then_inc(e_hcols, 1)
            pool.wait_ge(e_hcols, n + 1)

        residual_bias(0)
        keep_columns(0)
        residual_bias(1)
        keep_columns(1)
        with pool.Fori(2, NG) as n:
            pool.wait_ge(xs_psum, n)
            pool.tensor_copy(xs_slot, xs1[:, bass.ts(n, GB), :]).then_inc(xs_staged, 1)
            pool.wait_ge(xs_staged, n - 1)
            residual_bias(n)
            keep_columns(n)


CONSTS = ["c_ident", "c_cols", "c_iota8", "c_eye_row"]
OUT_SHAPE = (B, S, D)


def kernel(**inputs):
    import concourse.bacc as bacc
    from concourse.bass_utils import run_bass_kernel_spmd

    def arr(name):
        return np.asarray(inputs[name])

    def column(v):
        n = v.shape[0]
        if n > 128:
            return v.reshape(-1, 128).T
        c = np.zeros((128, 1), v.dtype)
        c[:n, 0] = v
        return c

    l0, l1, l2, l3 = "L0_cond_", "L1_cond_", "L2_cond_", "L3_cond_"
    half = D // 2
    freq = np.exp(np.arange(half, dtype=np.float32) * np.float32(-np.log(10000.0) / (half - 1))).astype(np.float32)
    cc = np.zeros((128, 32), np.float32)
    cc[:, 0] = np.arange(128)
    cc[:, 1] = np.concatenate([freq, freq])
    cc[half:, 2] = np.float32(np.pi / 2)
    cc[half:, 3] = 0.25
    for p in range(3):
        cc[p * H:(p + 1) * H, 8:8 + H] = np.eye(H)

    data = {
        "x": arr("x"),
        "attn_bias": arr("fside_Bx16xSxS_0").transpose(0, 2, 1, 3),
        "mask": np.ascontiguousarray(arr("mask_Bx1xSxS_bk0")[:, 0].transpose(1, 0, 2)),
        "expert_W": arr(l0 + "expert_W").reshape(E0, A0 * A0),
        "expert_b": arr(l0 + "expert_b"), "domain_emb": arr(l0 + "domain_emb"),
        "down_WT": arr(l0 + "down_W").T,
        "up_WTb": np.concatenate([arr(l0 + "up_W").T, arr(l0 + "up_b")[None]], 0),
        "W_ada": arr(l1 + "W_ada"), "Wq": arr(l1 + "Wq"), "Wk": arr(l1 + "Wk"), "Wv": arr(l1 + "Wv"),
        "Wo": arr(l1 + "Wo"), "W1": arr(l1 + "W1"),
        "W2": arr(l1 + "W2").reshape(FC, 128, D).transpose(1, 0, 2),
        "subj_emb": arr(l3 + "subj_emb"), "bi": arr(l2 + "bi"),
        "hyp_w1": arr(l3 + "hyp_w1"), "hyp_w2": arr(l3 + "hyp_w2"), "sty_w1": arr(l3 + "sty_w1"),
        "sty_w2": arr(l3 + "sty_w2"), "router_w": arr(l3 + "router_w"), "exp_b2": arr(l3 + "exp_b2"),
        "exp_b1T": arr(l3 + "exp_b1").reshape(E3 * FC, 128).T,
        "exp_w1": arr(l3 + "exp_w1"),
        "exp_w2": arr(l3 + "exp_w2").reshape(E3, FC, 128, D).transpose(2, 0, 1, 3),
        "l2_w": np.concatenate([arr(l2 + "Wi"), arr(l2 + "Wo").reshape(E2, FC, 128, D).transpose(0, 2, 1, 3)
                                .reshape(E2, 128, FC * D)], 2),
        "l2_rows": np.stack([arr(l2 + "bo"), arr(l2 + "gamma"), arr(l2 + "beta")], 1),
        "rows": np.stack([arr(l0 + "ln_gamma"), arr(l0 + "ln_beta"), arr(l1 + "bv"), arr(l1 + "bo"), arr(l1 + "b2")], 0),
        "cols": np.concatenate([column(c) for c in (
            arr(l0 + "down_b"), arr(l1 + "b_ada")[:D], arr(l1 + "b_ada")[D:], arr(l1 + "bq"), arr(l1 + "bk"),
            arr(l1 + "g2"), arr(l1 + "beta2"), arr(l3 + "ln_g"), arr(l3 + "ln_b"), arr(l3 + "hyp_b1"),
            arr(l3 + "hyp_b2"), arr(l3 + "sty_b1"), arr(l3 + "sty_b2")[:D], arr(l3 + "sty_b2")[D:], arr(l1 + "b1"))], 1),
        "c_ident": np.eye(128, dtype=np.float32), "c_cols": cc,
        "c_iota8": np.arange(8, dtype=np.float32), "c_eye_row": np.eye(A0, dtype=np.float32).reshape(1, -1),
    }
    for name in ("itok_B_0_15", "itok_B_34_63", "itok_B_0_7", "itok_B_6_14"):
        data[name] = arr(name)

    nc = bacc.Bacc("TRN2", target_bir_lowering=False, num_devices=1)
    arrays, aps = {}, {}
    for name, a in data.items():
        a = np.ascontiguousarray(a)
        arrays[f"in_{name}"] = a
        aps[name] = nc.dram_tensor(f"in_{name}", a.shape, mybir.dt.from_np(a.dtype), kind="ExternalInput").ap()
    out = nc.dram_tensor("out_0", OUT_SHAPE, F32, kind="ExternalOutput").ap()
    program(nc, aps, out)
    return run_bass_kernel_spmd(nc, [arrays], core_ids=[0]).results[0]["out_0"]
```

```python
from contextlib import ExitStack

import numpy as np

import concourse.bass as bass
from concourse import mybir

F32, BF16, F32R = mybir.dt.float32, mybir.dt.bfloat16, mybir.dt.float32r
I32, U32, U8 = mybir.dt.int32, mybir.dt.uint32, mybir.dt.uint8
ALU = mybir.AluOpType
ACT = mybir.ActivationFunctionType
AX = mybir.AxisListType.X

B, S, D = 16, 128, 128
GB = 4
NG, GT = B // GB, GB * S
A0, E0 = 32, 16
H, DH = 16, 8
HQ = 4
NQ = H // HQ
FF, FC = 512, 4
E2, E3 = 8, 8
SUB, SE = 32, 64
N_CONST, N_EARLY, N_WEIGHT = 200, 1632, 1832
CW = 32
C_VECTORS = 14
MASKED = -1.0e30
Q_PIECES = (0, 0, 1, 1, 0, 2)
K_PIECES = (0, 1, 0, 1, 2, 0)
TWO_PI_PARTS = (6.28125, 0.0019340515136718750, 1.2556659146e-06)
ROUNDER = 12582912.0


SETUP_ID2 = 11
SETUP_ONEHOT = 14
SETUP_ANGLE = 22
SETUP_WSEL = 24
SETUP_ADA = 31


def wait_apart(eng, sem, value, met, met_value):
    value = value if isinstance(value, int) else eng.to_reg(value)
    eng.wait_ge(met, met_value)
    eng.wait_ge(sem, value)


def after_start(eng, sem, value):
    if not (isinstance(value, int) and value <= 0):
        eng.wait_ge(sem, value)


class Chain:

    def __init__(self, eng, sem, base=0):
        self.eng, self.sem, self.base, self.n = eng, sem, base, 0

    def did(self, ins):
        ins.then_inc(self.sem, 1)
        self.n += 1

    def join(self):
        self.eng.wait_ge(self.sem, self.base + self.n)

    def join_apart(self, met, met_value):
        wait_apart(self.eng, self.sem, self.base + self.n, met, met_value)

    def step(self, ins):
        self.did(ins)
        self.join()


def program(nc, t, out):
    ctx = ExitStack()
    with ctx:
        build(nc, ctx, t, out)


def build(nc, ctx, dram, out):
    def sb(name, shape, dt=F32):
        return ctx.enter_context(nc.sbuf_tensor(name, shape, dt))

    def sem(name):
        return ctx.enter_context(nc.semaphore(name))

    x_in = sb("x_in", [S, B, D])
    x2 = x_in
    xn1 = sb("xn1", [S, B, D])
    x4 = xn1
    biasx = sb("biasx", [S, GB, H, S])
    w2_area = sb("w2_area", [128, 4096])
    eT = w2_area[0:A0 + 1, 0:2048]
    x1 = w2_area[:, 2048:4096].rearrange("p (b d) -> p b d", b=B)
    w2e = w2_area[:, 0:4096].rearrange("p (e c d) -> p e c d", e=E3, c=FC)
    w2slot = [biasx[:, j, 0:8, :].rearrange("p a b -> p (a b)") for j in range(GB)]
    rows2 = biasx[:, :, 8:11, :]
    p_area = sb("p_area", [128, 1024])
    pT = [p_area[:, 512 * p:512 * p + 512].rearrange("p (h q) -> p h q", h=HQ) for p in range(2)]
    ew0 = p_area[0:E0 + 1, :]
    wsel = sb("wsel", [A0, B, A0])
    yT = [sb(f"yT{p}", [D, GB, S]) for p in range(2)]
    qkf = [sb(f"qkf{p}", [D, GT]) for p in range(2)]
    pieces = [sb(f"pieces{p}", [D, 3, GT], BF16) for p in range(2)]
    vaug = [sb(f"vaug{p}", [S, H, CW]) for p in range(2)]
    mneg = [sb(f"mneg{j}", [S, S], BF16) for j in range(GB)]
    mask = sb("mask", [S, B, S], U8)
    msel = sb("msel", [128, H], BF16)
    mx = sb("mx", [S, 2, H])
    mres = sb("mres", [S, H])
    mp = sb("mp", [S, 128], BF16)
    mT = sb("mT", [128, S], BF16)
    ctxs = sb("ctxs", [128, NQ, S])
    ctxn = sb("ctxn", [S, D])
    ctx2T = sb("ctx2T", [D, S])
    den = sb("den", [S, H])
    ones = sb("ones", [1, S])
    rden = sb("rden", [S, H])
    nanfix = sb("nanfix", [S, B])
    packed = sb("packed", [128, N_CONST])
    ident, cst, iota8 = packed[:, 0:128], packed[:, 128:160], packed[:, 160:168]
    cols = packed[:, 168:200]
    identb = sb("identb", [128, 128], BF16)
    ids = sb("ids", [128, 4, B], I32)
    idf = sb("idf", [128, 8, B])
    oh = sb("oh", [128, 5, B])
    id2 = sb("id2", [1, B], I32)
    rows = sb("rows", [128, 5, D])
    tmp = sb("tmp", [128, 8, B])
    ada = sb("ada", [D, 2, B])
    domb = sb("domb", [A0, B])
    bi2 = sb("bi2", [128, FC, B])
    sty = sb("sty", [D, 4, B])
    hyp = sb("hyp", [128, 4, B])
    weights = sb("weights", [128, N_WEIGHT])
    w_q, w_k, w_vi, w_o = weights[:, 0:128], weights[:, 128:256], weights[:, 256:512], weights[:, 512:640]
    w_1, w_2 = weights[:, 640:1152], weights[:, 1152:1664].rearrange("p (c d) -> p c d", c=FC)
    w_r, be2, b1e = weights[:, 1664:1672], weights[0:E3, 1672:1800], weights[:, 1800:1832]
    st = sb("st", [128, B, 6])
    mv = sb("mv", [128, B, 2])
    rs = sb("rs", [128, 4, B])
    top = sb("top", [S, GB, 8])
    topi = sb("topi", [S, GB, 8], U32)
    topf = sb("topf", [S, GB, 8])
    gate = sb("gate", [S, 4, GB])
    comb = sb("comb", [S, B, E3])
    comb2 = sb("comb2", [S, GB, E3])
    combs = sb("combs", [S, GB, E3])
    with nc.sbuf_tensor("w1e", [128, 4096], F32) as w1e, \
            nc.sbuf_tensor("v_rows", [S, B, D], F32) as v_rows, \
            nc.sbuf_tensor("y_rows", [S, B, D], F32) as y_rows, \
            nc.sbuf_tensor("query_stack", [128, 2 * H * GT], BF16) as query_stack, \
            nc.sbuf_tensor("key_stack", [128, 2 * H * GT], BF16) as key_stack:
        pass
    xT, hT = w1e[:, 0:2048], w1e[0:A0, 2048:4096]
    qst = query_stack[:, :].rearrange("p (r h t) -> p r h t", r=2, h=H)
    kst = key_stack[:, :].rearrange("p (r h t) -> p r h t", r=2, h=H)
    xs1 = y_rows
    w1e_low = sb("w1e_low", [128, 4096], F32R)
    hcols = sb("hcols", [D, B * S], F32R)
    hcols_low = sb("hcols_low", [D, B * S], F32R)
    ff_area = sb("ff_area", [128, 11776])
    w1e_high = sb("w1e_high", [128, 4096], F32R)
    ffT = [ff_area[:, 2048 * p:2048 * p + 2048].rearrange("p (c t) -> p c t", c=FC) for p in range(2)]
    ff1T = ff_area[:, 4096:6144].rearrange("p (c t) -> p c t", c=FC)
    h2T = [ff_area[:, 6144 + 512 * p:6656 + 512 * p].rearrange("p (c t) -> p c t", c=FC) for p in range(2)]
    hf, x3T, x3, r3, xs3, hl, hfs, xs_slot = (ff_area[:, a:a + 512].rearrange("p (b d) -> p b d", b=GB)
                                              for a in range(7168, 11264, 512))
    combT = ff_area[0:E3, 11264:11776]
    early = y_rows[:, :, :].rearrange("p b d -> p (b d)")
    w_down, w_up, sel_small = early[:, 0:32], early[0:A0 + 1, 32:160], early[0:SUB, 160:288]
    bi_sb, w_h1, w_h2 = early[0:E2, 288:800], early[0:SE, 800:928], early[:, 928:1056]
    w_s1, w_s2, w_ada = early[:, 1056:1120], early[0:64, 1120:1376], early[:, 1376:1632]
    ps = ctx.enter_context(nc.psum_tensor("ps", [128, 8, 512], F32))
    scr = nc.dram_tensor("qk_pieces", [2, 3, 128, B * S], BF16).ap()

    def bank4(n):
        return ps[:, n, :].rearrange("p (a b) -> p a b", a=4)

    IOTA, FREQ, PHASE, TURN = (cst[:, i:i + 1] for i in range(4))
    hsel = cst[:, 8:24]
    (C_DOWN, C_ADA0, C_ADA1, C_BQ, C_BK, C_G2, C_BETA2, C_LNG, C_LNB, C_HB1, C_HB2, C_SB1, C_SG, C_SB,
     C_B1) = range(C_VECTORS + 1)

    def flat(x):
        return x.rearrange("p b d -> p (b d)")

    def col(i, n=128):
        return cols[0:n, i:i + 1]

    x_loaded = [sem(f"x_loaded{g}") for g in range(NG)]
    mask_loaded = sem("mask_loaded")
    first_loaded, early_loaded, weights_loaded = sem("first_loaded"), sem("early_loaded"), sem("weights_loaded")
    bias_loaded = [sem(f"bias_loaded{j}") for j in range(GB)]
    memsets = sem("memsets")
    setup_v = sem("setup_v")
    setup_pe = sem("setup_pe")
    setup_a = sem("setup_a")
    xT_psum, xT_ready = sem("xT_psum"), sem("xT_ready")
    down_psum, gelu_ready = sem("down_psum"), sem("gelu_ready")
    exp_psum, eT_ready = sem("exp_psum"), sem("eT_ready")
    up_psum, up_read = sem("up_psum"), sem("up_read")
    xa_ready, x1_ready, pool_own = sem("xa_ready"), sem("x1_ready"), sem("pool_own")
    xn1_ready, yT_psum, yT_ready = sem("xn1_ready"), sem("yT_psum"), sem("yT_ready")
    qk_psum, qkf_ready, vy_psum, vy_read = sem("qk_psum"), sem("qkf_ready"), sem("vy_psum"), sem("vy_read")
    pieces_v, pieces_p, piece3 = sem("pieces_v"), sem("pieces_p"), [sem("piece3_q"), sem("piece3_k")]
    pieces_out = [sem(f"pieces_out{p}") for p in range(2)]
    stack_in = sem("stack_in")
    vaug_ready, mneg_ready, bias_masked = sem("vaug_ready"), sem("mneg_ready"), sem("bias_masked")
    scores_ready, scores_read = sem("scores_ready"), sem("scores_read")
    mp_ready, mT_psum, mT_ready = sem("mp_ready"), sem("mT_psum"), sem("mT_ready")
    xt_ready, exp_ready = sem("xt_ready"), sem("exp_ready")
    pv_done, ctxs_ready, ctxn_psum, ctxn_ready = (sem("pv_done"), sem("ctxs_ready"), sem("ctxn_psum"),
                                                  sem("ctxn_ready"))
    ctx2_psum, ctx2_ready, wo_psum, x2_ready = sem("ctx2_psum"), sem("ctx2_ready"), sem("wo_psum"), sem("x2_ready")
    l_act, den_v = sem("l_act"), sem("den_v")
    att_v, l0_v, ffn_v, side_v = sem("att_v"), sem("l0_v"), sem("ffn_v"), sem("side_v")
    w2_loaded = [sem(f"w2_loaded{j}") for j in range(GB)]
    rows2_loaded = sem("rows2_loaded")
    w1e_rounded, w1e_split, style_v = sem("w1e_rounded"), sem("w1e_split"), sem("style_v")
    experts_loaded, xs_staged = sem("experts_loaded"), sem("xs_staged")
    xs_ready, xs_psum, hf_ready = sem("xs_ready"), sem("xs_psum"), sem("hf_ready")
    w1_psum, ff_ready, w2_psum, x3_ready, x2b_ready = (sem("w1_psum"), sem("ff_ready"), sem("w2_psum"),
                                                       sem("x3_ready"), sem("x2b_ready"))
    x3T_psum, x3T_ready = sem("x3T_psum"), sem("x3T_ready")
    wi_psum, h2_ready, wo2_psum = sem("wi_psum"), sem("h2_ready"), sem("wo2_psum")
    r3_sum, x4_ready = sem("r3_sum"), sem("x4_ready")
    e_xs, e_psum, e_hl, e_hfs, e_hcols = (sem(n) for n in ("e_xs", "e_psum", "e_hl", "e_hfs", "e_hcols"))
    e_logit, e_top, e_gate, e_comb, e_combT, e_cT, e_b2, e_acc = (
        sem(n) for n in ("e_logit", "e_top", "e_gate", "e_comb", "e_combT", "e_cT", "e_b2", "e_acc"))
    m_w1, m_hid, m_w2, m_acc = (sem(n) for n in ("m_w1", "m_hid", "m_w2", "m_acc"))
    stored = sem("stored")

    block = ctx.enter_context(nc.Block())

    FIRST, EARLY, WEIGHTS = 16 * 4, 16, 16 * 2

    @block.sync
    def _(sp):
        x_dram = dram["x"].rearrange("b s d -> s b d")

        def load_bias(b, j):
            sp.dma_start(biasx[:, j, :, :], dram["attn_bias"][b]).then_inc(bias_loaded[j], 16)

        def load_x(g):
            sp.dma_start(x_in[:, g * GB:(g + 1) * GB, :], x_dram[:, g * GB:(g + 1) * GB, :]).then_inc(x_loaded[g], 16)

        sp.dma_start(ids[:, :, :], dram["ids"].partition_broadcast(128)).then_inc(first_loaded, 16)
        sp.dma_start(packed[:, :], dram["consts"]).then_inc(first_loaded, 16)
        load_x(0)
        sp.dma_start(early[:, 0:288], dram["early"][:, 0:288]).then_inc(first_loaded, 16)
        sp.dma_start(ew0, dram["adapters"]).then_inc(first_loaded, 16)
        for g in range(1, NG):
            load_x(g)
        sp.dma_start(mask[:, :, :], dram["mask"]).then_inc(mask_loaded, 16)
        sp.dma_start(early[:, 288:N_EARLY], dram["early"][:, 288:N_EARLY]).then_inc(early_loaded, 16)
        sp.dma_start(rows[:, :, :], dram["rows"].partition_broadcast(128)).then_inc(weights_loaded, 16)
        sp.dma_start(weights[:, :], dram["weights"]).then_inc(weights_loaded, 16)
        for j in range(GB):
            load_bias(j, j)

        def store_pieces(g, which):
            sp.wait_ge(piece3[which], g + 1)
            sp.dma_start(scr[which, :, :, g * GT:(g + 1) * GT].rearrange("p d t -> d p t"),
                         pieces[which][:, :, :]).then_inc(pieces_out[which], 16)

        def load_stack(g, par):
            for which, st_, pcs in ((0, qst, Q_PIECES), (1, kst, K_PIECES)):
                for c, p in enumerate(pcs):
                    sp.dma_start(st_[DH * c:DH * c + DH, par, :, :],
                                 scr[which, p, :, bass.ts(g, GT)].rearrange("(h r) t -> r h t", r=DH)
                                 ).then_inc(stack_in, 16)

        for g in range(NG):
            for which in range(2):
                store_pieces(g, which)
            if g == 0:
                sp.wait_ge(memsets, 4)
                sp.wait_ge(pieces_out[0], 16)
                sp.wait_ge(pieces_out[1], 16)
                load_stack(0, 0)
        sp.wait_ge(pieces_out[0], 16 * NG)
        sp.wait_ge(pieces_out[1], 16 * NG)

        def load_group(g):
            if not (isinstance(g, int) and g == 1):
                sp.wait_ge(scores_ready, (g - 1) * GB * NQ)
            sp.wait_ge(stack_in, g * 12 * 16)
            load_stack(g, g % 2)
            for j in range(GB):
                sp.wait_ge(xt_ready, ((g - 1) * GB + j + 1) * NQ)
                load_bias(g * GB + j, j)

        load_group(1)
        with sp.Fori(2, NG) as g:
            load_group(g)
        sp.wait_ge(xn1_ready, NG)
        sp.dma_start(w1e[:, :].rearrange("p (e f) -> p e f", e=E3),
                     dram["exp_w1"].rearrange("e d f -> d e f")).then_inc(experts_loaded, 16)
        sp.dma_start(w2e, dram["exp_w2"]).then_inc(experts_loaded, 16)

        def load_l2(b, j):
            e = sp.value_load(id2[0:1, bass.ds(b, 1)], min_val=0, max_val=E2 - 1)
            sp.dma_start(w2slot[j], dram["l2_w"][e]).then_inc(w2_loaded[j], 16)

        def load_rows2(b, j):
            e = sp.value_load(id2[0:1, bass.ds(b, 1)], min_val=0, max_val=E2 - 1)
            sp.dma_start(rows2[:, j, :, :], dram["l2_rows"][e].partition_broadcast(128)).then_inc(rows2_loaded, 16)

        sp.wait_ge(setup_v, SETUP_ID2)
        for j in range(GB):
            sp.wait_ge(xt_ready, (B - GB + j + 1) * NQ)
            load_l2(j, j)
            load_rows2(j, j)

        def refill(g):
            for j in range(GB):
                wait_apart(sp, wo2_psum, (g - 1) * GB + j + 1, setup_v, SETUP_ID2)
                load_l2(g * GB + j, j)
            wait_apart(sp, x4_ready, g, setup_v, SETUP_ID2)
            for j in range(GB):
                load_rows2(g * GB + j, j)

        out_rows = out.rearrange("b s d -> s b d")

        def store(g):
            sp.wait_ge(m_acc, (g + 1) * E3 * GB)
            sp.dma_start(out_rows[:, bass.ts(g, GB), :], x4[:, bass.ts(g, GB), :]).then_inc(stored, 16)

        refill(1)
        with sp.Fori(2, NG) as g:
            refill(g)
            store(g - 2)
        store(NG - 2)
        store(NG - 1)
        sp.wait_ge(stored, 16 * NG)

    @block.tensor
    def _(pe):
        def mm(o, l, r, start=True, stop=True, **kw):
            return pe.matmul(o, l, r, start=start, stop=stop, **kw)

        def turn_x(g):
            pe.wait_ge(x_loaded[g], 16)
            if g >= 2:
                pe.wait_ge(xT_ready, g - 1)
            for j in range(GB):
                ins = pe.transpose(bank4(g % 2)[:, j, :], x_in[:, g * GB + j, :], ident[:, :])
            ins.then_inc(xT_psum, 1)

        pe.wait_ge(first_loaded, FIRST)
        turn_x(0)
        turn_x(1)
        pe.wait_ge(setup_v, SETUP_ONEHOT)
        for o in range(A0):
            ins = mm(ps[0:A0, 4, o * B:(o + 1) * B], ew0[:, o * A0:(o + 1) * A0], oh[0:E0 + 1, 0, :])
        ins.then_inc(setup_pe, 1)
        mm(ps[0:A0, 5, 0:B], sel_small[0:E0, 64:96], oh[0:E0, 0, :], stop=False)
        mm(ps[0:A0, 5, 0:B], sel_small[0:E0, 96:128], oh[0:E0, 1, :], start=False).then_inc(setup_pe, 1)
        turn_x(2)
        turn_x(3)
        for g in range(NG):
            pe.wait_ge(xT_ready, g + 1)
            if g >= 2:
                pe.wait_ge(gelu_ready, g - 1)
            mm(ps[0:A0, 2 + g % 2, :], w_down[:, :], xT[:, g * GT:(g + 1) * GT]).then_inc(down_psum, 1)

        def adapt(g):
            pe.wait_ge(gelu_ready, g + 1)
            if g >= 2:
                pe.wait_ge(eT_ready, g - 1)
            for j in range(GB):
                b = g * GB + j
                ins = mm(ps[0:A0, 4 + g % 2, j * S:(j + 1) * S], wsel[:, b, :], hT[:, b * S:(b + 1) * S])
            ins.then_inc(exp_psum, 1)

        def up(g):
            pe.wait_ge(eT_ready, g + 1)
            if g >= 2:
                pe.wait_ge(up_read, g - 1)
            for j in range(GB):
                b = g * GB + j
                ins = mm(bank4(6 + g % 2)[:, j, :], eT[:, b * S:(b + 1) * S], w_up[:, :])
            ins.then_inc(up_psum, 1)

        pe.wait_ge(memsets, 2)
        pe.wait_ge(setup_v, SETUP_WSEL)
        adapt(0)
        adapt(1)
        up(0)
        adapt(2)
        up(1)
        pe.wait_ge(early_loaded, EARLY)
        for c in range(FC):
            mm(ps[:, 0, 32 + c * B:32 + (c + 1) * B], bi_sb[:, c * 128:(c + 1) * 128], oh[0:E2, 2, :])
        mm(ps[0:SE, 1, 96:112], sel_small[0:SUB, 0:64], oh[0:SUB, 3, :]).then_inc(setup_pe, 1)
        pe.wait_ge(setup_a, 1)
        for i in range(2):
            ins = mm(ps[:, 0, i * B:(i + 1) * B], w_ada[:, i * D:(i + 1) * D], tmp[:, 7, :])
        ins.then_inc(setup_pe, 1)
        adapt(3)
        pe.wait_ge(setup_a, 2)
        mm(ps[:, 1, 112:128], w_h1[:, :], hyp[0:SE, 0, :]).then_inc(setup_pe, 1)
        up(2)
        pe.wait_ge(setup_a, 3)
        mm(ps[:, 1, 128:144], w_h2[:, :], hyp[:, 1, :]).then_inc(setup_pe, 1)
        up(3)
        pe.wait_ge(setup_a, 4)
        mm(ps[0:64, 1, 144:160], w_s1[:, :], hyp[:, 2, :]).then_inc(setup_pe, 1)
        pe.wait_ge(setup_a, 5)
        mm(ps[:, 1, 160:176], w_s2[:, 0:128], hyp[0:64, 3, :])
        mm(ps[:, 1, 176:192], w_s2[:, 128:256], hyp[0:64, 3, :]).then_inc(setup_pe, 1)
        pe.wait_ge(setup_a, 6)
        pe.wait_ge(setup_v, SETUP_ADA)
        pe.wait_ge(weights_loaded, WEIGHTS)

        def turn_x1(g):
            pe.wait_ge(xn1_ready, g + 1)
            if g >= 2:
                pe.wait_ge(yT_ready, g - 1)
            for j in range(GB):
                ins = pe.transpose(bank4(g % 2)[:, j, :], xn1[:, g * GB + j, :], ident[:, :])
            ins.then_inc(yT_psum, 1)

        turn_x1(0)
        for g in range(NG):
            pe.wait_ge(yT_ready, g + 1)
            y = yT[g % 2][:, :, :].rearrange("p b s -> p (b s)")
            for which, w in ((0, w_q), (1, w_k)):
                if g >= 1:
                    pe.wait_ge(qkf_ready, 2 * g - 1 + which)
                mm(ps[:, 2 + which, :], w[:, :], y).then_inc(qk_psum, 1)
            if g < NG - 1:
                turn_x1(g + 1)
            if g == 1:
                pe.wait_ge(up_read, NG)
            if g >= 2:
                pe.wait_ge(vy_read, g - 1)
            for j in range(GB):
                bank = 4 + 2 * (g % 2) + j // 2
                here = ps[:, bank, (j % 2) * 256:(j % 2) * 256 + 256]
                mm(here, yT[g % 2][:, j, :], w_vi[:, :], stop=False)
                ins = mm(here, ones[:, :], rows[0:1, 2:4, :].rearrange("p a d -> p (a d)"), start=False)
            ins.then_inc(vy_psum, 1)

        def scores(tn, gn, jn, q):
            if q == 0 and jn == 0:
                pe.wait_ge(stack_in, (gn + 1) * 12 * 16)
            if not (isinstance(tn, int) and 4 * tn + q < 2):
                pe.wait_ge(scores_read, NQ * tn + q - 1)
            par = gn % 2
            for i in range(HQ):
                h = q * HQ + i
                ins = mm(bank4(q % 2)[:, i, :], qst[:, par, h, jn * S:(jn + 1) * S],
                         kst[:, par, h, jn * S:(jn + 1) * S])
            ins.then_inc(scores_ready, 1)

        def turn(t, j, q):
            if not (isinstance(t, int) and 4 * t + q < 2):
                pe.wait_ge(exp_ready, NQ * t + q - 1)
            for i in range(HQ):
                pe.matmul(bank4(2 + q % 2)[:, i, :], biasx[:, j, q * HQ + i, :], ident[:, :], start=(i == 0),
                          stop=False, is_transpose=True, skip_group_check=True)
            for i in range(HQ):
                ins = mm(bank4(2 + q % 2)[:, i, :], msel[:, q * HQ + i:q * HQ + i + 1].to_broadcast([128, S]), mT[:, :], start=False,
                         stop=True, skip_group_check=True)
            ins.then_inc(xt_ready, 1)

        def values(t, j, q):
            pe.wait_ge(exp_ready, NQ * t + q + 1)
            if q == 0:
                pe.wait_ge(vaug_ready, t + 1)
                if not (isinstance(t, int) and t == 0):
                    pe.wait_ge(ctxs_ready, t)
            for i in range(HQ):
                ins = mm(ps[CW * i:CW * i + CW, 4, q * S:(q + 1) * S], vaug[j % 2][:, q * HQ + i, :],
                         pT[q % 2][:, i, :], tile_position=(0, CW * i))
            ins.then_inc(pv_done, 1)

        def project_a(t):
            pe.wait_ge(ctxs_ready, t + 1)
            if not (isinstance(t, int) and t == 0):
                pe.wait_ge(ctxn_ready, t)
            for q in range(NQ):
                ins = pe.transpose(bank4(6)[:, q, :], ctxs[:, q, :], ident[:, :])
            ins.then_inc(ctxn_psum, 1)

        def project_b(t):
            pe.wait_ge(ctxn_ready, t + 1)
            if not (isinstance(t, int) and t == 0):
                pe.wait_ge(x2_ready, t)
            pe.transpose(ps[:, 7, 0:128], ctxn[:, :], ident[:, :]).then_inc(ctx2_psum, 1)

        def project_c(t):
            pe.wait_ge(ctx2_ready, t + 1)
            mm(ps[:, 7, 128:256], ctx2T[:, :], w_o[:, :]).then_inc(wo_psum, 1)

        def attend(t, g, j, first=False, ahead=2):
            one, two = ((t + k, g if j + k < GB else g + 1, (j + k) % GB) for k in (1, 2))
            pe.wait_ge(mp_ready, t + 1)
            if not first:
                pe.wait_ge(mT_ready, t)
            pe.transpose(ps[:, 5, 0:64].bitcast(BF16), mp[:, :], identb[:, :]).then_inc(mT_psum, 1)
            if ahead >= 1:
                scores(*one, 1)
            pe.wait_ge(mT_ready, t + 1)
            turn(t, j, 0)
            if not first:
                project_a(t - 1)
            turn(t, j, 1)
            if ahead >= 1:
                scores(*one, 2)
            values(t, j, 0)
            if not first:
                project_b(t - 1)
            turn(t, j, 2)
            if ahead >= 1:
                scores(*one, 3)
            values(t, j, 1)
            if not first:
                project_c(t - 1)
            turn(t, j, 3)
            values(t, j, 2)
            if ahead >= 2:
                scores(*two, 0)
            values(t, j, 3)

        pe.wait_ge(memsets, 6)
        pe.wait_ge(yT_ready, NG)
        pe.wait_ge(qkf_ready, 2 * NG)
        pe.wait_ge(vy_read, NG)
        for q in range(NQ):
            scores(0, 0, 0, q)
        scores(1, 0, 1, 0)
        for j in range(GB):
            attend(j, 0, j, first=(j == 0))
        with pe.Fori(1, NG - 1) as g:
            for j in range(GB):
                attend(g * GB + j, g, j)
        for j in range(GB):
            attend(B - GB + j, NG - 1, j, ahead=GB - 1 - j)
        def turn_x2(n, bank=6):
            if isinstance(n, int):
                pe.wait_ge(xs_ready, n + 1)
            else:
                pe.wait_ge(xs_staged, n - 1)
            for j in range(GB):
                x = xs1[:, n * GB + j, :] if isinstance(n, int) else xs_slot[:, j, :]
                ins = pe.transpose(bank4(bank)[:, j, :], x, ident[:, :])
            ins.then_inc(xs_psum, 1)

        def ff_hidden(n, chunks):
            pe.wait_ge(hf_ready, n + 1)
            for c in chunks:
                if c >= 2:
                    pe.wait_ge(ff_ready, FC * n + c - 1)
                mm(ps[:, 4 + c % 2, :], w_1[:, c * 128:(c + 1) * 128], flat(hf)).then_inc(w1_psum, 1)

        def ff_out(n, bank_read=None):
            pe.wait_ge(ff_ready, FC * (n + 1))
            if bank_read:
                pe.wait_ge(*bank_read)
            for j in range(GB):
                for c in range(FC):
                    ins = mm(bank4(7)[:, j, :], ff1T[:, c, j * S:(j + 1) * S], w_2[:, c, :],
                             start=(c == 0), stop=(c == FC - 1))
            ins.then_inc(w2_psum, 1)

        def turn_x3(n):
            pe.wait_ge(x3_ready, n + 1)
            for j in range(GB):
                ins = pe.transpose(bank4(6)[:, j, :], x3[:, j, :], ident[:, :])
            ins.then_inc(x3T_psum, 1)

        def l2_hidden(n, j):
            if j == 0:
                pe.wait_ge(x3T_ready, n + 1)
            pe.wait_ge(w2_loaded[j], 16 * (n + 1))
            if j >= 2:
                pe.wait_ge(h2_ready, GB * n + j - 1)
            for c in range(FC):
                ins = mm(bank4(4 + j % 2)[:, c, :], w2slot[j][:, c * 128:(c + 1) * 128], x3T[:, j, :])
            ins.then_inc(wi_psum, 1)

        def l2_out(n, j):
            pe.wait_ge(h2_ready, GB * n + j + 1)
            for c in range(FC):
                ins = mm(bank4(7)[:, j, :], h2T[j % 2][:, c, :], w2slot[j][:, 512 + c * 128:512 + (c + 1) * 128],
                         start=(c == 0), stop=(c == FC - 1))
            ins.then_inc(wo2_psum, 1)

        def turn_x4(n):
            pe.wait_ge(e_xs, n + 1)
            for j in range(GB):
                ins = pe.transpose(bank4(6)[:, j, :], xs3[:, j, :], ident[:, :])
            ins.then_inc(e_psum, 1)

        def router(n):
            pe.wait_ge(e_hfs, n + 1)
            for j in range(GB):
                ins = mm(ps[:, 7, j * E3:(j + 1) * E3], hfs[:, j, :], w_r[:, :])
            ins.then_inc(e_logit, 1)

        def turn_gates(n):
            pe.wait_ge(e_comb, n + 1)
            for j in range(GB):
                ins = pe.transpose(ps[0:E3, 6, j * S:(j + 1) * S], combs[:, j, :], ident[:, :])
            ins.then_inc(e_combT, 1)

        def gated_bias(n):
            pe.wait_ge(e_cT, n + 1)
            for j in range(GB):
                ins = mm(bank4(7)[:, j, :], combT[:, j * S:(j + 1) * S], be2[:, :])
            ins.then_inc(e_b2, 1)

        def hidden(m, e, chunks):
            if e == 0 and chunks[0] == 0:
                pe.wait_ge(e_hcols, m + 1)
            for c in chunks:
                after_start(pe, m_hid, FC * (m * E3 + e) + c - 1)
                w = slice(e * FF + c * 128, e * FF + (c + 1) * 128)
                low, high = w1e_low[:, w], w1e_high[:, w]
                tokens = bass.ts(m, GT)
                mm(ps[:, c % 2, :], low, hcols[:, tokens], stop=False)
                mm(ps[:, c % 2, :], high, hcols_low[:, tokens], start=False, stop=False)
                mm(ps[:, c % 2, :], high, hcols[:, tokens], start=False).then_inc(m_w1, 1)

        def output(m, e, sequences):
            if sequences[0] == 0:
                pe.wait_ge(m_hid, FC * (m * E3 + e + 1))
                after_start(pe, m_acc, GB * (m * E3 + e - 1))
            for j in sequences:
                for c in range(FC):
                    ins = mm(bank4(2 + e % 2)[:, j, :], ffT[e % 2][:, c, j * S:(j + 1) * S], w2e[:, e, c, :],
                             start=(c == 0), stop=(c == FC - 1))
            if sequences[-1] == GB - 1:
                ins.then_inc(m_w2, 1)

        def side_by_side(n, m, begun=False):
            side = n is not None
            first, second = (0, 1), (2, 3)
            hidden(m, 0, first)
            router(m)
            if side and not begun:
                turn_x2(n)
            hidden(m, 0, second)
            hidden(m, 1, first)
            if side and not begun:
                ff_hidden(n, first)
            output(m, 0, first)
            turn_gates(m)
            hidden(m, 1, second)
            if side and not begun:
                ff_hidden(n, second)
            output(m, 0, second)
            gated_bias(m)
            hidden(m, 2, first)
            output(m, 1, first)
            hidden(m, 2, second)
            if side and not begun:
                ff_out(n, (e_acc, n))
            output(m, 1, second)
            if side and not begun:
                turn_x3(n)
            hidden(m, 3, first)
            output(m, 2, first)
            if side and not begun:
                l2_hidden(n, 0)
                l2_hidden(n, 1)
            hidden(m, 3, second)
            if side:
                l2_out(n, 0)
                l2_hidden(n, 2)
                l2_out(n, 1)
                l2_hidden(n, 3)
                l2_out(n, 2)
            output(m, 2, second)
            if side:
                l2_out(n, 3)
            for e in range(4, E3):
                hidden(m, e, first)
                output(m, e - 1, first)
                hidden(m, e, second)
                if side and e == 6:
                    turn_x4(n)
                output(m, e - 1, second)
            output(m, E3 - 1, first + second)

        pe.wait_ge(scores_read, NQ * B)
        project_a(B - 1)
        turn_x2(0, 0)
        pe.wait_ge(mT_ready, B)
        project_b(B - 1)
        ff_hidden(0, (0,))
        project_c(B - 1)
        ff_hidden(0, (1, 2, 3))
        pe.wait_ge(x2_ready, B)
        pe.wait_ge(exp_ready, NQ * B)
        ff_out(0)
        turn_x3(0)
        l2_hidden(0, 0)
        for j in range(1, GB):
            l2_hidden(0, j)
            l2_out(0, j - 1)
        l2_out(0, GB - 1)
        turn_x2(1)
        ff_hidden(1, range(FC))
        ff_out(1, (r3_sum, 1))
        turn_x4(0)
        pe.wait_ge(e_hl, 1)
        turn_x3(1)
        l2_hidden(1, 0)
        l2_hidden(1, 1)
        pe.wait_ge(experts_loaded, 32)
        pe.wait_ge(w1e_split, E3)
        side_by_side(1, 0, begun=True)
        with pe.Fori(2, NG) as n:
            side_by_side(n, n - 1)
        side_by_side(None, NG - 1)

    @block.scalar
    def _(act):
        def affine(o, i, scale, bias):
            return act.activation(o, i, ACT.Identity, scale=scale, bias=bias)

        act.preload_act_table(ACT.Gelu)
        for g in range(NG):
            act.wait_ge(xT_psum, g + 1)
            act.activation(xT[:, g * GT:(g + 1) * GT], ps[:, g % 2, :], ACT.Copy).then_inc(xT_ready, 1)
        for g in range(NG):
            act.wait_ge(down_psum, g + 1)
            act.activation(hT[:, g * GT:(g + 1) * GT], ps[0:A0, 2 + g % 2, :], ACT.Gelu,
                           bias=col(C_DOWN, A0)).then_inc(gelu_ready, 1)
        act.wait_ge(setup_v, SETUP_ANGLE)
        act.activation(tmp[:, 6, :], tmp[:, 5, :], ACT.Sin).then_inc(l_act, 1)
        act.wait_ge(l_act, 1)
        act.activation(tmp[:, 7, :], tmp[:, 6, :], ACT.Silu).then_inc(setup_a, 1)
        act.wait_ge(setup_pe, 3)
        act.activation(hyp[0:SE, 0, :], ps[0:SE, 1, 96:112], ACT.Copy).then_inc(setup_a, 1)
        act.wait_ge(setup_pe, 5)
        act.activation(hyp[:, 1, :], ps[:, 1, 112:128], ACT.Relu, bias=col(C_HB1)).then_inc(setup_a, 1)
        act.wait_ge(setup_pe, 6)
        affine(hyp[:, 2, :], ps[:, 1, 128:144], 1.0, col(C_HB2)).then_inc(setup_a, 1)
        act.wait_ge(setup_pe, 7)
        act.activation(hyp[0:64, 3, :], ps[0:64, 1, 144:160], ACT.Relu, bias=col(C_SB1, 64)).then_inc(setup_a, 1)
        act.wait_ge(setup_pe, 8)
        affine(sty[:, 2, :], ps[:, 1, 160:176], 1.0, col(C_SG)).then_inc(l_act, 1)
        affine(sty[:, 1, :], ps[:, 1, 176:192], 1.0, col(C_SB)).then_inc(setup_a, 1)

        act.wait_ge(setup_v, SETUP_ADA)
        act.preload_act_table(ACT.Exp)

        def scale_mask(t, j):
            act.activation(mneg[j][:, :], mask[:, bass.ds(t, 1), :].rearrange("p a k -> p (a k)"), ACT.Copy,
                           scale=MASKED).then_inc(mneg_ready, 1)

        act.wait_ge(mask_loaded, 16)
        scale_mask(0, 0)
        scale_mask(1, 1)
        scale_mask(2, 2)
        def modulate(g):
            act.wait_ge(yT_psum, g + 1)
            if g >= 2:
                act.wait_ge(vy_psum, g - 1)
            for j in range(GB):
                b = g * GB + j
                ins = affine(yT[g % 2][:, j, :], bank4(g % 2)[:, j, :], ada[:, 0, b:b + 1], ada[:, 1, b:b + 1])
            ins.then_inc(yT_ready, 1)

        modulate(0)
        for g in range(NG):
            for which, cb, sc in ((0, C_BQ, DH ** -0.5), (1, C_BK, 1.0)):
                act.wait_ge(qk_psum, 2 * g + which + 1)
                if g >= 1:
                    act.wait_ge(piece3[which], g)
                    act.wait_ge(pieces_out[which], 16 * g)
                affine(pieces[which][:, 0, :], ps[:, 2 + which, :], sc, col(cb))
                affine(qkf[which][:, :], ps[:, 2 + which, :], sc, col(cb)).then_inc(qkf_ready, 1)
            if g < NG - 1:
                modulate(g + 1)
            act.wait_ge(vy_psum, g + 1)
            b0 = 4 + 2 * (g % 2)
            vy = ps[:, b0:b0 + 2, :].rearrange("p n (j c) -> p (n j) c", j=2)
            act.activation(v_rows[:, g * GB:(g + 1) * GB, :], vy[:, :, 0:D], ACT.Copy)
            act.activation(y_rows[:, g * GB:(g + 1) * GB, :], vy[:, :, D:2 * D], ACT.Copy).then_inc(vy_read, 1)

        def context_out(t):
            act.wait_ge(pv_done, NQ * (t + 1))
            if not (isinstance(t, int) and t == 0):
                act.wait_ge(ctxn_psum, t)
            act.activation(ctxs[:, :, :], bank4(4), ACT.Copy).then_inc(ctxs_ready, 1)

        def context_turned(t):
            act.wait_ge(ctx2_psum, t + 1)
            if not (isinstance(t, int) and t == 0):
                act.wait_ge(wo_psum, t)
            act.activation(ctx2T[:, :], ps[:, 7, 0:128], ACT.Copy).then_inc(ctx2_ready, 1)

        def exponent(t, q):
            act.wait_ge(xt_ready, NQ * t + q + 1)
            if not (isinstance(t, int) and 4 * t + q < 2):
                act.wait_ge(pv_done, NQ * t + q - 1)
            act.activation(pT[q % 2], bank4(2 + q % 2), ACT.Exp).then_inc(exp_ready, 1)

        def attend(t, j, first=False, ahead=3):
            act.wait_ge(mT_psum, t + 1)
            if not first:
                act.wait_ge(xt_ready, NQ * t)
            act.activation(mT[:, :], ps[:, 5, 0:64].bitcast(BF16), ACT.Copy).then_inc(mT_ready, 1)
            if not first:
                context_out(t - 1)
            exponent(t, 0)
            if ahead >= 3:
                if not first:
                    act.wait_ge(bias_masked, t)
                scale_mask(t + 3, (j + 3) % GB)
            exponent(t, 1)
            if not first:
                context_turned(t - 1)
            exponent(t, 2)
            exponent(t, 3)

        for j in range(GB):
            attend(j, j, first=(j == 0))
        with act.Fori(1, NG - 1) as g:
            for j in range(GB):
                attend(g * GB + j, j)
        for j in range(GB):
            attend(B - GB + j, j, ahead=GB - 1 - j)

        def x2_turned(n, bank=6):
            act.wait_ge(xs_psum, n + 1)
            affine(hf, bank4(bank), col(C_G2), col(C_BETA2)).then_inc(hf_ready, 1)

        def ff_hidden(n, chunks):
            for c in chunks:
                act.wait_ge(w1_psum, FC * n + c + 1)
                act.activation(ff1T[:, c, :], ps[:, 4 + c % 2, :], ACT.Gelu_apprx_sigmoid,
                               bias=col(C_B1 + c)).then_inc(ff_ready, 1)

        def x3_turned(n):
            act.wait_ge(x3T_psum, n + 1)
            act.activation(x3T, bank4(6), ACT.Copy).then_inc(x3T_ready, 1)

        def l2_hidden(n, j):
            act.wait_ge(wi_psum, GB * n + j + 1)
            if j >= 2:
                act.wait_ge(wo2_psum, GB * n + j - 1)
            for c in range(FC):
                ins = act.activation(h2T[j % 2][:, c, :], bank4(4 + j % 2)[:, c, :], ACT.Gelu,
                                     bias=bi2[:, c, bass.ds(n * GB + j, 1)])
            ins.then_inc(h2_ready, 1)

        def x4_turned(n):
            act.wait_ge(e_psum, n + 1)
            affine(hl, bank4(6), col(C_LNG), col(C_LNB)).then_inc(e_hl, 1)

        def gate_tanh(n):
            act.wait_ge(e_top, n + 1)
            act.activation(gate[:, 1, :], gate[:, 0, :], ACT.Tanh, scale=0.5).then_inc(e_gate, 1)

        def gates_turned(n):
            act.wait_ge(e_combT, n + 1)
            act.activation(combT[:, :], ps[0:E3, 6, :], ACT.Copy).then_inc(e_cT, 1)

        def hidden(m, e, chunks=range(FC)):
            if chunks[0] == 0:
                after_start(act, m_w2, m * E3 + e - 1)
            for c in chunks:
                act.wait_ge(m_w1, FC * (m * E3 + e) + c + 1)
                act.activation(ffT[e % 2][:, c, :], ps[:, c % 2, :], ACT.Relu,
                               bias=b1e[:, e * FC + c:e * FC + c + 1]).then_inc(m_hid, 1)

        def side_by_side(n, m, begun=False):
            side = n is not None
            first, second = (0, 1), (2, 3)
            hidden(m, 0, first)
            if side and not begun:
                x2_turned(n)
            gate_tanh(m)
            hidden(m, 0, second)
            hidden(m, 1, first)
            if side and not begun:
                ff_hidden(n, first)
            gates_turned(m)
            hidden(m, 1, second)
            if side and not begun:
                ff_hidden(n, second)
            hidden(m, 2)
            if side and not begun:
                x3_turned(n)
            hidden(m, 3, first)
            if side and not begun:
                l2_hidden(n, 0)
                l2_hidden(n, 1)
            hidden(m, 3, second)
            if side:
                l2_hidden(n, 2)
                l2_hidden(n, 3)
            for e in range(4, 7):
                hidden(m, e)
            if side:
                x4_turned(n)
            hidden(m, 7)

        context_out(B - 1)
        x2_turned(0, 0)
        context_turned(B - 1)
        ff_hidden(0, range(FC))
        act.wait_ge(scores_ready, NQ * B)
        act.wait_ge(experts_loaded, 32)
        for e in range(0, E3, 4):
            act.activation(w1e_high[:, e * FF:(e + 4) * FF], w1e[:, e * FF:(e + 4) * FF], ACT.Copy).then_inc(w1e_rounded, 1)
        x3_turned(0)
        for j in range(GB):
            l2_hidden(0, j)
        x2_turned(1)
        ff_hidden(1, range(FC))
        act.wait_ge(l_act, 2)
        act.activation(sty[:, 3, :], sty[:, 2, :], ACT.Abs).then_inc(l_act, 1)
        act.wait_ge(l_act, 3)
        act.activation(sty[:, 3, :], sty[:, 3, :], ACT.Exp, scale=-1.0).then_inc(l_act, 1)
        act.wait_ge(l_act, 4)
        act.activation(sty[:, 3, :], sty[:, 3, :], ACT.Ln, bias=1.0).then_inc(l_act, 1)

        x4_turned(0)
        x3_turned(1)
        l2_hidden(1, 0)
        l2_hidden(1, 1)
        side_by_side(1, 0, begun=True)
        with act.Fori(2, NG) as n:
            side_by_side(n, n - 1)
        side_by_side(None, NG - 1)

    def rsqrt(ch, v, var, eps, n):
        ve, a, y = rs[:, 0, 0:n], rs[:, 1, 0:n], rs[:, 3, 0:n]
        ch.step(v.tensor_scalar(ve, var, eps, None, ALU.add))
        ch.step(v.tensor_scalar(a.bitcast(I32), ve.bitcast(I32), 1, None, ALU.logical_shift_right))
        ch.step(v.tensor_scalar(y.bitcast(I32), a.bitcast(I32), -1.0, float(0x5F3759DF), ALU.mult, ALU.add))
        for _ in range(3):
            ch.step(v.tensor_tensor(a, y, y, ALU.mult))
            ch.step(v.scalar_tensor_tensor(out=a, in0=a, scalar=-0.5, in1=ve, op0=ALU.mult, op1=ALU.mult))
            ch.step(v.scalar_tensor_tensor(out=y, in0=a, scalar=1.5, in1=y, op0=ALU.add, op1=ALU.mult))

    def norm_stats(ch, v, src, eps, n=GB):
        for j in range(n):
            ch.did(v.bn_stats(st[:, j, :], src(j)))
        ch.join_apart(first_loaded, FIRST)
        for j in range(n):
            ch.did(v.bn_aggr(mv[:, j, :], st[:, j, :]))
        ch.join()
        rsqrt(ch, v, mv[:, 0:n, 1], eps, n)

    def apply_norm(v, o, i, j):
        return v.tensor_scalar(o, i, mv[:, j, 0:1], rs[:, 3, j:j + 1], ALU.subtract, ALU.mult)

    @block.vector
    def _(v):
        ch = Chain(v, setup_v)
        v.wait_ge(first_loaded, FIRST)
        ch.step(v.tensor_copy(idf[:, 0:4, :], ids[:, :, :]))
        id0, tim, i2, i3 = (idf[:, i, :] for i in range(4))
        ch.did(v.tensor_scalar(idf[:, 4, :], id0, 0.0, float(E0 - 1), ALU.max, ALU.min))
        ch.did(v.tensor_scalar(idf[:, 7, :], id0, -float(E0), None, ALU.add))
        ch.did(v.tensor_scalar(tmp[:, 0, :], tim, 40.0, FREQ, ALU.mult, ALU.mult))
        ch.did(v.tensor_scalar(i2, i2, 0.0, float(E2 - 1), ALU.max, ALU.min))
        ch.did(v.tensor_scalar(i3, i3, 0.0, float(SUB - 1), ALU.max, ALU.min))
        ch.join()
        ch.did(v.tensor_tensor(idf[:, 5, :], idf[:, 4, :], id0, ALU.is_equal))
        ch.did(v.tensor_scalar(oh[:, 1, :], idf[:, 4, :], IOTA, None, ALU.is_equal))
        ch.did(v.tensor_scalar(oh[:, 2, :], i2, IOTA, None, ALU.is_equal))
        ch.did(v.tensor_scalar(oh[:, 3, :], i3, IOTA, None, ALU.is_equal))
        ch.did(v.tensor_copy(id2[:, :], i2[0:1, :]))
        ch.join()
        assert ch.n == SETUP_ID2, ch.n
        ch.step(v.tensor_tensor(idf[:, 6, :], idf[:, 7, :], idf[:, 5, :], ALU.mult))
        ch.step(v.tensor_scalar(idf[:, 6, :], idf[:, 6, :], float(E0), None, ALU.add))
        ch.step(v.tensor_scalar(oh[:, 0, :], idf[:, 6, :], IOTA, None, ALU.is_equal))
        assert ch.n == SETUP_ONEHOT, ch.n
        ch.step(v.tensor_scalar(tmp[:, 1, :], tmp[:, 0, :], 1.0 / (2.0 * np.pi), TURN, ALU.mult, ALU.add))
        ch.step(v.tensor_scalar(tmp[:, 2, :], tmp[:, 1, :], ROUNDER, None, ALU.add))
        ch.step(v.tensor_scalar(tmp[:, 2, :], tmp[:, 2, :], -ROUNDER, None, ALU.add))
        for part in TWO_PI_PARTS:
            ch.step(v.scalar_tensor_tensor(out=tmp[:, 0, :], in0=tmp[:, 2, :], scalar=-part, in1=tmp[:, 0, :],
                                           op0=ALU.mult, op1=ALU.add))
        ch.step(v.tensor_scalar(tmp[:, 0, :], tmp[:, 0, :], PHASE, float(np.float32(3.1415925)), ALU.add, ALU.min))
        ch.step(v.tensor_scalar(tmp[:, 5, :], tmp[:, 0, :], -float(np.float32(3.1415925)), None, ALU.max))
        assert ch.n == SETUP_ANGLE, ch.n
        v.wait_ge(setup_pe, 1)
        ch.did(v.tensor_copy(wsel[:, :, :], ps[0:A0, 4, :].rearrange("p (o b) -> p b o", o=A0)))
        v.wait_ge(setup_pe, 2)
        ch.did(v.tensor_copy(domb[:, :], ps[0:A0, 5, 0:B]))
        assert ch.n == SETUP_WSEL, ch.n

        def adaptive():
            v.wait_ge(setup_pe, 4)
            ch.did(v.tensor_copy(bi2[:, :, :], ps[:, 0, 32:32 + FC * B].rearrange("p (c b) -> p c b", c=FC)))
            ch.did(v.tensor_scalar(ada[:, 0, :], ps[:, 0, 0:B], col(C_ADA0), 1.0, ALU.add, ALU.add))
            ch.did(v.tensor_scalar(ada[:, 1, :], ps[:, 0, B:2 * B], col(C_ADA1), None, ALU.add))
            ch.did(v.tensor_scalar(col(C_BQ), col(C_BQ), DH ** -0.5, None, ALU.mult))
            assert ch.n == SETUP_ADA, ch.n

        def all_masked():
            v.wait_ge(mask_loaded, 16)
            ch.step(v.tensor_reduce(nanfix[:, :], mask[:, :, :], AX, ALU.min))
            ch.step(v.tensor_scalar(nanfix[:, :], nanfix[:, :], 3.0e38, 3.0e38, ALU.mult, ALU.mult))
            ch.step(v.tensor_scalar(nanfix[:, :], nanfix[:, :], 0.0, None, ALU.mult))

        lc = Chain(v, l0_v)

        def domain_bias(g):
            v.wait_ge(exp_psum, g + 1)
            v.tensor_tensor(eT[0:A0, g * GT:(g + 1) * GT].rearrange("p (b s) -> p b s", b=GB),
                            ps[0:A0, 4 + g % 2, :].rearrange("p (b s) -> p b s", b=GB),
                            domb[:, g * GB:(g + 1) * GB].unsqueeze(2).to_broadcast([A0, GB, S]),
                            ALU.add).then_inc(eT_ready, 1)

        def norms(g):
            first = list(range(g * GB, (g + 1) * GB)) if g < NG else []
            second = list(range((g - 1) * GB, g * GB)) if g else []
            if first:
                v.wait_ge(up_psum, g + 1)
                v.tensor_tensor(x1[:, first[0]:first[0] + GB, :], bank4(6 + g % 2), x_in[:, first[0]:first[0] + GB, :],
                                ALU.add).then_inc(up_read, 1)
                v.wait_ge(up_read, g + 1)
            if second:
                v.wait_ge(x1_ready, g)
            both = first + second
            norm_stats(lc, v, lambda j: x1[:, both[j], :], 1e-5, len(both))
            for j, b in enumerate(both):
                ins = apply_norm(v, xn1[:, b, :], x1[:, b, :], j)
                if j == len(first) - 1:
                    ins.then_inc(xa_ready, 1)
                elif j == len(both) - 1:
                    ins.then_inc(xn1_ready, 1)
                else:
                    lc.did(ins)

        def project_in(g):
            v.wait_ge(qkf_ready, 2 * g + 1)
            whole, p = qkf[0][:, :], pieces[0]
            pc.step(v.tensor_tensor(whole, whole, p[:, 0, :], ALU.subtract))
            pc.step(v.tensor_copy(p[:, 1, :], whole))
            v.tensor_tensor(p[:, 2, :], whole, p[:, 1, :], ALU.subtract).then_inc(piece3[0], 1)

        pc = Chain(v, pieces_v)
        all_masked()
        domain_bias(0)
        domain_bias(1)
        norms(0)
        domain_bias(2)
        adaptive()
        domain_bias(3)
        norms(1)
        norms(2)
        project_in(0)
        norms(3)
        project_in(1)
        norms(4)
        project_in(2)
        project_in(3)

        v.wait_ge(memsets, 7)
        NATT = 3
        def attend(t, j, first):
            for q in range(NQ):
                if q == 0:
                    v.wait_ge(bias_masked, t + 1)
                wait_apart(v, scores_ready, NQ * t + q + 1, first_loaded, FIRST)
                for i in range(HQ):
                    h = q * HQ + i
                    ins = v.tensor_tensor_reduce(biasx[:, j, h, :], bank4(q % 2)[:, i, :], biasx[:, j, h, :], 1.0,
                                                 -3.0e38, ALU.add, ALU.max, mx[:, j % 2, h:h + 1])
                ins.then_inc(scores_read, 1)
                if q == 1 and not (isinstance(t, int) and t < 2):
                    divide(t - 2)
            v.wait_ge(scores_read, NQ * (t + 1))
            if not first:
                v.wait_ge(mT_psum, t)
            m, n = mx[:, j % 2, :], NATT * t
            v.tensor_scalar(mp[:, 0:16], m, -1.0, None, ALU.mult).then_inc(att_v, 1)
            v.wait_ge(att_v, n + 1)
            v.scalar_tensor_tensor(out=mres[:, :], in0=m, scalar=-1.0, in1=mp[:, 0:16], op0=ALU.mult,
                                   op1=ALU.subtract).then_inc(att_v, 1)
            v.wait_ge(att_v, n + 2)
            v.tensor_copy(mp[:, 16:32], mres[:, :]).then_inc(att_v, 1)
            v.wait_ge(att_v, n + 3)
            v.tensor_tensor(mp[:, 32:48], mres[:, :], mp[:, 16:32], ALU.subtract).then_inc(mp_ready, 1)
            v.wait_ge(mp_ready, t + 1)
            if not (isinstance(t, int) and t < 2):
                finish(t - 2)

        def divide(t):
            v.wait_ge(ctxn_psum, t + 1)
            if not (isinstance(t, int) and t == 0):
                v.wait_ge(ctx2_psum, t)
            nat = bank4(6).rearrange("p q (i r) -> p (q i) r", i=HQ)
            v.tensor_scalar(den[:, :], nat[:, :, DH], nanfix[:, bass.ds(t, 1)], None, ALU.add).then_inc(den_v, 1)
            v.wait_ge(den_v, 2 * t + 1)
            v.reciprocal(rden[:, :], den[:, :]).then_inc(den_v, 1)
            v.wait_ge(den_v, 2 * t + 2)
            v.tensor_tensor(ctxn[:, :].rearrange("p (h r) -> p h r", h=H), nat[:, :, 0:DH],
                            rden[:, :].unsqueeze(2).to_broadcast([S, H, DH]), ALU.mult).then_inc(ctxn_ready, 1)

        def finish(t):
            v.wait_ge(wo_psum, t + 1)
            v.tensor_tensor(x2[:, bass.ds(t, 1), :].rearrange("p a d -> p (a d)"), ps[:, 7, 128:256],
                            y_rows[:, bass.ds(t, 1), :].rearrange("p a d -> p (a d)"), ALU.add).then_inc(x2_ready, 1)

        N_NORM = 23
        def norm_x2(g):
            nc_ = Chain(v, ffn_v, N_NORM * g)
            row = lambda x, j: x[:, g * GB + j, :]
            v.wait_ge(x2_ready, GB * (g + 1))
            norm_stats(nc_, v, lambda j: row(x2, j), 1e-5)
            for j in range(GB):
                ins = apply_norm(v, row(xs1, j), row(x2, j), j)
                if j < GB - 1:
                    nc_.did(ins)
            ins.then_inc(xs_ready, 1)
            v.wait_ge(xs_ready, g + 1)
            assert nc_.n == N_NORM, nc_.n

        for j in range(GB):
            attend(j, j, j == 0)
        with v.Fori(1, NG) as g:
            for j in range(GB):
                attend(g * GB + j, j, False)
        divide(B - 2)
        norm_x2(0)
        finish(B - 2)
        divide(B - 1)
        finish(B - 1)

        def residual3(n):
            v.wait_ge(w2_psum, n + 1)
            v.wait_ge(x2b_ready, n + 1)
            v.tensor_tensor(x3, bank4(7), x2[:, bass.ts(n, GB), :], ALU.add).then_inc(x3_ready, 1)

        def norm4(sc, n):
            v.wait_ge(wo2_psum, GB * (n + 1))
            v.wait_ge(x3_ready, n + 1)
            v.tensor_tensor(r3, bank4(7), x3, ALU.add).then_inc(r3_sum, 1)
            v.wait_ge(r3_sum, n + 1)
            v.wait_ge(rows2_loaded, 16 * GB * (n + 1))
            sc.step(v.tensor_tensor(r3, r3, rows2[:, :, 0, :], ALU.add))
            norm_stats(sc, v, lambda j: r3[:, j, :], 1e-12)
            for j in range(GB):
                sc.did(v.scalar_tensor_tensor(out=r3[:, j, :], in0=r3[:, j, :], scalar=mv[:, j, 0:1],
                                              in1=rows2[:, j, 1, :], op0=ALU.subtract, op1=ALU.mult))
            sc.join()
            for j in range(GB):
                ins = v.scalar_tensor_tensor(out=x4[:, bass.ds(n * GB + j, 1), :].rearrange("p a d -> p (a d)"),
                                             in0=r3[:, j, :], scalar=rs[:, 3, j:j + 1], in1=rows2[:, j, 2, :],
                                             op0=ALU.mult, op1=ALU.add)
                if j < GB - 1:
                    sc.did(ins)
            ins.then_inc(x4_ready, 1)
            v.wait_ge(x4_ready, n + 1)

        def norm_l3(sc, n):
            row = lambda j: x4[:, bass.ds(n * GB + j, 1), :].rearrange("p a d -> p (a d)")
            norm_stats(sc, v, row, 1e-5)
            for j in range(GB):
                ins = apply_norm(v, xs3[:, j, :], row(j), j)
                if j < GB - 1:
                    sc.did(ins)
            ins.then_inc(e_xs, 1)
            v.wait_ge(e_xs, n + 1)

        def token_norm(sc, n):
            v.wait_ge(e_hl, n + 1)
            norm_stats(sc, v, lambda j: hl[:, j, :], 1e-8)
            sl = bass.ts(n, GB)
            sc.step(v.tensor_tensor(rs[:, 3, 0:GB], rs[:, 3, 0:GB], sty[:, 0, sl], ALU.mult))
            sc.step(v.tensor_tensor(rs[:, 1, 0:GB], mv[:, 0:GB, 0], rs[:, 3, 0:GB], ALU.mult))
            sc.step(v.tensor_tensor(rs[:, 2, 0:GB], sty[:, 1, sl], rs[:, 1, 0:GB], ALU.subtract))
            for j in range(GB):
                ins = v.tensor_scalar(hfs[:, j, :], hl[:, j, :], rs[:, 3, j:j + 1], rs[:, 2, j:j + 1], ALU.mult, ALU.add)
                if j < GB - 1:
                    sc.did(ins)
            ins.then_inc(e_hfs, 1)
            v.wait_ge(e_hfs, n + 1)
            v.wait_ge(xs_psum, n + 1)
            sc.step(v.tensor_copy(hcols[:, bass.ts(n, GT)], flat(hfs)))
            v.tensor_tensor(hcols_low[:, bass.ts(n, GT)], flat(hfs), hcols[:, bass.ts(n, GT)].bitcast(F32),
                            ALU.subtract).then_inc(e_hcols, 1)

        def pick(sc, n):
            wait_apart(v, e_logit, n + 1, first_loaded, FIRST)
            for j in range(GB):
                sc.did(v.max(top[:, j, :], ps[:, 7, j * E3:(j + 1) * E3]))
            sc.join_apart(first_loaded, FIRST)
            for j in range(GB):
                sc.did(v.max_index(topi[:, j, :], top[:, j, :], ps[:, 7, j * E3:(j + 1) * E3]))
            sc.join()
            sc.did(v.tensor_copy(topf[:, :, :], topi[:, :, :]))
            v.tensor_tensor(gate[:, 0, :], top[:, :, 1], top[:, :, 0], ALU.subtract).then_inc(e_top, 1)
            v.wait_ge(e_gate, n + 1)
            sc.did(v.tensor_scalar(gate[:, 2, :], gate[:, 1, :], -0.5, 0.5, ALU.mult, ALU.add))
            sc.did(v.tensor_scalar(gate[:, 3, :], gate[:, 1, :], 0.5, 0.5, ALU.mult, ALU.add))
            sc.join()
            for j in range(GB):
                sc.did(v.tensor_scalar(combs[:, j, :], iota8[:, :], topf[:, j, 0:1], gate[:, 2, j:j + 1],
                                       ALU.is_equal, ALU.mult))
                sc.did(v.tensor_scalar(comb2[:, j, :], iota8[:, :], topf[:, j, 1:2], gate[:, 3, j:j + 1],
                                       ALU.is_equal, ALU.mult))
            sc.join()
            v.tensor_tensor(combs[:, :, :], combs[:, :, :], comb2[:, :, :], ALU.add).then_inc(e_comb, 1)
            v.wait_ge(e_comb, n + 1)
            sc.step(v.tensor_copy(comb[:, bass.ts(n, GB), :], combs[:, :, :]))

        def add_bias(n):
            v.wait_ge(e_b2, n + 1)
            v.tensor_tensor(x4[:, bass.ts(n, GB), :], bank4(7), x4[:, bass.ts(n, GB), :], ALU.add).then_inc(e_acc, 1)
            v.wait_ge(e_acc, n + 1)

        def add_expert(m, e):
            v.wait_ge(m_w2, m * E3 + e + 1)
            if e:
                v.wait_ge(m_acc, GB * (m * E3 + e))
            for j in range(GB):
                b = m * GB + j
                row = x4[:, bass.ds(b, 1), :].rearrange("p a d -> p (a d)")
                v.scalar_tensor_tensor(out=row, in0=bank4(2 + e % 2)[:, j, :],
                                       scalar=comb[:, bass.ds(b, 1), e], in1=row,
                                       op0=ALU.mult, op1=ALU.add).then_inc(m_acc, 1)

        N_NORMS, N_PICK = 78, 20
        def side_by_side(n, m, begun=False):
            side = n is not None
            sc = Chain(v, side_v, N_NORMS + (N_NORMS + N_PICK) * m)
            pick(sc, m)
            assert sc.n == N_PICK, sc.n
            add_bias(m)
            add_expert(m, 0)
            if side and not begun:
                residual3(n)
            add_expert(m, 1)
            add_expert(m, 2)
            if side:
                norm4(sc, n)
            add_expert(m, 3)
            if side:
                norm_l3(sc, n)
            add_expert(m, 4)
            add_expert(m, 5)
            if side:
                token_norm(sc, n)
                assert sc.n == N_PICK + N_NORMS, sc.n
            add_expert(m, 6)
            add_expert(m, 7)

        sc = Chain(v, side_v)
        norm_x2(1)
        residual3(0)
        norm_x2(2)
        norm_x2(3)
        norm4(sc, 0)
        norm_l3(sc, 0)
        residual3(1)
        v.wait_ge(l_act, 5)
        fc = Chain(v, style_v)
        fc.step(v.scalar_tensor_tensor(out=sty[:, 0, :], in0=sty[:, 2, :], scalar=0.0, in1=sty[:, 3, :],
                                       op0=ALU.max, op1=ALU.add))
        fc.step(v.tensor_scalar(sty[:, 0, :], sty[:, 0, :], 1e-8, None, ALU.add))
        token_norm(sc, 0)
        assert sc.n == N_NORMS, sc.n
        side_by_side(1, 0, begun=True)
        with v.Fori(2, NG) as n:
            side_by_side(n, n - 1)
        side_by_side(None, NG - 1)

    @block.gpsimd
    def _(pool):
        ms = Chain(pool, memsets)
        ms.step(pool.memset(w2_area[32:33, 0:2048], 1.0))
        ms.step(pool.memset(ones[:, :], 1.0))
        for stack in (query_stack, key_stack):
            ms.step(pool.memset(stack[:, :].bitcast(U32), 0))
        pool.wait_ge(first_loaded, FIRST)
        ms.step(pool.tensor_copy(identb[:, :], ident[:, :]))
        ms.step(pool.tensor_copy(msel[:, :], hsel))
        ms.step(pool.memset(mp[:, :], 0.0))
        for p in range(2):
            ms.step(pool.memset(vaug[p][:, :, :], 0.0))
            ms.step(pool.memset(vaug[p][:, :, DH:DH + 1], 1.0))
        pool.wait_ge(weights_loaded, WEIGHTS)
        po, pk = Chain(pool, pool_own), Chain(pool, pieces_p)

        def scale_x1(g):
            pool.wait_ge(xa_ready, g + 1)
            sl = slice(g * GB, (g + 1) * GB)
            po.step(pool.tensor_tensor(x1[:, sl, :], xn1[:, sl, :], rows[:, 0:1, :].to_broadcast([S, GB, D]), ALU.mult))
            pool.tensor_tensor(x1[:, sl, :], x1[:, sl, :], rows[:, 1:2, :].to_broadcast([S, GB, D]),
                               ALU.add).then_inc(x1_ready, 1)
            pool.wait_ge(x1_ready, g + 1)

        def key_pieces(g):
            pool.wait_ge(qkf_ready, 2 * g + 2)
            whole, p = qkf[1][:, :], pieces[1]
            pk.step(pool.tensor_tensor(whole, whole, p[:, 0, :], ALU.subtract))
            pk.step(pool.tensor_copy(p[:, 1, :], whole))
            pool.tensor_tensor(p[:, 2, :], whole, p[:, 1, :], ALU.subtract).then_inc(piece3[1], 1)
            pool.wait_ge(piece3[1], g + 1)


        def mask_bias(t, j):
            pool.wait_ge(mneg_ready, t + 1)
            pool.wait_ge(bias_loaded[j], 4 * (t - j + GB))
            pool.tensor_tensor(biasx[:, j, :, :], biasx[:, j, :, :], mneg[j][:, :].unsqueeze(1).to_broadcast([S, H, S]),
                               ALU.add).then_inc(bias_masked, 1)
            pool.wait_ge(bias_masked, t + 1)

        def values(t, j, early):
            if not early:
                pool.wait_ge(pv_done, NQ * (t - 1))
            pool.tensor_copy(vaug[j % 2][:, :, 0:DH],
                             v_rows[:, bass.ds(t, 1), :].rearrange("p a (h r) -> p (a h) r", h=H)).then_inc(vaug_ready, 1)
            pool.wait_ge(vaug_ready, t + 1)

        scale_x1(0)
        scale_x1(1)
        mask_bias(0, 0)
        scale_x1(2)
        key_pieces(0)
        scale_x1(3)
        key_pieces(1)
        key_pieces(2)
        mask_bias(1, 1)
        key_pieces(3)
        pool.wait_ge(vy_read, NG)
        for j in range(1, GB):
            if j >= 2:
                mask_bias(j, j)
            values(j - 1, j - 1, j < 3)
        with pool.Fori(1, NG) as g:
            for j in range(GB):
                mask_bias(g * GB + j, j)
                values(g * GB + j - 1, (j - 1) % GB, False)
        values(B - 1, B - 1, False)

        def residual_bias(n):
            pool.wait_ge(xs_ready, n + 1)
            pool.tensor_tensor(x2[:, bass.ts(n, GB), :], x2[:, bass.ts(n, GB), :],
                               rows[:, 4:5, :].to_broadcast([S, GB, D]), ALU.add).then_inc(x2b_ready, 1)
            pool.wait_ge(x2b_ready, n + 1)

        residual_bias(0)
        residual_bias(1)
        for c in range(E3):
            w = slice(c * FF, (c + 1) * FF)
            pool.wait_ge(w1e_rounded, c // 4 + 1)
            pool.tensor_tensor(w1e_low[:, w], w1e[:, w], w1e_high[:, w].bitcast(F32), ALU.subtract
                               ).then_inc(w1e_split, 1)
            pool.wait_ge(w1e_split, c + 1)
        with pool.Fori(2, NG) as n:
            pool.wait_ge(xs_psum, n)
            pool.wait_ge(xs_ready, n + 1)
            pool.tensor_copy(xs_slot, xs1[:, bass.ts(n, GB), :]).then_inc(xs_staged, 1)
            pool.wait_ge(xs_staged, n - 1)
            residual_bias(n)


OUT_SHAPE = (B, S, D)


def kernel(**inputs):
    import concourse.bacc as bacc
    from concourse.bass_utils import run_bass_kernel_spmd

    def arr(name):
        return np.asarray(inputs[name])

    def column(v):
        n = v.shape[0]
        if n > 128:
            return v.reshape(-1, 128).T
        c = np.zeros((128, 1), v.dtype)
        c[:n, 0] = v
        return c

    def beside(*arrays):
        return np.concatenate([np.concatenate([a, np.zeros((128 - a.shape[0], a.shape[1]), a.dtype)], 0)
                               for a in arrays], 1)

    l0, l1, l2, l3 = "L0_cond_", "L1_cond_", "L2_cond_", "L3_cond_"
    half = D // 2
    freq = np.exp(np.arange(half, dtype=np.float32) * np.float32(-np.log(10000.0) / (half - 1))).astype(np.float32)
    cc = np.zeros((128, 32), np.float32)
    cc[:, 0] = np.arange(128)
    cc[:, 1] = np.concatenate([freq, freq])
    cc[half:, 2] = np.float32(np.pi / 2)
    cc[half:, 3] = 0.25
    for p in range(3):
        cc[p * H:(p + 1) * H, 8:8 + H] = np.eye(H)

    vectors = beside(*[column(c) for c in (
        arr(l0 + "down_b"), arr(l1 + "b_ada")[:D], arr(l1 + "b_ada")[D:], arr(l1 + "bq"), arr(l1 + "bk"),
        arr(l1 + "g2"), arr(l1 + "beta2"), arr(l3 + "ln_g"), arr(l3 + "ln_b"), arr(l3 + "hyp_b1"),
        arr(l3 + "hyp_b2"), arr(l3 + "sty_b1"), arr(l3 + "sty_b2")[:D], arr(l3 + "sty_b2")[D:], arr(l1 + "b1"))],
        np.zeros((128, 32 - (C_VECTORS + FC)), np.float32))

    data = {
        "x": arr("x"),
        "attn_bias": arr("fside_Bx16xSxS_0").transpose(0, 2, 1, 3),
        "mask": np.ascontiguousarray(arr("mask_Bx1xSxS_bk0")[:, 0].transpose(1, 0, 2)),
        "ids": np.stack([arr("itok_B_0_15"), arr("itok_B_34_63"), arr("itok_B_0_7"), arr("itok_B_6_14")], 0),
        "consts": beside(np.eye(128, dtype=np.float32), cc, np.tile(np.arange(8, dtype=np.float32), (128, 1)), vectors),
        "adapters": np.concatenate([arr(l0 + "expert_W").reshape(E0, A0 * A0),
                                    np.eye(A0, dtype=np.float32).reshape(1, -1)], 0),
        "early": beside(
            arr(l0 + "down_W").T, np.concatenate([arr(l0 + "up_W").T, arr(l0 + "up_b")[None]], 0),
            beside(arr(l3 + "subj_emb"), arr(l0 + "expert_b"), arr(l0 + "domain_emb")),
            arr(l2 + "bi"), arr(l3 + "hyp_w1"), arr(l3 + "hyp_w2"), arr(l3 + "sty_w1"), arr(l3 + "sty_w2"),
            arr(l1 + "W_ada")),
        "weights": beside(
            arr(l1 + "Wq"), arr(l1 + "Wk"), arr(l1 + "Wv"), np.eye(128, dtype=np.float32), arr(l1 + "Wo"),
            arr(l1 + "W1"), arr(l1 + "W2").reshape(FC, 128, D).transpose(1, 0, 2).reshape(128, FC * D),
            arr(l3 + "router_w"), arr(l3 + "exp_b2"), arr(l3 + "exp_b1").reshape(E3 * FC, 128).T),
        "exp_w1": arr(l3 + "exp_w1"),
        "exp_w2": arr(l3 + "exp_w2").reshape(E3, FC, 128, D).transpose(2, 0, 1, 3),
        "l2_w": np.concatenate([arr(l2 + "Wi"), arr(l2 + "Wo").reshape(E2, FC, 128, D).transpose(0, 2, 1, 3)
                                .reshape(E2, 128, FC * D)], 2),
        "l2_rows": np.stack([arr(l2 + "bo"), arr(l2 + "gamma"), arr(l2 + "beta")], 1),
        "rows": np.stack([arr(l0 + "ln_gamma"), arr(l0 + "ln_beta"), arr(l1 + "bv"), arr(l1 + "bo"), arr(l1 + "b2")], 0),
    }
    nc = bacc.Bacc("TRN2", target_bir_lowering=False, num_devices=1)
    arrays, aps = {}, {}
    for name, a in data.items():
        a = np.ascontiguousarray(a)
        arrays[f"in_{name}"] = a
        aps[name] = nc.dram_tensor(f"in_{name}", a.shape, mybir.dt.from_np(a.dtype), kind="ExternalInput").ap()
    out = nc.dram_tensor("out_0", OUT_SHAPE, F32, kind="ExternalOutput").ap()
    program(nc, aps, out)
    return run_bass_kernel_spmd(nc, [arrays], core_ids=[0]).results[0]["out_0"]
```
